# Optimizing a Trainium2 kernel written in Bass

```python
import numpy as np
import jax
import jax.numpy as jnp

def _softmax(x, axis=-1):
    return jax.nn.softmax(x, axis=axis)

def _gelu(x):
    return jax.nn.gelu(x, approximate=True)

def _silu(x):
    return jax.nn.silu(x)

def _sigmoid(x):
    return jax.nn.sigmoid(x)

def _layernorm(x, axis=-1, eps=1e-05):
    m = jnp.mean(x, axis=axis, keepdims=True)
    v = jnp.var(x, axis=axis, keepdims=True)
    return (x - m) / jnp.sqrt(v + eps)

def _scatter_add(tgt, idx, src, axis=0):
    return tgt.at[idx].add(src)

def _segment_sum(src, seg, n):
    return jax.ops.segment_sum(src, seg, n)
kernel_name = 'mk_pixart_seq_d4_seqx_r8_f0dda6'

def setup_inputs(seed: int=0):
    np.random.seed(seed)
    _w = jnp.asarray

    def _rec_inputs():
        import jax
        import jax.numpy as jnp
        _rk = jax.random.key(seed)
        x = 7.22e-05 + 1 * jax.random.normal(jax.random.fold_in(_rk, 1), (8, 256, 128), jnp.float32)
        _lenS = 256 - jax.random.randint(jax.random.fold_in(_rk, 7), (8,), 0, max(1, 256 // 4) + 1, jnp.int32)
        _lenS2 = 64 - jax.random.randint(jax.random.fold_in(_rk, 8), (8,), 0, max(1, 64 // 4) + 1, jnp.int32)
        cond_1024 = 0.0061147 + 1.02565 * jax.random.normal(jax.random.fold_in(_rk, 11), (8, 128), jnp.float32)
        _ctx_768P = jax.random.normal(jax.random.fold_in(_rk, 12), (8, 16, 96), jnp.float32)
        _ctx_768c = jax.random.dirichlet(jax.random.fold_in(_rk, 512), 0.3 * jnp.ones((16,), jnp.float32), (8, 64))
        _ctx_768t = jnp.einsum('bsk,bkd->bsd', _ctx_768c, _ctx_768P)
        _ctx_768t = _ctx_768t * jax.lax.rsqrt(jnp.mean(jnp.square(_ctx_768t)) + 1e-12) * 0.953939
        ctx_768 = 0.000599585 + 1.00006 * (_ctx_768t + 0.3 * jax.random.normal(jax.random.fold_in(_rk, 612), (8, 64, 96), jnp.float32))
        return (x, cond_1024, ctx_768)
    x, cond_1024, ctx_768 = _rec_inputs()

    def _L0_xcond_setup():
        import jax, jax.numpy as jnp
        import numpy as np
        EPS = 1e-05

        def _ada_ln(x, t, W, b):
            emb = t @ W + b
            scale, shift = jnp.split(emb, 2, axis=-1)
            mu = x.mean(-1, keepdims=True)
            var = ((x - mu) ** 2).mean(-1, keepdims=True)
            xn = (x - mu) * jax.lax.rsqrt(var + EPS)
            return xn * (1.0 + scale) + shift

        def _attn(x, ctx, Wq, Wk, Wv, Wo, bo, heads):
            b, n, _ = x.shape
            j = ctx.shape[1]
            q = (x @ Wq).reshape(b, n, heads, -1)
            k = (ctx @ Wk).reshape(b, j, heads, -1)
            v = (ctx @ Wv).reshape(b, j, heads, -1)
            scale = q.shape[-1] ** (-0.5)
            sim = jnp.einsum('bihd,bjhd->bhij', q, k) * scale
            attn = jax.nn.softmax(sim, axis=-1)
            out = jnp.einsum('bhij,bjhd->bihd', attn, v).reshape(b, n, -1)
            return out @ Wo + bo

        def _ff(x, W1, b1, W2, b2):
            p = x @ W1 + b1
            a, gate = jnp.split(p, 2, axis=-1)
            return a * jax.nn.gelu(gate, approximate=False) @ W2 + b2
        key = jax.random.key(seed)
        ks = jax.random.split(key, 32)
        B, N, D = (4, 256, 128)
        J, CD = (32, 96)
        H, DH = (16, 64)
        INNER = H * DH
        FF = 4 * D
        w = lambda k, shp: jax.random.normal(k, shp, jnp.float32) * 0.02
        inp = {'x': jax.random.normal(ks[0], (B, N, D), jnp.float32), 't': jax.random.normal(ks[1], (B, 1, D), jnp.float32), 'context': jax.random.normal(ks[2], (B, J, CD), jnp.float32), 'n1_w': w(ks[3], (D, 2 * D)), 'n1_b': jnp.zeros((2 * D,), jnp.float32), 'n2_w': w(ks[4], (D, 2 * D)), 'n2_b': jnp.zeros((2 * D,), jnp.float32), 'n3_w': w(ks[5], (D, 2 * D)), 'n3_b': jnp.zeros((2 * D,), jnp.float32), 'q1': w(ks[6], (D, INNER)), 'k1': w(ks[7], (D, INNER)), 'v1': w(ks[8], (D, INNER)), 'o1_w': w(ks[9], (INNER, D)), 'o1_b': jnp.zeros((D,), jnp.float32), 'q2': w(ks[10], (D, INNER)), 'k2': w(ks[11], (CD, INNER)), 'v2': w(ks[12], (CD, INNER)), 'o2_w': w(ks[13], (INNER, D)), 'o2_b': jnp.zeros((D,), jnp.float32), 'ff_w1': w(ks[14], (D, 2 * FF)), 'ff_b1': jnp.zeros((2 * FF,), jnp.float32), 'ff_w2': w(ks[15], (FF, D)), 'ff_b2': jnp.zeros((D,), jnp.float32)}
        return inp
    _L0_xcond_all = _L0_xcond_setup()
    _L0_xcond_in = {k: v for k, v in _L0_xcond_all.items() if k in ('n1_w', 'n1_b', 'n2_w', 'n2_b', 'n3_w', 'n3_b', 'q1', 'k1', 'v1', 'o1_w', 'o1_b', 'q2', 'k2', 'v2', 'o2_w', 'o2_b', 'ff_w1', 'ff_b1', 'ff_w2', 'ff_b2')}
    del _L0_xcond_all

    def _L1_xcond_setup():
        import jax, jax.numpy as jnp
        import numpy as np
        B, N, D, H, TD, TL = (4, 128, 128, 16, 96, 77)
        HD = D // H
        EPS = 1e-06

        def _ln(x):
            mu = jnp.mean(x, axis=-1, keepdims=True)
            var = jnp.var(x, axis=-1, keepdims=True)
            return (x - mu) * jax.lax.rsqrt(var + EPS)

        def _modulate(x, shift, scale):
            return x * (1.0 + scale[:, None, :]) + shift[:, None, :]

        def _heads(t):
            return t.reshape(t.shape[0], t.shape[1], H, HD).transpose(0, 2, 1, 3)

        def _attend(q, k, v):
            sim = jnp.einsum('bhid,bhjd->bhij', q, k) * HD ** (-0.5)
            attn = jax.nn.softmax(sim, axis=-1)
            out = jnp.einsum('bhij,bhjd->bhid', attn, v)
            return out.transpose(0, 2, 1, 3).reshape(out.shape[0], -1, D)
        key = jax.random.key(seed)
        ks = jax.random.split(key, 16)
        s = 0.02
        return {'x': jax.random.normal(ks[0], (B, N, D), jnp.float32), 'c': jax.random.normal(ks[1], (B, D), jnp.float32), 'text_embed': jax.random.normal(ks[2], (B, TL, TD), jnp.float32), 'W_ada': jax.random.normal(ks[3], (D, 6 * D), jnp.float32) * s, 'b_ada': jnp.zeros((6 * D,), jnp.float32), 'W_qkv': jax.random.normal(ks[4], (D, 3 * D), jnp.float32) * s, 'b_qkv': jnp.zeros((3 * D,), jnp.float32), 'W_proj': jax.random.normal(ks[5], (D, D), jnp.float32) * s, 'b_proj': jnp.zeros((D,), jnp.float32), 'W_ctx': jax.random.normal(ks[6], (TD, D), jnp.float32) * s, 'b_ctx': jnp.zeros((D,), jnp.float32), 'W_q': jax.random.normal(ks[7], (D, D), jnp.float32) * s, 'W_k': jax.random.normal(ks[8], (D, D), jnp.float32) * s, 'W_v': jax.random.normal(ks[9], (D, D), jnp.float32) * s, 'W_out': jax.random.normal(ks[10], (D, D), jnp.float32) * s, 'b_out': jnp.zeros((D,), jnp.float32), 'W_fc1': jax.random.normal(ks[11], (D, 4 * D), jnp.float32) * s, 'b_fc1': jnp.zeros((4 * D,), jnp.float32), 'W_fc2': jax.random.normal(ks[12], (4 * D, D), jnp.float32) * s, 'b_fc2': jnp.zeros((D,), jnp.float32)}
    _L1_xcond_all = _L1_xcond_setup()
    _L1_xcond_in = {k: v for k, v in _L1_xcond_all.items() if k in ('W_ada', 'b_ada', 'W_qkv', 'b_qkv', 'W_proj', 'b_proj', 'W_ctx', 'b_ctx', 'W_q', 'W_k', 'W_v', 'W_out', 'b_out', 'W_fc1', 'b_fc1', 'W_fc2', 'b_fc2')}
    del _L1_xcond_all

    def _L2_xcond_setup():
        import jax, jax.numpy as jnp
        import numpy as np
        B, N, M = (2, 128, 64)
        D, H, DH = (128, 16, 64)
        MID = H * DH
        DC = 96
        MULT = 4
        EPS = 1e-05

        def _ln(x, w, b):
            mu = jnp.mean(x, -1, keepdims=True)
            var = jnp.mean((x - mu) ** 2, -1, keepdims=True)
            return (x - mu) * jax.lax.rsqrt(var + EPS) * w + b

        def _sincos(n, d):
            inv = 1.0 / 10000.0 ** (jnp.arange(0, d, 2, dtype=jnp.float32) / d)
            ang = jnp.arange(n, dtype=jnp.float32)[:, None] * inv[None, :]
            return (jnp.sin(ang), jnp.cos(ang))

        def _rope(x, sin, cos):
            s = sin[None, None]
            c = cos[None, None]
            xe = x[..., ::2]
            xo = x[..., 1::2]
            re = xe * c - xo * s
            ro = xe * s + xo * c
            return jnp.stack((re, ro), axis=-1).reshape(x.shape)

        def _heads(t):
            b, n, _ = t.shape
            return t.reshape(b, n, H, DH).transpose(0, 2, 1, 3)

        def _attn(xq, ctx, wq, wkv, wo, bo):
            q = _heads(xq @ wq)
            k, v = jnp.split(ctx @ wkv, 2, axis=-1)
            k = _heads(k)
            v = _heads(v)
            sq, cq = _sincos(q.shape[2], DH)
            sk, ck = _sincos(k.shape[2], DH)
            q = _rope(q, sq, cq)
            k = _rope(k, sk, ck)
            sim = jnp.einsum('bhnd,bhmd->bhnm', q, k) * DH ** (-0.5)
            a = jax.nn.softmax(sim, axis=-1)
            o = jnp.einsum('bhnm,bhmd->bhnd', a, v)
            o = o.transpose(0, 2, 1, 3).reshape(xq.shape[0], xq.shape[1], MID)
            return o @ wo + bo

        def _adaln(x, c, lw, lb, gw, gb, bw, bb):
            g = (c @ gw + gb)[:, None, :]
            bt = (c @ bw + bb)[:, None, :]
            return _ln(x, lw, lb) * (1.0 + g) + bt
        ks = jax.random.split(jax.random.key(seed), 24)
        s = 0.02
        inp = {'x': jax.random.normal(ks[0], (B, N, D), jnp.float32), 'cond': jax.random.normal(ks[1], (B, D), jnp.float32), 'context': jax.random.normal(ks[2], (B, M, DC), jnp.float32), 'ln1_w': jnp.ones((D,), jnp.float32), 'ln1_b': jnp.zeros((D,), jnp.float32), 'g1_w': jax.random.normal(ks[3], (D, D), jnp.float32) * s, 'g1_b': jnp.zeros((D,), jnp.float32), 'b1_w': jax.random.normal(ks[4], (D, D), jnp.float32) * s, 'b1_b': jnp.zeros((D,), jnp.float32), 'ln2_w': jnp.ones((D,), jnp.float32), 'ln2_b': jnp.zeros((D,), jnp.float32), 'g2_w': jax.random.normal(ks[5], (D, D), jnp.float32) * s, 'g2_b': jnp.zeros((D,), jnp.float32), 'b2_w': jax.random.normal(ks[6], (D, D), jnp.float32) * s, 'b2_b': jnp.zeros((D,), jnp.float32), 'sa_wq': jax.random.normal(ks[7], (D, MID), jnp.float32) * s, 'sa_wkv': jax.random.normal(ks[8], (D, 2 * MID), jnp.float32) * s, 'sa_wo': jax.random.normal(ks[9], (MID, D), jnp.float32) * s, 'sa_bo': jnp.zeros((D,), jnp.float32), 'ca_lnc_w': jnp.ones((DC,), jnp.float32), 'ca_lnc_b': jnp.zeros((DC,), jnp.float32), 'ca_wq': jax.random.normal(ks[10], (D, MID), jnp.float32) * s, 'ca_wkv': jax.random.normal(ks[11], (DC, 2 * MID), jnp.float32) * s, 'ca_wo': jax.random.normal(ks[12], (MID, D), jnp.float32) * s, 'ca_bo': jnp.zeros((D,), jnp.float32), 'ff_w1': jax.random.normal(ks[13], (D, MULT * D), jnp.float32) * s, 'ff_b1': jnp.zeros((MULT * D,), jnp.float32), 'ff_w2': jax.random.normal(ks[14], (MULT * D, D), jnp.float32) * s, 'ff_b2': jnp.zeros((D,), jnp.float32)}
        return inp
    _L2_xcond_all = _L2_xcond_setup()
    _L2_xcond_in = {k: v for k, v in _L2_xcond_all.items() if k in ('ln1_w', 'ln1_b', 'g1_w', 'g1_b', 'b1_w', 'b1_b', 'ln2_w', 'ln2_b', 'g2_w', 'g2_b', 'b2_w', 'b2_b', 'sa_wq', 'sa_wkv', 'sa_wo', 'sa_bo', 'ca_lnc_w', 'ca_lnc_b', 'ca_wq', 'ca_wkv', 'ca_wo', 'ca_bo', 'ff_w1', 'ff_b1', 'ff_w2', 'ff_b2')}
    del _L2_xcond_all

    def _L3_xcond_setup():
        import jax, jax.numpy as jnp
        import numpy as np
        D = 128
        CD = 96
        H = 16
        HD = D // H
        EPS = 1e-05

        def _ln(x, w, b):
            m = jnp.mean(x, axis=-1, keepdims=True)
            v = jnp.var(x, axis=-1, keepdims=True)
            return (x - m) * jax.lax.rsqrt(v + EPS) * w + b

        def _attn(q, k, v):
            q = q.reshape(q.shape[0], q.shape[1], H, HD).transpose(0, 2, 1, 3)
            k = k.reshape(k.shape[0], k.shape[1], H, HD).transpose(0, 2, 1, 3)
            v = v.reshape(v.shape[0], v.shape[1], H, HD).transpose(0, 2, 1, 3)
            scores = jnp.einsum('bhnd,bhmd->bhnm', q, k) * HD ** (-0.5)
            p = jax.nn.softmax(scores, axis=-1)
            o = jnp.einsum('bhnm,bhmd->bhnd', p, v)
            return o.transpose(0, 2, 1, 3).reshape(o.shape[0], o.shape[2], D)
        key = jax.random.key(seed)
        ks = iter(jax.random.split(key, 32))
        s = 0.02
        inp = {'x': jax.random.normal(next(ks), (4, 128, D), jnp.float32), 'context': jax.random.normal(next(ks), (4, 32, CD), jnp.float32), 'time_emb': jax.random.normal(next(ks), (4, D), jnp.float32), 'ln1_w': jnp.ones((D,)), 'ln1_b': jnp.zeros((D,)), 'ln2_w': jnp.ones((D,)), 'ln2_b': jnp.zeros((D,)), 'ln3_w': jnp.ones((D,)), 'ln3_b': jnp.zeros((D,)), 'Wqkv': jax.random.normal(next(ks), (D, 3 * D)) * s, 'bqkv': jnp.zeros((3 * D,)), 'Wos': jax.random.normal(next(ks), (D, D)) * s, 'bos': jnp.zeros((D,)), 'Wq': jax.random.normal(next(ks), (D, D)) * s, 'bq': jnp.zeros((D,)), 'Wk': jax.random.normal(next(ks), (CD, D)) * s, 'bk': jnp.zeros((D,)), 'Wv': jax.random.normal(next(ks), (CD, D)) * s, 'bv': jnp.zeros((D,)), 'Woc': jax.random.normal(next(ks), (D, D)) * s, 'boc': jnp.zeros((D,)), 'W1': jax.random.normal(next(ks), (D, 4 * D)) * s, 'b1': jnp.zeros((4 * D,)), 'W2': jax.random.normal(next(ks), (4 * D, D)) * s, 'b2': jnp.zeros((D,)), 'Wmod': jax.random.normal(next(ks), (D, 6 * D)) * s, 'bmod': jnp.zeros((6 * D,))}
        return inp
    _L3_xcond_all = _L3_xcond_setup()
    _L3_xcond_in = {k: v for k, v in _L3_xcond_all.items() if k in ('ln1_w', 'ln1_b', 'ln2_w', 'ln2_b', 'ln3_w', 'ln3_b', 'Wqkv', 'bqkv', 'Wos', 'bos', 'Wq', 'bq', 'Wk', 'bk', 'Wv', 'bv', 'Woc', 'boc', 'W1', 'b1', 'W2', 'b2', 'Wmod', 'bmod')}
    del _L3_xcond_all
    return {'x': x, 'cond_1024': cond_1024, 'ctx_768': ctx_768, 'L0_xcond_n1_w': _L0_xcond_in['n1_w'], 'L0_xcond_n1_b': _L0_xcond_in['n1_b'], 'L0_xcond_n2_w': _L0_xcond_in['n2_w'], 'L0_xcond_n2_b': _L0_xcond_in['n2_b'], 'L0_xcond_n3_w': _L0_xcond_in['n3_w'], 'L0_xcond_n3_b': _L0_xcond_in['n3_b'], 'L0_xcond_q1': _L0_xcond_in['q1'], 'L0_xcond_k1': _L0_xcond_in['k1'], 'L0_xcond_v1': _L0_xcond_in['v1'], 'L0_xcond_o1_w': _L0_xcond_in['o1_w'], 'L0_xcond_o1_b': _L0_xcond_in['o1_b'], 'L0_xcond_q2': _L0_xcond_in['q2'], 'L0_xcond_k2': _L0_xcond_in['k2'], 'L0_xcond_v2': _L0_xcond_in['v2'], 'L0_xcond_o2_w': _L0_xcond_in['o2_w'], 'L0_xcond_o2_b': _L0_xcond_in['o2_b'], 'L0_xcond_ff_w1': _L0_xcond_in['ff_w1'], 'L0_xcond_ff_b1': _L0_xcond_in['ff_b1'], 'L0_xcond_ff_w2': _L0_xcond_in['ff_w2'], 'L0_xcond_ff_b2': _L0_xcond_in['ff_b2'], 'L1_xcond_W_ada': _L1_xcond_in['W_ada'], 'L1_xcond_b_ada': _L1_xcond_in['b_ada'], 'L1_xcond_W_qkv': _L1_xcond_in['W_qkv'], 'L1_xcond_b_qkv': _L1_xcond_in['b_qkv'], 'L1_xcond_W_proj': _L1_xcond_in['W_proj'], 'L1_xcond_b_proj': _L1_xcond_in['b_proj'], 'L1_xcond_W_ctx': _L1_xcond_in['W_ctx'], 'L1_xcond_b_ctx': _L1_xcond_in['b_ctx'], 'L1_xcond_W_q': _L1_xcond_in['W_q'], 'L1_xcond_W_k': _L1_xcond_in['W_k'], 'L1_xcond_W_v': _L1_xcond_in['W_v'], 'L1_xcond_W_out': _L1_xcond_in['W_out'], 'L1_xcond_b_out': _L1_xcond_in['b_out'], 'L1_xcond_W_fc1': _L1_xcond_in['W_fc1'], 'L1_xcond_b_fc1': _L1_xcond_in['b_fc1'], 'L1_xcond_W_fc2': _L1_xcond_in['W_fc2'], 'L1_xcond_b_fc2': _L1_xcond_in['b_fc2'], 'L2_xcond_ln1_w': _L2_xcond_in['ln1_w'], 'L2_xcond_ln1_b': _L2_xcond_in['ln1_b'], 'L2_xcond_g1_w': _L2_xcond_in['g1_w'], 'L2_xcond_g1_b': _L2_xcond_in['g1_b'], 'L2_xcond_b1_w': _L2_xcond_in['b1_w'], 'L2_xcond_b1_b': _L2_xcond_in['b1_b'], 'L2_xcond_ln2_w': _L2_xcond_in['ln2_w'], 'L2_xcond_ln2_b': _L2_xcond_in['ln2_b'], 'L2_xcond_g2_w': _L2_xcond_in['g2_w'], 'L2_xcond_g2_b': _L2_xcond_in['g2_b'], 'L2_xcond_b2_w': _L2_xcond_in['b2_w'], 'L2_xcond_b2_b': _L2_xcond_in['b2_b'], 'L2_xcond_sa_wq': _L2_xcond_in['sa_wq'], 'L2_xcond_sa_wkv': _L2_xcond_in['sa_wkv'], 'L2_xcond_sa_wo': _L2_xcond_in['sa_wo'], 'L2_xcond_sa_bo': _L2_xcond_in['sa_bo'], 'L2_xcond_ca_lnc_w': _L2_xcond_in['ca_lnc_w'], 'L2_xcond_ca_lnc_b': _L2_xcond_in['ca_lnc_b'], 'L2_xcond_ca_wq': _L2_xcond_in['ca_wq'], 'L2_xcond_ca_wkv': _L2_xcond_in['ca_wkv'], 'L2_xcond_ca_wo': _L2_xcond_in['ca_wo'], 'L2_xcond_ca_bo': _L2_xcond_in['ca_bo'], 'L2_xcond_ff_w1': _L2_xcond_in['ff_w1'], 'L2_xcond_ff_b1': _L2_xcond_in['ff_b1'], 'L2_xcond_ff_w2': _L2_xcond_in['ff_w2'], 'L2_xcond_ff_b2': _L2_xcond_in['ff_b2'], 'L3_xcond_ln1_w': _L3_xcond_in['ln1_w'], 'L3_xcond_ln1_b': _L3_xcond_in['ln1_b'], 'L3_xcond_ln2_w': _L3_xcond_in['ln2_w'], 'L3_xcond_ln2_b': _L3_xcond_in['ln2_b'], 'L3_xcond_ln3_w': _L3_xcond_in['ln3_w'], 'L3_xcond_ln3_b': _L3_xcond_in['ln3_b'], 'L3_xcond_Wqkv': _L3_xcond_in['Wqkv'], 'L3_xcond_bqkv': _L3_xcond_in['bqkv'], 'L3_xcond_Wos': _L3_xcond_in['Wos'], 'L3_xcond_bos': _L3_xcond_in['bos'], 'L3_xcond_Wq': _L3_xcond_in['Wq'], 'L3_xcond_bq': _L3_xcond_in['bq'], 'L3_xcond_Wk': _L3_xcond_in['Wk'], 'L3_xcond_bk': _L3_xcond_in['bk'], 'L3_xcond_Wv': _L3_xcond_in['Wv'], 'L3_xcond_bv': _L3_xcond_in['bv'], 'L3_xcond_Woc': _L3_xcond_in['Woc'], 'L3_xcond_boc': _L3_xcond_in['boc'], 'L3_xcond_W1': _L3_xcond_in['W1'], 'L3_xcond_b1': _L3_xcond_in['b1'], 'L3_xcond_W2': _L3_xcond_in['W2'], 'L3_xcond_b2': _L3_xcond_in['b2'], 'L3_xcond_Wmod': _L3_xcond_in['Wmod'], 'L3_xcond_bmod': _L3_xcond_in['bmod']}

def reference(x, cond_1024, ctx_768, L0_xcond_n1_w, L0_xcond_n1_b, L0_xcond_n2_w, L0_xcond_n2_b, L0_xcond_n3_w, L0_xcond_n3_b, L0_xcond_q1, L0_xcond_k1, L0_xcond_v1, L0_xcond_o1_w, L0_xcond_o1_b, L0_xcond_q2, L0_xcond_k2, L0_xcond_v2, L0_xcond_o2_w, L0_xcond_o2_b, L0_xcond_ff_w1, L0_xcond_ff_b1, L0_xcond_ff_w2, L0_xcond_ff_b2, L1_xcond_W_ada, L1_xcond_b_ada, L1_xcond_W_qkv, L1_xcond_b_qkv, L1_xcond_W_proj, L1_xcond_b_proj, L1_xcond_W_ctx, L1_xcond_b_ctx, L1_xcond_W_q, L1_xcond_W_k, L1_xcond_W_v, L1_xcond_W_out, L1_xcond_b_out, L1_xcond_W_fc1, L1_xcond_b_fc1, L1_xcond_W_fc2, L1_xcond_b_fc2, L2_xcond_ln1_w, L2_xcond_ln1_b, L2_xcond_g1_w, L2_xcond_g1_b, L2_xcond_b1_w, L2_xcond_b1_b, L2_xcond_ln2_w, L2_xcond_ln2_b, L2_xcond_g2_w, L2_xcond_g2_b, L2_xcond_b2_w, L2_xcond_b2_b, L2_xcond_sa_wq, L2_xcond_sa_wkv, L2_xcond_sa_wo, L2_xcond_sa_bo, L2_xcond_ca_lnc_w, L2_xcond_ca_lnc_b, L2_xcond_ca_wq, L2_xcond_ca_wkv, L2_xcond_ca_wo, L2_xcond_ca_bo, L2_xcond_ff_w1, L2_xcond_ff_b1, L2_xcond_ff_w2, L2_xcond_ff_b2, L3_xcond_ln1_w, L3_xcond_ln1_b, L3_xcond_ln2_w, L3_xcond_ln2_b, L3_xcond_ln3_w, L3_xcond_ln3_b, L3_xcond_Wqkv, L3_xcond_bqkv, L3_xcond_Wos, L3_xcond_bos, L3_xcond_Wq, L3_xcond_bq, L3_xcond_Wk, L3_xcond_bk, L3_xcond_Wv, L3_xcond_bv, L3_xcond_Woc, L3_xcond_boc, L3_xcond_W1, L3_xcond_b1, L3_xcond_W2, L3_xcond_b2, L3_xcond_Wmod, L3_xcond_bmod):
    import jax
    import jax.numpy as jnp

    def _L0_xcond_ref(x, t, context, n1_w, n1_b, n2_w, n2_b, n3_w, n3_b, q1, k1, v1, o1_w, o1_b, q2, k2, v2, o2_w, o2_b, ff_w1, ff_b1, ff_w2, ff_b2):
        import jax, jax.numpy as jnp
        import numpy as np
        EPS = 1e-05

        def _ada_ln(x, t, W, b):
            emb = t @ W + b
            scale, shift = jnp.split(emb, 2, axis=-1)
            mu = x.mean(-1, keepdims=True)
            var = ((x - mu) ** 2).mean(-1, keepdims=True)
            xn = (x - mu) * jax.lax.rsqrt(var + EPS)
            return xn * (1.0 + scale) + shift

        def _attn(x, ctx, Wq, Wk, Wv, Wo, bo, heads):
            b, n, _ = x.shape
            j = ctx.shape[1]
            q = (x @ Wq).reshape(b, n, heads, -1)
            k = (ctx @ Wk).reshape(b, j, heads, -1)
            v = (ctx @ Wv).reshape(b, j, heads, -1)
            scale = q.shape[-1] ** (-0.5)
            sim = jnp.einsum('bihd,bjhd->bhij', q, k) * scale
            attn = jax.nn.softmax(sim, axis=-1)
            out = jnp.einsum('bhij,bjhd->bihd', attn, v).reshape(b, n, -1)
            return out @ Wo + bo

        def _ff(x, W1, b1, W2, b2):
            p = x @ W1 + b1
            a, gate = jnp.split(p, 2, axis=-1)
            return a * jax.nn.gelu(gate, approximate=False) @ W2 + b2
        H = 16
        h = _ada_ln(x, t, n1_w, n1_b)
        x = _attn(h, h, q1, k1, v1, o1_w, o1_b, H) + x
        h = _ada_ln(x, t, n2_w, n2_b)
        x = _attn(h, context, q2, k2, v2, o2_w, o2_b, H) + x
        h = _ada_ln(x, t, n3_w, n3_b)
        x = _ff(h, ff_w1, ff_b1, ff_w2, ff_b2) + x
        return x

    def _L1_xcond_ref(x, c, text_embed, W_ada, b_ada, W_qkv, b_qkv, W_proj, b_proj, W_ctx, b_ctx, W_q, W_k, W_v, W_out, b_out, W_fc1, b_fc1, W_fc2, b_fc2):
        import jax, jax.numpy as jnp
        import numpy as np
        B, N, D, H, TD, TL = (4, 128, 128, 16, 96, 77)
        HD = D // H
        EPS = 1e-06

        def _ln(x):
            mu = jnp.mean(x, axis=-1, keepdims=True)
            var = jnp.var(x, axis=-1, keepdims=True)
            return (x - mu) * jax.lax.rsqrt(var + EPS)

        def _modulate(x, shift, scale):
            return x * (1.0 + scale[:, None, :]) + shift[:, None, :]

        def _heads(t):
            return t.reshape(t.shape[0], t.shape[1], H, HD).transpose(0, 2, 1, 3)

        def _attend(q, k, v):
            sim = jnp.einsum('bhid,bhjd->bhij', q, k) * HD ** (-0.5)
            attn = jax.nn.softmax(sim, axis=-1)
            out = jnp.einsum('bhij,bhjd->bhid', attn, v)
            return out.transpose(0, 2, 1, 3).reshape(out.shape[0], -1, D)
        mod = jax.nn.silu(c) @ W_ada + b_ada
        sh_msa, sc_msa, sh_x, sc_x, sh_mlp, sc_mlp = jnp.split(mod, 6, axis=-1)
        h1 = _modulate(_ln(x), sh_msa, sc_msa)
        qkv = h1 @ W_qkv + b_qkv
        q, k, v = jnp.split(qkv, 3, axis=-1)
        out = _attend(_heads(q), _heads(k), _heads(v))
        x = x + (out @ W_proj + b_proj)
        h2 = _modulate(_ln(x), sh_x, sc_x)
        ctx = text_embed @ W_ctx + b_ctx
        q = _heads(h2 @ W_q)
        k = _heads(ctx @ W_k)
        v = _heads(ctx @ W_v)
        out = _attend(q, k, v)
        x = x + (out @ W_out + b_out)
        h3 = _modulate(_ln(x), sh_mlp, sc_mlp)
        hidden = jax.nn.gelu(h3 @ W_fc1 + b_fc1, approximate=True)
        x = x + (hidden @ W_fc2 + b_fc2)
        return x

    def _L2_xcond_ref(x, cond, context, ln1_w, ln1_b, g1_w, g1_b, b1_w, b1_b, ln2_w, ln2_b, g2_w, g2_b, b2_w, b2_b, sa_wq, sa_wkv, sa_wo, sa_bo, ca_lnc_w, ca_lnc_b, ca_wq, ca_wkv, ca_wo, ca_bo, ff_w1, ff_b1, ff_w2, ff_b2):
        import jax, jax.numpy as jnp
        import numpy as np
        B, N, M = (2, 128, 64)
        D, H, DH = (128, 16, 64)
        MID = H * DH
        DC = 96
        MULT = 4
        EPS = 1e-05

        def _ln(x, w, b):
            mu = jnp.mean(x, -1, keepdims=True)
            var = jnp.mean((x - mu) ** 2, -1, keepdims=True)
            return (x - mu) * jax.lax.rsqrt(var + EPS) * w + b

        def _sincos(n, d):
            inv = 1.0 / 10000.0 ** (jnp.arange(0, d, 2, dtype=jnp.float32) / d)
            ang = jnp.arange(n, dtype=jnp.float32)[:, None] * inv[None, :]
            return (jnp.sin(ang), jnp.cos(ang))

        def _rope(x, sin, cos):
            s = sin[None, None]
            c = cos[None, None]
            xe = x[..., ::2]
            xo = x[..., 1::2]
            re = xe * c - xo * s
            ro = xe * s + xo * c
            return jnp.stack((re, ro), axis=-1).reshape(x.shape)

        def _heads(t):
            b, n, _ = t.shape
            return t.reshape(b, n, H, DH).transpose(0, 2, 1, 3)

        def _attn(xq, ctx, wq, wkv, wo, bo):
            q = _heads(xq @ wq)
            k, v = jnp.split(ctx @ wkv, 2, axis=-1)
            k = _heads(k)
            v = _heads(v)
            sq, cq = _sincos(q.shape[2], DH)
            sk, ck = _sincos(k.shape[2], DH)
            q = _rope(q, sq, cq)
            k = _rope(k, sk, ck)
            sim = jnp.einsum('bhnd,bhmd->bhnm', q, k) * DH ** (-0.5)
            a = jax.nn.softmax(sim, axis=-1)
            o = jnp.einsum('bhnm,bhmd->bhnd', a, v)
            o = o.transpose(0, 2, 1, 3).reshape(xq.shape[0], xq.shape[1], MID)
            return o @ wo + bo

        def _adaln(x, c, lw, lb, gw, gb, bw, bb):
            g = (c @ gw + gb)[:, None, :]
            bt = (c @ bw + bb)[:, None, :]
            return _ln(x, lw, lb) * (1.0 + g) + bt
        attn_in = _adaln(x, cond, ln1_w, ln1_b, g1_w, g1_b, b1_w, b1_b)
        x = _attn(attn_in, attn_in, sa_wq, sa_wkv, sa_wo, sa_bo) + x
        cross_in = _adaln(x, cond, ln1_w, ln1_b, g1_w, g1_b, b1_w, b1_b)
        ctx_n = _ln(context, ca_lnc_w, ca_lnc_b)
        x = _attn(cross_in, ctx_n, ca_wq, ca_wkv, ca_wo, ca_bo) + x
        ffn_in = _adaln(x, cond, ln2_w, ln2_b, g2_w, g2_b, b2_w, b2_b)
        h = jax.nn.gelu(ffn_in @ ff_w1 + ff_b1, approximate=False)
        x = h @ ff_w2 + ff_b2 + x
        return x

    def _L3_xcond_ref(x, context, time_emb, ln1_w, ln1_b, ln2_w, ln2_b, ln3_w, ln3_b, Wqkv, bqkv, Wos, bos, Wq, bq, Wk, bk, Wv, bv, Woc, boc, W1, b1, W2, b2, Wmod, bmod):
        import jax, jax.numpy as jnp
        import numpy as np
        D = 128
        CD = 96
        H = 16
        HD = D // H
        EPS = 1e-05

        def _ln(x, w, b):
            m = jnp.mean(x, axis=-1, keepdims=True)
            v = jnp.var(x, axis=-1, keepdims=True)
            return (x - m) * jax.lax.rsqrt(v + EPS) * w + b

        def _attn(q, k, v):
            q = q.reshape(q.shape[0], q.shape[1], H, HD).transpose(0, 2, 1, 3)
            k = k.reshape(k.shape[0], k.shape[1], H, HD).transpose(0, 2, 1, 3)
            v = v.reshape(v.shape[0], v.shape[1], H, HD).transpose(0, 2, 1, 3)
            scores = jnp.einsum('bhnd,bhmd->bhnm', q, k) * HD ** (-0.5)
            p = jax.nn.softmax(scores, axis=-1)
            o = jnp.einsum('bhnm,bhmd->bhnd', p, v)
            return o.transpose(0, 2, 1, 3).reshape(o.shape[0], o.shape[2], D)
        mod = jax.nn.silu(time_emb) @ Wmod + bmod
        sh1, sc1, sh2, sc2, sh3, sc3 = jnp.split(mod, 6, axis=-1)
        h = _ln(x, ln1_w, ln1_b) * (1 + sc1[:, None, :]) + sh1[:, None, :]
        qkv = h @ Wqkv + bqkv
        q, k, v = jnp.split(qkv, 3, axis=-1)
        x = x + _attn(q, k, v) @ Wos + bos
        h = _ln(x, ln2_w, ln2_b) * (1 + sc2[:, None, :]) + sh2[:, None, :]
        x = x + _attn(h @ Wq + bq, context @ Wk + bk, context @ Wv + bv) @ Woc + boc
        h = _ln(x, ln3_w, ln3_b) * (1 + sc3[:, None, :]) + sh3[:, None, :]
        x = x + jax.nn.gelu(h @ W1 + b1, approximate=False) @ W2 + b2
        return x
    x = _L0_xcond_ref(x, cond_1024[:, None, :], ctx_768, L0_xcond_n1_w, L0_xcond_n1_b, L0_xcond_n2_w, L0_xcond_n2_b, L0_xcond_n3_w, L0_xcond_n3_b, L0_xcond_q1, L0_xcond_k1, L0_xcond_v1, L0_xcond_o1_w, L0_xcond_o1_b, L0_xcond_q2, L0_xcond_k2, L0_xcond_v2, L0_xcond_o2_w, L0_xcond_o2_b, L0_xcond_ff_w1, L0_xcond_ff_b1, L0_xcond_ff_w2, L0_xcond_ff_b2)
    x = _L1_xcond_ref(x, cond_1024, ctx_768, L1_xcond_W_ada, L1_xcond_b_ada, L1_xcond_W_qkv, L1_xcond_b_qkv, L1_xcond_W_proj, L1_xcond_b_proj, L1_xcond_W_ctx, L1_xcond_b_ctx, L1_xcond_W_q, L1_xcond_W_k, L1_xcond_W_v, L1_xcond_W_out, L1_xcond_b_out, L1_xcond_W_fc1, L1_xcond_b_fc1, L1_xcond_W_fc2, L1_xcond_b_fc2)
    x = _L2_xcond_ref(x, cond_1024, ctx_768, L2_xcond_ln1_w, L2_xcond_ln1_b, L2_xcond_g1_w, L2_xcond_g1_b, L2_xcond_b1_w, L2_xcond_b1_b, L2_xcond_ln2_w, L2_xcond_ln2_b, L2_xcond_g2_w, L2_xcond_g2_b, L2_xcond_b2_w, L2_xcond_b2_b, L2_xcond_sa_wq, L2_xcond_sa_wkv, L2_xcond_sa_wo, L2_xcond_sa_bo, L2_xcond_ca_lnc_w, L2_xcond_ca_lnc_b, L2_xcond_ca_wq, L2_xcond_ca_wkv, L2_xcond_ca_wo, L2_xcond_ca_bo, L2_xcond_ff_w1, L2_xcond_ff_b1, L2_xcond_ff_w2, L2_xcond_ff_b2)
    x = _L3_xcond_ref(x, ctx_768, cond_1024, L3_xcond_ln1_w, L3_xcond_ln1_b, L3_xcond_ln2_w, L3_xcond_ln2_b, L3_xcond_ln3_w, L3_xcond_ln3_b, L3_xcond_Wqkv, L3_xcond_bqkv, L3_xcond_Wos, L3_xcond_bos, L3_xcond_Wq, L3_xcond_bq, L3_xcond_Wk, L3_xcond_bk, L3_xcond_Wv, L3_xcond_bv, L3_xcond_Woc, L3_xcond_boc, L3_xcond_W1, L3_xcond_b1, L3_xcond_W2, L3_xcond_b2, L3_xcond_Wmod, L3_xcond_bmod)
    return x

_drawn_inputs = setup_inputs


def setup_inputs(seed=0):
    import zlib

    import numpy as np

    out = dict(_drawn_inputs(seed))
    spreads = {'L0_xcond_n1_b': (0.0, 0.508),
     'L0_xcond_n2_b': (0.0, 0.8),
     'L0_xcond_n3_b': (0.0, 0.8),
     'L0_xcond_o1_b': (0.0, 0.1),
     'L0_xcond_o2_b': (0.0, 0.1),
     'L0_xcond_ff_b1': (0.0, 0.8),
     'L0_xcond_ff_b2': (0.0, 0.662),
     'L1_xcond_b_ada': (0.0, 0.8),
     'L1_xcond_b_qkv': (0.0, 2.0),
     'L1_xcond_b_proj': (0.0, 0.607),
     'L1_xcond_b_ctx': (0.0, 0.8),
     'L1_xcond_b_out': (0.0, 0.8),
     'L1_xcond_b_fc1': (0.0, 2.0),
     'L1_xcond_b_fc2': (0.0, 0.8),
     'L2_xcond_ln1_w': (1.0, 0.6),
     'L2_xcond_ln1_b': (0.0, 2.0),
     'L2_xcond_g1_b': (0.0, 2.0),
     'L2_xcond_b1_b': (0.0, 2.0),
     'L2_xcond_ln2_w': (1.0, 0.6),
     'L2_xcond_ln2_b': (0.0, 2.0),
     'L2_xcond_g2_b': (0.0, 2.0),
     'L2_xcond_b2_b': (0.0, 2.0),
     'L2_xcond_sa_bo': (0.0, 0.8),
     'L2_xcond_ca_lnc_w': (1.0, 0.6),
     'L2_xcond_ca_lnc_b': (0.0, 2.0),
     'L2_xcond_ca_bo': (0.0, 0.8),
     'L2_xcond_ff_b1': (0.0, 2.0),
     'L2_xcond_ff_b2': (0.0, 0.8),
     'L3_xcond_ln1_w': (1.0, 0.6),
     'L3_xcond_ln1_b': (0.0, 2.0),
     'L3_xcond_ln2_w': (1.0, 0.6),
     'L3_xcond_ln2_b': (0.0, 2.0),
     'L3_xcond_ln3_w': (1.0, 0.6),
     'L3_xcond_ln3_b': (0.0, 2.0),
     'L3_xcond_bqkv': (0.0, 2.0),
     'L3_xcond_bos': (0.0, 0.781),
     'L3_xcond_bq': (0.0, 2.0),
     'L3_xcond_bk': (0.0, 2.0),
     'L3_xcond_bv': (0.0, 2.0),
     'L3_xcond_boc': (0.0, 0.8),
     'L3_xcond_b1': (0.0, 2.0),
     'L3_xcond_b2': (0.0, 0.8),
     'L3_xcond_bmod': (0.0, 2.0)}
    factors = {'L0_xcond_n2_w': 8.0,
     'L0_xcond_n3_w': 8.0,
     'L0_xcond_q1': 8.0,
     'L0_xcond_k1': 8.0,
     'L0_xcond_q2': 8.0,
     'L0_xcond_k2': 8.0,
     'L0_xcond_ff_w1': 3.735,
     'L0_xcond_ff_w2': 3.694,
     'L1_xcond_W_ada': 4.459,
     'L1_xcond_W_qkv': 4.854,
     'L1_xcond_W_ctx': 8.0,
     'L1_xcond_W_q': 8.0,
     'L1_xcond_W_k': 8.0,
     'L1_xcond_W_v': 7.761,
     'L1_xcond_W_out': 7.843,
     'L2_xcond_g1_w': 6.927,
     'L2_xcond_g2_w': 26.21,
     'L2_xcond_b2_w': 38.464,
     'L2_xcond_sa_wq': 21.677,
     'L2_xcond_ca_wq': 64.0,
     'L3_xcond_Wqkv': 2.922,
     'L3_xcond_Wq': 64.0,
     'L3_xcond_Wk': 64.0,
     'L3_xcond_Wmod': 13.25,
     'L1_xcond_W_fc1': 6.002,
     'L1_xcond_W_fc2': 4.189,
     'L2_xcond_b1_w': 8.0,
     'L2_xcond_ca_wkv': 3.853,
     'L2_xcond_ca_wo': 3.911,
     'L2_xcond_ff_w1': 3.112,
     'L2_xcond_ff_w2': 2.699,
     'L3_xcond_Wv': 8.0,
     'L3_xcond_Woc': 5.996,
     'L3_xcond_W1': 4.528,
     'L3_xcond_W2': 3.598}
    for name, (base, spread) in spreads.items():
        noise = np.random.default_rng([zlib.crc32(name.encode()), seed]).standard_normal(out[name].shape)
        drawn = base * np.exp(spread * noise) if base else spread * noise
        out[name] = jnp.asarray(drawn.astype(out[name].dtype))
    for name, factor in factors.items():
        out[name] = (out[name] * factor).astype(out[name].dtype)
    return out
```

```python
import concourse.bass as bass
from concourse import mybir
from contextlib import ExitStack
import numpy as np

F32 = mybir.dt.float32
ACT = mybir.ActivationFunctionType
ALU = mybir.AluOpType
AXX = mybir.AxisListType.X

NB, N, D = 8, 256, 128
J, CD = 64, 96
H = 16
P = 128
NT = N // P
STREAMS = 2
NORMS = 11

WEIGHTS = [
    [("q1", 1, 1024), ("k1", 1, 1024), ("v1", 1, 1024), ("o1_w", 8, 128), ("q2", 1, 1024), ("k2", 1, 1024),
     ("v2", 1, 1024), ("o2_w", 8, 128), ("ff_w1", 1, 1024), ("ff_w2", 4, 128)],
    [("W_qkv", 1, 384), ("W_proj", 1, 128), ("W_ctx", 1, 128), ("W_q", 1, 128), ("W_k", 1, 128), ("W_v", 1, 128),
     ("W_out", 1, 128), ("W_fc1", 1, 512), ("W_fc2", 4, 128)],
    [("sa_wq", 1, 1024), ("sa_wkv", 1, 2048), ("sa_wo", 8, 128), ("ca_wq", 1, 1024), ("ca_wkv", 1, 2048),
     ("ca_wo", 8, 128), ("ff_w1", 1, 512), ("ff_w2", 4, 128)],
    [("Wqkv", 1, 384), ("Wos", 1, 128), ("Wq", 1, 128), ("Wk", 1, 128), ("Wv", 1, 128), ("Woc", 1, 128),
     ("W1", 1, 512), ("W2", 4, 128)],
]

MODS = (
    [(0, f"n{m}_w", c) for m in (1, 2, 3) for c in (0, 1)]
    + [(1, "W_ada", c) for c in (1, 0, 3, 2, 5, 4)]
    + [(2, n, 0) for n in ("g1_w", "b1_w", "g2_w", "b2_w")]
    + [(3, "Wmod", c) for c in (1, 0, 3, 2, 5, 4)]
)
MOD_BIAS = (
    [(0, f"n{m}_b", c) for m in (1, 2, 3) for c in (0, 1)]
    + [(1, "b_ada", c) for c in (1, 0, 3, 2, 5, 4)]
    + [(2, n, 0) for n in ("g1_b", "b1_b", "g2_b", "b2_b")]
    + [(3, "bmod", c) for c in (1, 0, 3, 2, 5, 4)]
)
VECS = [(0, "ff_b1", 8), (1, "b_qkv", 3), (1, "b_ctx", 1), (1, "b_fc1", 4), (2, "ca_lnc_w", 1), (2, "ca_lnc_b", 1),
        (2, "ff_b1", 4), (3, "bqkv", 3), (3, "bq", 1), (3, "bk", 1), (3, "bv", 1), (3, "b1", 4)]
OUT_BIAS = [(0, "o1_b"), (0, "o2_b"), (0, "ff_b2"), (1, "b_proj"), (1, "b_out"), (1, "b_fc2"),
            (2, "sa_bo"), (2, "ca_bo"), (2, "ff_b2"), (3, "bos"), (3, "boc"), (3, "b2")]

BLOCKS = [
    dict(kind="self", layer=0, norm=0, hd=64, q=("q1", 0), k=("k1", 0), v=("v1", 0), o="o1_w"),
    dict(kind="cross", layer=0, norm=1, hd=64, q=("q2", 0), k=("k2", 0), v=("v2", 0), o="o2_w"),
    dict(kind="ff", layer=0, norm=2, w1="ff_w1", b1="ff_b1", w2="ff_w2", act="glu"),
    dict(kind="self", layer=1, norm=3, hd=8, q=("W_qkv", 0), k=("W_qkv", 128), v=("W_qkv", 256), o="W_proj",
         bq=("b_qkv", 0), bk=("b_qkv", 1), bv=("b_qkv", 2)),
    dict(kind="cross", layer=1, norm=4, hd=8, q=("W_q", 0), k=("W_k", 0), v=("W_v", 0), o="W_out", project=True),
    dict(kind="ff", layer=1, norm=5, w1="W_fc1", b1="b_fc1", w2="W_fc2", act="tanh"),
    dict(kind="self", layer=2, norm=6, hd=64, q=("sa_wq", 0), k=("sa_wkv", 0), v=("sa_wkv", 1024), o="sa_wo",
         rope=True),
    dict(kind="cross", layer=2, norm=6, hd=64, q=("ca_wq", 0), k=("ca_wkv", 0), v=("ca_wkv", 1024), o="ca_wo",
         rope=True, normed=True),
    dict(kind="ff", layer=2, norm=7, w1="ff_w1", b1="ff_b1", w2="ff_w2", act="erf"),
    dict(kind="self", layer=3, norm=8, hd=8, q=("Wqkv", 0), k=("Wqkv", 128), v=("Wqkv", 256), o="Wos",
         bq=("bqkv", 0), bk=("bqkv", 1), bv=("bqkv", 2)),
    dict(kind="cross", layer=3, norm=9, hd=8, q=("Wq", 0), k=("Wk", 0), v=("Wv", 0), o="Woc",
         bq=("bq", 0), bk=("bk", 0), bv=("bv", 0)),
    dict(kind="ff", layer=3, norm=10, w1="W1", b1="b1", w2="W2", act="erf"),
]
EPS = [1e-5, 1e-6, 1e-5, 1e-5]
LENGTH = [{("self", 64): 60, ("self", 8): 52, ("cross", 64): 32, ("cross", 8): 32, ("ff", 0): 12}[
    b["kind"], b.get("hd", 0)] for b in BLOCKS]
START = [sum(LENGTH[:k]) for k in range(len(BLOCKS))]
LAG = 30
STEP = {64: 5, 8: 4}

ORDER8 = [(4 * (2 * (p % 2)) + p // 2, 4 * (2 * (p % 2) + 1) + p // 2) for p in range(8)]

CONSTS = dict(ident=128, mask16=16, mask64=2, mask_rope=2, cos_q=N, sin_q=N, cos_k=N, sin_k=N)


def columns(sizes):
    at, out = 0, {}
    for name, n in sizes:
        out[name] = (at, at + n)
        at += n
    return out, at


WCOLS = [columns([(n, c * w) for n, c, w in ws]) for ws in WEIGHTS]
CCOLS = columns(CONSTS.items())
VCOLS = columns([("mod_bias", 2 * NORMS), ("ln_w", NORMS), ("ln_b", NORMS), ("cond", NB)]
                + [((la, n), c) for la, n, c in VECS])


class Signal:

    def __init__(self, sem, counts):
        self.sem, self.counts, self.n = sem, counts, 0

    def mark(self, *label):
        self.n += 1
        assert self.counts.setdefault(label, self.n) == self.n, label
        return self.sem, 1

    def at(self, *label):
        return self.sem, self.counts.get(label, 1)


def in_turn(programs, lags):
    times = [next(g) + lag for g, lag in zip(programs, lags)]
    while min(times) < float("inf"):
        s = times.index(min(times))
        following = next(programs[s], float("inf")) + lags[s]
        assert following >= times[s], "a stream's steps must come in the order of their times"
        times[s] = following


def program(nc, t, counts):
    ctx = ExitStack()
    with ctx:
        def sb(name, shape):
            return ctx.enter_context(nc.sbuf_tensor(name, shape, F32))

        consts = sb("consts", [P, CCOLS[1]])
        vecs = sb("vecs", [P, VCOLS[1]])
        out_bias = sb("out_bias", [P, len(BLOCKS), D])
        weights = [sb(f"weights{la}", [P, WCOLS[la][1]]) for la in range(4)]
        mod_all = sb("mod_all", [P, NB, 2 * NORMS])
        silu = sb("silu", [P, 4, NB])
        minus_half = sb("minus_half", [P, 2])

        def const(name):
            a, b = CCOLS[0][name]
            return consts[:, a:b]

        def vec(key, i=0, n=1):
            a = VCOLS[0][key][0] + i
            return vecs[:, a:a + n]

        def w(layer, name, rows=P):
            a, b = WCOLS[layer][0][name]
            return weights[layer][0:rows, a:b]

        ident, mask16, mask64, mask_rope = (const(n) for n in ("ident", "mask16", "mask64", "mask_rope"))
        table = {"q": (const("cos_q"), const("sin_q")), "k": (const("cos_k"), const("sin_k"))}

        class Stream:
            pass

        S = []
        for s in range(STREAMS):
            b = Stream()
            b.x = sb(f"x{s}", [P, NT, D])
            b.xb = sb(f"x_plus_bias{s}", [P, NT, D])
            b.xn = sb(f"x_normed{s}", [P, NT, D])
            b.hT = sb(f"hT{s}", [P, N])
            b.mod = sb(f"mod{s}", [P, 2 * NORMS])
            b.stats = sb(f"stats{s}", [P, NT, 6])
            b.mv = sb(f"mean_var{s}", [P, NT, 2])
            b.ve = sb(f"var_eps{s}", [P, NT])
            b.rstd = sb(f"rstd{s}", [P, NT])
            b.ctx = sb(f"ctx{s}", [J, CD])
            b.ctxT = sb(f"ctxT{s}", [CD, 2 * J])
            b.ctx_nT = sb(f"ctx_nT{s}", [P, 2 * J])
            b.ctx_n = sb(f"ctx_n{s}", [J, CD])
            b.cstats = sb(f"cstats{s}", [J, 6])
            b.cmv = sb(f"cmv{s}", [J, 2])
            b.cve = sb(f"cve{s}", [J, 2])
            b.qT = sb(f"qT{s}", [P, 8, N])
            b.kk = sb(f"keys{s}", [P, 16 * N])
            b.v = sb(f"values{s}", [P, NT * 1024])
            b.p = sb(f"probs{s}", [P, 2, 1024])
            b.pT = sb(f"probsT{s}", [P, 2, 512])
            b.nm = sb(f"negmax{s}", [P, 32])
            b.sums = sb(f"sums{s}", [P, 32])
            b.rs = sb(f"rsums{s}", [P, 32])
            b.bank = {n: ctx.enter_context(nc.psum_tensor(f"psum_{n}{s}", [P, 512], F32)) for n in ("A", "B", "T", "O")}
            S.append(b)

        sem_numbers = []

        def sem(name):
            x = ctx.enter_context(nc.semaphore(name))
            return x

        consts_loaded = sem("consts_loaded")
        mods_loaded = sem("mods_loaded")
        weights_loaded = [sem(f"weights_loaded{la}") for la in range(4)]
        pre_act, pre_dve, pre_pe = sem("pre_act"), sem("pre_dve"), sem("pre_pe")

        def signal(name):
            x = sem(name)
            sem_numbers.append(x.num)
            return Signal(x, counts.setdefault(name, {}))

        for s, b in enumerate(S):
            b.x_loaded = signal(f"x_loaded{s}").sem
            b.ctx_loaded = signal(f"ctx_loaded{s}").sem
            b.stored = signal(f"stored{s}").sem
            b.pe = signal(f"tensor_done{s}")
            b.act = signal(f"scalar_done{s}")
            b.dve = signal(f"vector_done{s}")
            b.pool = signal(f"gpsimd_done{s}")

        mod_w = S[0].kk[:, 0:2 * NORMS * D]
        with nc.Block() as block:

            @block.sync
            def _(sp):
                sp.dma_start(vecs[:, :], t["vecs"]).then_inc(mods_loaded, 16)
                sp.dma_start(mod_w, t["mod_w"]).then_inc(mods_loaded, 16)
                sp.dma_start(consts[:, :], t["consts"]).then_inc(consts_loaded, 16)
                sp.dma_start(out_bias[:, :, :].rearrange("p k d -> p (k d)"),
                             t["out_bias"].partition_broadcast(P)).then_inc(consts_loaded, 16)
                for la in range(4):
                    sp.dma_start(weights[la][:, :], t[f"weights{la}"]).then_inc(weights_loaded[la], 16)
                sp.wait_ge(consts_loaded, 32)
                sp.wait_ge(mods_loaded, 32)

            @block.scalar
            def _(act):
                act.wait_ge(mods_loaded, 32)
                nc.scalar.activation(silu[:, 0, :], vec("cond", 0, NB), ACT.Exp, scale=-1.0).then_inc(pre_act, 1)

            @block.tensor
            def _(pe):
                ps = S[0].bank["A"]
                pe.wait_ge(mods_loaded, 32)
                pe.wait_ge(pre_dve, 4)
                for j, (la, _, _) in enumerate(MODS):
                    rhs = silu[:, 3, :] if la in (1, 3) else vec("cond", 0, NB)
                    last = nc.tensor.matmul(ps[:, j * NB:(j + 1) * NB], mod_w[:, j * D:(j + 1) * D], rhs,
                                            start=True, stop=True)
                last.then_inc(pre_pe, 1)

            @block.vector
            def _(dve):
                nc.vector.memset(minus_half[:, :], -0.5).then_inc(pre_dve, 1)
                dve.wait_ge(pre_act, 1)
                nc.vector.tensor_scalar(silu[:, 1, :], silu[:, 0, :], 1.0, None, ALU.add).then_inc(pre_dve, 1)
                dve.wait_ge(pre_dve, 2)
                nc.vector.reciprocal(silu[:, 2, :], silu[:, 1, :]).then_inc(pre_dve, 1)
                dve.wait_ge(pre_dve, 3)
                dve.wait_ge(mods_loaded, 32)
                nc.vector.tensor_tensor(silu[:, 3, :], silu[:, 2, :], vec("cond", 0, NB), ALU.mult).then_inc(pre_dve, 1)
                dve.wait_ge(pre_pe, 1)
                m = mod_all[:, :, :].rearrange("p b j -> p j b")
                nc.vector.tensor_tensor(m, S[0].bank["A"][:, 0:2 * NORMS * NB].rearrange("p (j b) -> p j b", b=NB),
                                        vec("mod_bias", 0, 2 * NORMS).unsqueeze(2).broadcast_to([P, 2 * NORMS, NB]),
                                        ALU.add).then_inc(pre_dve, 1)
                sc = mod_all[:, :, 0:2 * NORMS:2]
                sh = mod_all[:, :, 1:2 * NORMS:2]
                tmp = S[0].p[:, 0, 0:NB * NORMS].rearrange("p (b m) -> p b m", b=NB)
                dve.wait_ge(pre_dve, 5)
                nc.vector.tensor_scalar(tmp, sc, 1.0, None, ALU.add).then_inc(pre_dve, 1)
                dve.wait_ge(pre_dve, 6)
                nc.vector.tensor_tensor(sc, tmp, vec("ln_w", 0, NORMS).unsqueeze(1).broadcast_to([P, NB, NORMS]),
                                        ALU.mult).then_inc(pre_dve, 1)
                tmp2 = S[0].p[:, 1, 0:NB * NORMS].rearrange("p (b m) -> p b m", b=NB)
                nc.vector.tensor_tensor(tmp2, tmp, vec("ln_b", 0, NORMS).unsqueeze(1).broadcast_to([P, NB, NORMS]),
                                        ALU.mult).then_inc(pre_dve, 1)
                dve.wait_ge(pre_dve, 8)
                nc.vector.tensor_tensor(sh, sh, tmp2, ALU.add).then_inc(pre_dve, 1)


        def tensor_program(s, pe):
            b = S[s]
            reader = {}

            def claim(name, sig, *label):
                if name in reader:
                    pe.wait_ge(*reader[name])
                reader[name] = sig.at(*label)
                return b.bank[name]

            def mm(out, lhsT, rhs, start=True, stop=True):
                return nc.tensor.matmul(out, lhsT, rhs, start=start, stop=stop)

            def tr(out, in_, n=P):
                return nc.tensor.transpose(out, in_, ident[0:n, 0:n])

            def mm_swapped(out, lhsT, rhs):
                mm(out[0:64, :], lhsT[:, 64:P], rhs)
                return mm(out[64:P, :], lhsT[:, 0:64], rhs)

            for k, blk in enumerate(BLOCKS):
                t0, kind, la = START[k], blk["kind"], blk["layer"]
                yield t0 + 2
                T = claim("T", b.act, k, "hT")
                for ti in range(NT):
                    pe.wait_ge(*b.dve.at(k, "xn", ti))
                    last = tr(T[:, ti * P:(ti + 1) * P], b.xn[:, ti, :])
                last.then_inc(*b.pe.mark(k, "xnT"))
                pe.wait_ge(weights_loaded[la], 16)
                ctxT = b.ctxT
                if kind == "cross":
                    if k == 1:
                        pe.wait_ge(b.ctx_loaded, 32)
                    if blk.get("normed"):
                        yield t0 + 2.5
                        O = claim("O", b.act, k, "ctx_nT")
                        pe.wait_ge(*b.dve.at(k, "ctx_n"))
                        tr(O[0:CD, 0:J], b.ctx_n[:, :], J).then_inc(*b.pe.mark(k, "ctxT"))
                        ctxT = b.ctx_nT[0:CD, :]
                    if blk.get("project"):
                        yield t0 + 2.5
                        O = claim("O", b.act, k, "ctx_nT")
                        mm(O[:, 0:2 * J], w(la, "W_ctx", CD), b.ctxT[:, :]).then_inc(*b.pe.mark(k, "ctxT"))
                        ctxT = b.ctx_nT
                rows = P if blk.get("project") else CD

                if kind in ("self", "cross"):
                    wq = w(la, blk["q"][0])[:, blk["q"][1]:]
                    hd, rope = blk["hd"], blk.get("rope")
                    q_maker = b.pool if rope else b.act if hd == 64 else b.dve
                    if kind == "cross":
                        yield t0 + 2.8
                        wk = w(la, blk["k"][0], rows)[:, blk["k"][1]:]
                        wv = w(la, blk["v"][0], rows)[:, blk["v"][1]:]
                        if k == 7 or k == 4:
                            pe.wait_ge(*b.act.at(k, "ctx_nT"))
                        if hd == 64:
                            A = claim("A", b.dve, k, "k_cos" if rope else "k")
                            for c in range(8):
                                last = mm(A[:, c * J:(c + 1) * J], wk[:, c * P:(c + 1) * P], ctxT[:, 0:J])
                            last.then_inc(*b.pe.mark(k, "k"))
                            if rope:
                                B = claim("B", b.dve, k, "k_sin")
                                for c in range(8):
                                    last = mm_swapped(B[:, c * J:(c + 1) * J], wk[:, c * P:(c + 1) * P], ctxT[:, 0:J])
                                last.then_inc(*b.pe.mark(k, "k_swapped"))
                            for half in range(2):
                                B = claim("BA"[half], b.act, k, "v", half)
                                mm(B[:, :], ctxT[:, :], wv[:, half * 512:(half + 1) * 512])\
                                    .then_inc(*b.pe.mark(k, "v", half))
                        else:
                            A = claim("A", b.act, k, "k_plain")
                            mm(A[:, 0:J], wk[:, 0:P], ctxT[:, 0:J]).then_inc(*b.pe.mark(k, "k"))
                            B = claim("B", b.dve, k, "v")
                            mm(B[:, 0:D], ctxT[:, :], wv[:, 0:P]).then_inc(*b.pe.mark(k, "v"))
                    yield t0 + 4
                    pe.wait_ge(*b.act.at(k, "hT"))
                    if hd == 64:
                        for g in range(4):
                            if g:
                                yield t0 + 4 + 1.2 * g
                            names = ("A", "B") if rope else ("AT"[g % 2],)
                            for r, name in enumerate(names):
                                A = claim(name, *((b.dve, k, ("q_cos", "q_sin")[r], g) if rope else (b.act, k, "q", g)))
                                for i in range(2):
                                    c = 2 * g + i
                                    lhsT = wq[:, c * P:(c + 1) * P]
                                    last = (mm_swapped if r else mm)(A[:, i * N:(i + 1) * N], lhsT, b.hT[:, :])
                                last.then_inc(*b.pe.mark(k, ("q", "q_swapped")[r], g))
                            if kind == "self":
                                wk = w(la, blk["k"][0])[:, blk["k"][1]:]
                                names = ("T", "O") if rope else ("BO"[g % 2],)
                                for r, name in enumerate(names):
                                    A = claim(name, b.dve, k, *((("k_cos", "k_sin")[r], g) if rope else ("k", g)))
                                    for i in range(2):
                                        c = 2 * g + i
                                        lhsT = wk[:, c * P:(c + 1) * P]
                                        last = (mm_swapped if r else mm)(A[:, i * N:(i + 1) * N], lhsT, b.hT[:, :])
                                    last.then_inc(*b.pe.mark(k, ("k", "k_swapped")[r], g))
                    else:
                        A = claim("A", b.dve, k, "q", 0)
                        mm(A[:, 0:N], wq[:, 0:P], b.hT[:, :]).then_inc(*b.pe.mark(k, "q", 0))
                        if kind == "self":
                            wk = w(la, blk["k"][0])[:, blk["k"][1]:]
                            A = claim("B", b.act, k, "k_plain")
                            mm(A[:, 0:N], wk[:, 0:P], b.hT[:, :]).then_inc(*b.pe.mark(k, "k", 0))
                    if kind == "self":
                        wv = w(la, blk["v"][0])[:, blk["v"][1]:]
                        if hd == 64:
                            for ti in range(NT):
                                yield t0 + 9 + ti
                                for half in range(2):
                                    A = claim(("AT", "BO")[half][ti], b.act, k, "v", ti, half)
                                    mm(A[:, :], b.hT[:, ti * P:(ti + 1) * P], wv[:, half * 512:(half + 1) * 512])\
                                        .then_inc(*b.pe.mark(k, "v", ti, half))
                        else:
                            A = claim("T", b.dve, k, "v")
                            for ti in range(NT):
                                last = mm(A[:, ti * P:(ti + 1) * P], b.hT[:, ti * P:(ti + 1) * P], wv[:, 0:P])
                            last.then_inc(*b.pe.mark(k, "v"))

                if kind == "self":
                    t1 = t0 + 12
                    for p in range(8 + 1):
                        if p < 8:
                            yield t1 + STEP[hd] * p
                            if p == 0:
                                for g in range(4 if hd == 64 else 1):
                                    pe.wait_ge(*q_maker.at(k, "q", g))
                                    if hd == 64:
                                        pe.wait_ge(*b.dve.at(k, "k", g))
                            if hd == 8:
                                pe.wait_ge(*b.dve.at(k, "kmask", p))
                            for ti in range(NT):
                                A = claim("AB"[ti], b.act, k, "exp", p, ti)
                                qc = b.qT[:, p if hd == 64 else 0, ti * P:(ti + 1) * P]
                                mm(A[:, :], qc, b.kk[:, p * 512:(p + 1) * 512]).then_inc(*b.pe.mark(k, "scores", p, ti))
                        if p > 0:
                            r = p - 1
                            for h2 in range(2):
                                yield t1 + STEP[hd] * p + 1 + h2
                                T = claim("T", (b.act, b.dve)[h2], k, "pT", r, h2)
                                pe.wait_ge(*b.dve.at(k, "norm", r))
                                for kt in range(NT):
                                    for ti in range(NT):
                                        last = tr(T[:, kt * N + ti * P:kt * N + (ti + 1) * P],
                                                  b.p[:, r % 2, (ti * 2 + h2) * N + kt * P:(ti * 2 + h2) * N + (kt + 1) * P])
                                last.then_inc(*b.pe.mark(k, "T", r, h2))
                            yield t1 + STEP[hd] * p + 3.5
                            if hd == 64 or r == 0:
                                O = claim("O", b.act, k, "attn", r if hd == 64 else 0)
                            if r == 0:
                                for ti in range(NT):
                                    for half in range(2):
                                        if hd == 64:
                                            pe.wait_ge(*b.act.at(k, "v", ti, half))
                                if hd == 8:
                                    pe.wait_ge(*b.dve.at(k, "v"))
                            pe.wait_ge(*b.act.at(k, "pT", r, 0))
                            pe.wait_ge(*b.dve.at(k, "pT", r, 1))
                            for kt in range(NT):
                                for h2 in range(2):
                                    rhs = b.pT[:, h2, kt * N:(kt + 1) * N]
                                    if hd == 64:
                                        c = (2 * r + h2) * 64
                                        last = mm(O[64 * h2:64 * h2 + 64, 0:N], b.v[:, kt * 1024 + c:kt * 1024 + c + 64],
                                                  rhs, kt == 0, kt == NT - 1)
                                    else:
                                        h = ORDER8[r][h2]
                                        q0 = 32 * (h // 4)
                                        last = mm(O[q0:q0 + 32, 0:N], b.v[:, kt * 512 + h * 32:kt * 512 + h * 32 + 32],
                                                  rhs, kt == 0 and r < 2, kt == NT - 1 and r >= 6)
                            last.then_inc(*b.pe.mark(k, "PV", r))

                if kind == "cross":
                    t1 = t0 + 10
                    for half in range(2):
                        yield t1 + 2 * half
                        if half == 0:
                            for g in range(4 if hd == 64 else 1):
                                pe.wait_ge(*q_maker.at(k, "q", g))
                            pe.wait_ge(*b.dve.at(k, "k"))
                        for ti in range(NT):
                            A = claim("AB"[ti], b.dve, k, "sub", half, ti)
                            if hd == 64:
                                for p in range(4 * half, 4 * half + 4):
                                    last = mm(A[:, (p % 4) * P:(p % 4 + 1) * P], b.qT[:, p, ti * P:(ti + 1) * P],
                                              b.kk[:, p * P:(p + 1) * P])
                            else:
                                last = mm(A[:, :], b.qT[:, 0, ti * P:(ti + 1) * P], b.kk[:, half * 512:(half + 1) * 512])
                            last.then_inc(*b.pe.mark(k, "scores", half, ti))
                    for half in range(2):
                        for i in range(2):
                            yield t1 + 8 + 6 * half + 3 * i
                            T = claim("T", (b.act, b.dve)[i], k, "pT", half, i)
                            for ti in range(NT):
                                pe.wait_ge(*b.dve.at(k, "norm", half, ti))
                            for pp in range(2):
                                for ti in range(NT):
                                    last = tr(T[:, pp * N + ti * P:pp * N + (ti + 1) * P],
                                              b.p[:, half, ti * 512 + (2 * i + pp) * P:ti * 512 + (2 * i + pp + 1) * P])
                            last.then_inc(*b.pe.mark(k, "T", half, i))
                            yield t1 + 8 + 6 * half + 3 * i + 1.5
                            g = 2 * half + i
                            if hd == 64 or g == 0:
                                O = claim("O", b.act, k, "attn", g if hd == 64 else 0)
                            if g == 0:
                                if hd == 64:
                                    pe.wait_ge(*b.act.at(k, "v", 1))
                                    pe.wait_ge(*b.act.at(k, "v", 0))
                                else:
                                    pe.wait_ge(*b.dve.at(k, "v"))
                            pe.wait_ge(*(b.act, b.dve)[i].at(k, "pT", half, i))
                            for pp in range(2):
                                p = 2 * g + pp
                                rhs = b.pT[:, i, pp * N:(pp + 1) * N]
                                if hd == 64:
                                    last = mm(O[:, pp * N:(pp + 1) * N], b.v[:, p * P:(p + 1) * P], rhs)
                                else:
                                    last = mm(O[32 * g:32 * g + 32, 0:N], b.v[:, p * 32:(p + 1) * 32], rhs,
                                              pp == 0, pp == 1)
                            last.then_inc(*b.pe.mark(k, "PV", g))

                if kind == "ff":
                    chunks = (4, 6, 0, 2) if blk["act"] == "glu" else (0, 2)
                    w1 = w(la, blk["w1"])
                    yield t0 + 4
                    pe.wait_ge(*b.act.at(k, "hT"))
                    for i, c0 in enumerate(chunks):
                        if i == 2:
                            A = claim("TO"[i - 2], b.dve, k, "hidden", c0 + 1)
                        elif i == 3:
                            A = claim("TO"[i - 2], b.dve, k, "hidden", c0 + 1)
                        else:
                            A = claim("AB"[i], b.act, k, "gelu", c0 % 4 + 1)
                        for c in (c0, c0 + 1):
                            last = mm(A[:, (c - c0) * N:(c - c0 + 1) * N], w1[:, c * P:(c + 1) * P], b.hT[:, :])
                        last.then_inc(*b.pe.mark(k, "h1", i))

                yield t0 + LENGTH[k] - 3
                O = claim("O", b.dve, k, "x")
                if kind == "ff":
                    nchunk, wo = 4, w(la, blk["w2"])
                    for c in range(4):
                        pe.wait_ge(*(b.dve.at(k, "hidden", c) if blk["act"] == "glu" else b.act.at(k, "gelu", c)))
                else:
                    nchunk, wo = (8 if hd == 64 else 1), w(la, blk["o"])
                    last_attn = 0 if hd == 8 else (7 if kind == "self" else 3)
                    pe.wait_ge(*b.act.at(k, "attn", last_attn))
                for ti in range(NT):
                    for c in range(nchunk):
                        last = mm(O[:, ti * D:(ti + 1) * D], b.qT[:, c, ti * P:(ti + 1) * P], wo[:, c * D:(c + 1) * D],
                                  c == 0, c == nchunk - 1)
                last.then_inc(*b.pe.mark(k, "out"))

        def scalar_program(s, eng):
            b = S[s]

            def act(out, in_, func=ACT.Identity, **kw):
                return nc.scalar.activation(out, in_, func, **kw)

            for k, blk in enumerate(BLOCKS):
                t0, kind, la, m = START[k], blk["kind"], blk["layer"], blk["norm"]
                hd, rope = blk.get("hd"), blk.get("rope")
                yield t0 + 2.1
                eng.wait_ge(*b.pe.at(k, "xnT"))
                if k == 0:
                    eng.wait_ge(*b.dve.at("mod"))
                act(b.hT[:, :], b.bank["T"][:, 0:N], scale=b.mod[:, 2 * m:2 * m + 1],
                    bias=b.mod[:, 2 * m + 1:2 * m + 2]).then_inc(*b.act.mark(k, "hT"))
                if blk.get("normed"):
                    yield t0 + 2.6
                    eng.wait_ge(*b.pe.at(k, "ctxT"))
                    for i in range(2):
                        last = act(b.ctx_nT[0:CD, i * J:(i + 1) * J], b.bank["O"][0:CD, 0:J],
                                   scale=vec((2, "ca_lnc_w"))[0:CD, :], bias=vec((2, "ca_lnc_b"))[0:CD, :])
                    last.then_inc(*b.act.mark(k, "ctx_nT"))
                if blk.get("project"):
                    yield t0 + 2.6
                    eng.wait_ge(*b.pe.at(k, "ctxT"))
                    act(b.ctx_nT[:, :], b.bank["O"][:, 0:2 * J], bias=vec((la, "b_ctx"))).then_inc(*b.act.mark(k, "ctx_nT"))

                def bias(name):
                    return vec((la, blk[name][0]), blk[name][1]) if name in blk else 0.0

                if kind == "cross":
                    yield t0 + 2.9
                    if hd == 64:
                        for half in range(2):
                            eng.wait_ge(*b.pe.at(k, "v", half))
                            bank = b.bank["BA"[half]][:, :].rearrange("p (c h d) -> p c h d", h=2, d=64)
                            out = b.v[:, half * 512:(half + 1) * 512].rearrange("p (c h d) -> p c h d", h=2, d=64)
                            for h2 in range(2):
                                last = act(out[:, :, h2, :], bank[:, :, h2, :], scale=mask64[:, h2:h2 + 1])
                            last.then_inc(*b.act.mark(k, "v", half))
                    else:
                        eng.wait_ge(*b.pe.at(k, "k"))
                        act(b.p[:, 0, 0:J], b.bank["A"][:, 0:J], bias=bias("bk")).then_inc(*b.act.mark(k, "k_plain"))
                if kind == "self" and hd == 8:
                    yield t0 + 4.1
                    eng.wait_ge(*b.pe.at(k, "k", 0))
                    act(b.p[:, 0, 0:N], b.bank["B"][:, 0:N], bias=bias("bk")).then_inc(*b.act.mark(k, "k_plain"))
                if kind in ("self", "cross") and hd == 64 and not rope:
                    for g in range(4):
                        yield t0 + 4.1 + 1.2 * g
                        eng.wait_ge(*b.pe.at(k, "q", g))
                        act(b.qT[:, 2 * g:2 * g + 2, :], b.bank["AT"[g % 2]][:, :].rearrange("p (c n) -> p c n", c=2), ACT.Copy, scale=0.125)\
                            .then_inc(*b.act.mark(k, "q", g))
                if kind == "self" and hd == 64:
                    for ti in range(NT):
                        yield t0 + 9.1 + ti
                        for half in range(2):
                            eng.wait_ge(*b.pe.at(k, "v", ti, half))
                            act(b.v[:, ti * 1024 + half * 512:ti * 1024 + (half + 1) * 512],
                                b.bank[("AT", "BO")[half][ti]][:, :], ACT.Copy).then_inc(*b.act.mark(k, "v", ti, half))

                if kind == "self":
                    t1 = t0 + 12
                    for p in range(8 + 1):
                        if p > 0:
                            r = p - 1
                            yield t1 + STEP[hd] * p + 1.1
                            eng.wait_ge(*b.pe.at(k, "T", r, 0))
                            if r > 0:
                                eng.wait_ge(*b.pe.at(k, "PV", r - 1))
                            act(b.pT[:, 0, :], b.bank["T"][:, :], ACT.Copy).then_inc(*b.act.mark(k, "pT", r, 0))
                        if p < 8:
                            yield t1 + STEP[hd] * p + 2.2
                            if p >= 2:
                                eng.wait_ge(*b.pe.at(k, "T", p - 2, 1))
                            for ti in range(NT):
                                eng.wait_ge(*b.dve.at(k, "max", p, ti))
                                for h2 in range(2):
                                    c = p * 4 + ti * 2 + h2
                                    last = act(b.p[:, p % 2, (ti * 2 + h2) * N:(ti * 2 + h2 + 1) * N],
                                               b.bank["AB"[ti]][:, h2 * N:(h2 + 1) * N], ACT.Exp,
                                               bias=b.nm[:, c:c + 1], accum_out=b.sums[:, c:c + 1])
                                last.then_inc(*b.act.mark(k, "exp", p, ti))
                        if p > 0 and (hd == 64 or p == 8):
                            yield t1 + STEP[hd] * p + 3.6
                            eng.wait_ge(*b.pe.at(k, "PV", r))
                            if hd == 64:
                                act(b.qT[:, r, :], b.bank["O"][:, 0:N], ACT.Copy).then_inc(*b.act.mark(k, "attn", r))
                            else:
                                act(b.qT[:, 0, :], b.bank["O"][:, 0:N], bias=bias("bv")).then_inc(*b.act.mark(k, "attn", 0))

                if kind == "cross":
                    t1 = t0 + 10
                    for half in range(2):
                        yield t1 + 2 * half + 0.6
                        for ti in range(NT):
                            eng.wait_ge(*b.dve.at(k, "sub", half, ti))
                            act(b.p[:, half, ti * 512:(ti + 1) * 512], b.p[:, half, ti * 512:(ti + 1) * 512], ACT.Exp)\
                                .then_inc(*b.act.mark(k, "exp", half, ti))
                    for half in range(2):
                        for i in range(2):
                            g = 2 * half + i
                            if i == 0:
                                yield t1 + 8 + 6 * half + 3 * i + 0.1
                                eng.wait_ge(*b.pe.at(k, "T", half, i))
                                if half:
                                    eng.wait_ge(*b.pe.at(k, "PV", g - 2))
                                act(b.pT[:, i, :], b.bank["T"][:, :], ACT.Copy).then_inc(*b.act.mark(k, "pT", half, i))
                            if hd == 64 or g == 3:
                                yield t1 + 8 + 6 * half + 3 * i + 1.6
                                eng.wait_ge(*b.pe.at(k, "PV", g))
                                if hd == 64:
                                    act(b.qT[:, 2 * g:2 * g + 2, :], b.bank["O"][:, :].rearrange("p (c n) -> p c n", c=2),
                                        ACT.Copy).then_inc(*b.act.mark(k, "attn", g))
                                else:
                                    act(b.qT[:, 0, :], b.bank["O"][:, 0:N], bias=bias("bv"))\
                                        .then_inc(*b.act.mark(k, "attn", 0))

                if kind == "ff":
                    yield t0 + 4.1
                    glu = blk["act"] == "glu"
                    func = ACT.Gelu_apprx_tanh if blk["act"] == "tanh" else ACT.Gelu
                    for c in range(4):
                        eng.wait_ge(*b.pe.at(k, "h1", c // 2))
                        out = b.p[:, 0, c * N:(c + 1) * N] if glu else b.qT[:, c, :]
                        act(out, b.bank["AB"[c // 2]][:, (c % 2) * N:(c % 2 + 1) * N], func,
                            bias=vec((la, blk["b1"]), c + (4 if glu else 0))).then_inc(*b.act.mark(k, "gelu", c))

        def vector_program(s, eng, turn):
            b = S[s]
            v = nc.vector

            def spread(ap, n):
                return ap.unsqueeze(2).broadcast_to([ap.shape[0], ap.shape[1], n])

            yield 0
            v.tensor_copy(b.mod[:, :].unsqueeze(1), mod_all[:, bass.ds(turn * STREAMS + s, 1), :])\
                .then_inc(*b.dve.mark("mod"))
            for k, blk in enumerate(BLOCKS):
                t0, kind, la, m = START[k], blk["kind"], blk["layer"], blk["norm"]
                hd, rope = blk.get("hd"), blk.get("rope")
                yield t0 + 0.1
                if k == 0:
                    eng.wait_ge(b.x_loaded, 16)
                else:
                    eng.wait_ge(*b.dve.at(k - 1, "x"))
                for ti in range(NT):
                    v.bn_stats(b.stats[:, ti, :], b.x[:, ti, :]).then_inc(*b.dve.mark(k, "stats", ti))
                for ti in range(NT):
                    eng.wait_ge(*b.dve.at(k, "stats", ti))
                    v.bn_aggr(b.mv[:, ti, :], b.stats[:, ti, :]).then_inc(*b.dve.mark(k, "mv", ti))
                if blk.get("normed"):
                    v.bn_stats(b.cstats[:, :], b.ctx[:, :]).then_inc(*b.dve.mark(k, "cstats"))
                    eng.wait_ge(*b.dve.at(k, "cstats"))
                    v.bn_aggr(b.cmv[:, :], b.cstats[:, :]).then_inc(*b.dve.mark(k, "cmv"))
                yield t0 + 1
                eng.wait_ge(*b.dve.at(k, "mv", 1))
                eng.wait_ge(*b.pool.at(k, "rstd"))
                for ti in range(NT):
                    v.tensor_scalar(b.xn[:, ti, :], b.x[:, ti, :], b.mv[:, ti, 0:1], b.rstd[:, ti:ti + 1],
                                    ALU.subtract, ALU.mult).then_inc(*b.dve.mark(k, "xn", ti))
                if blk.get("normed"):
                    eng.wait_ge(*b.pool.at(k, "crstd"))
                    v.tensor_scalar(b.ctx_n[:, :], b.ctx[:, :], b.cmv[:, 0:1], b.cve[:, 1:2],
                                    ALU.subtract, ALU.mult).then_inc(*b.dve.mark(k, "ctx_n"))

                if kind == "cross" and hd == 64:
                    yield t0 + 2.85
                    kv = b.kk[:, 0:16 * J].rearrange("p (c h n) -> p c h n", c=8, h=2)
                    src = b.bank["A"][:, :].rearrange("p (c n) -> p c n", c=8)
                    if rope:
                        cos, sin = table["k"]
                        t1_, t2_ = b.p[:, 1, 0:512], b.p[:, 1, 512:1024]
                        eng.wait_ge(*b.pe.at(k, "k"))
                        v.tensor_tensor(t1_.rearrange("p (c n) -> p c n", c=8), src,
                                        cos[:, 0:J].unsqueeze(1).broadcast_to([P, 8, J]), ALU.mult)\
                            .then_inc(*b.dve.mark(k, "k_cos"))
                        eng.wait_ge(*b.pe.at(k, "k_swapped"))
                        v.tensor_tensor(t2_.rearrange("p (c n) -> p c n", c=8),
                                        b.bank["B"][:, :].rearrange("p (c n) -> p c n", c=8),
                                        sin[:, 0:J].unsqueeze(1).broadcast_to([P, 8, J]), ALU.mult)\
                            .then_inc(*b.dve.mark(k, "k_sin"))
                        src = t1_.rearrange("p (c n) -> p c n", c=8)
                        eng.wait_ge(*b.pool.at(k, "k_sum"))
                    else:
                        eng.wait_ge(*b.pe.at(k, "k"))
                    for h2 in range(2):
                        last = v.tensor_scalar(kv[:, :, h2, :], src, (mask_rope if rope else mask64)[:, h2:h2 + 1], None,
                                               ALU.mult)
                    last.then_inc(*b.dve.mark(k, "k"))
                if kind == "cross" and hd == 8:
                    yield t0 + 2.95
                    eng.wait_ge(*b.act.at(k, "k_plain"))
                    v.tensor_tensor(b.kk[:, 0:16 * J].rearrange("p (h n) -> p h n", h=16),
                                    b.p[:, 0, 0:J].unsqueeze(1).broadcast_to([P, 16, J]), spread(mask16, J), ALU.mult)\
                        .then_inc(*b.dve.mark(k, "k"))
                    eng.wait_ge(*b.pe.at(k, "v"))
                    eng.wait_ge(*b.pool.at(k, "v_zero"))
                    bank = b.bank["B"][:, 0:D].rearrange("p (g j d) -> p g j d", g=4, j=4)
                    out = b.v[:, 0:256].rearrange("p (g i c) -> p g i c", g=4, i=2)
                    for j in range(4):
                        last = v.tensor_scalar(out[:, :, j // 2, 8 * j:8 * j + 8], bank[:, :, j, :],
                                               mask64[:, j % 2:j % 2 + 1], None, ALU.mult)
                    last.then_inc(*b.dve.mark(k, "v"))

                if kind in ("self", "cross") and hd == 64 and (rope or kind == "self"):
                    for g in range(4):
                        yield t0 + 4.2 + 1.2 * g
                        if rope:
                            cos, sin = table["q"]
                            if g:
                                eng.wait_ge(*b.pool.at(k, "q", g - 1))
                            for r, (tab, bank, name, src) in enumerate(
                                    ((cos, "A", "q_cos", "q"), (sin, "B", "q_sin", "q_swapped"))):
                                eng.wait_ge(*b.pe.at(k, src, g))
                                v.tensor_tensor(b.p[:, 0, r * 512:(r + 1) * 512].rearrange("p (c n) -> p c n", c=2),
                                                b.bank[bank][:, :].rearrange("p (c n) -> p c n", c=2),
                                                tab.unsqueeze(1).broadcast_to([P, 2, N]), ALU.mult)\
                                    .then_inc(*b.dve.mark(k, name, g))
                        if kind == "cross":
                            continue
                        src = b.bank["BO"[g % 2]][:, :].rearrange("p (c n) -> p c n", c=2)
                        if rope:
                            cos, sin = table["k"]
                            if g:
                                eng.wait_ge(*b.dve.at(k, "k", g - 1))
                            for r, (tab, bank, name, src) in enumerate(
                                    ((cos, "T", "k_cos", "k"), (sin, "O", "k_sin", "k_swapped"))):
                                eng.wait_ge(*b.pe.at(k, src, g))
                                v.tensor_tensor(b.p[:, 1, r * 512:(r + 1) * 512].rearrange("p (c n) -> p c n", c=2),
                                                b.bank[bank][:, :].rearrange("p (c n) -> p c n", c=2),
                                                tab.unsqueeze(1).broadcast_to([P, 2, N]), ALU.mult)\
                                    .then_inc(*b.dve.mark(k, name, g))
                            eng.wait_ge(*b.pool.at(k, "k_sum", g))
                            src = b.p[:, 1, 0:512].rearrange("p (c n) -> p c n", c=2)
                        else:
                            eng.wait_ge(*b.pe.at(k, "k", g))
                        kv = b.kk[:, g * 1024:(g + 1) * 1024].rearrange("p (c h n) -> p c h n", c=2, h=2)
                        for h2 in range(2):
                            last = v.tensor_scalar(kv[:, :, h2, :], src, (mask_rope if rope else mask64)[:, h2:h2 + 1], None,
                                               ALU.mult)
                        last.then_inc(*b.dve.mark(k, "k", g))
                if kind in ("self", "cross") and hd == 8:
                    yield t0 + 4.2
                    eng.wait_ge(*b.pe.at(k, "q", 0))
                    bq = vec((la, blk["bq"][0]), blk["bq"][1]) if "bq" in blk else 0.0
                    v.tensor_scalar(b.qT[:, 0, :], b.bank["A"][:, 0:N], bq, float(np.float32(8.0 ** -0.5)), ALU.add, ALU.mult)\
                        .then_inc(*b.dve.mark(k, "q", 0))
                    if kind == "self":
                        eng.wait_ge(*b.pe.at(k, "v"))
                        eng.wait_ge(*b.pool.at(k, "v_zero"))
                        bank = b.bank["T"][:, 0:N].rearrange("p (t g j d) -> p t g j d", t=2, g=4, j=4)
                        out = b.v[:, 0:1024].rearrange("p (t g j c) -> p t g j c", t=2, g=4, j=4)
                        for j in range(4):
                            last = v.tensor_copy(out[:, :, :, j, 8 * j:8 * j + 8], bank[:, :, :, j, :])
                        last.then_inc(*b.dve.mark(k, "v"))
                        eng.wait_ge(*b.act.at(k, "k_plain"))
                        for p in range(8):
                            for h2 in range(2):
                                h, c = ORDER8[p][h2], (2 * p + h2) * N
                                last = v.tensor_scalar(b.kk[:, c:c + N], b.p[:, 0, 0:N], mask16[:, h:h + 1], None, ALU.mult)
                            last.then_inc(*b.dve.mark(k, "kmask", p))

                if kind == "self":
                    t1 = t0 + 12
                    for p in range(8 + 1):
                        if p < 8:
                            yield t1 + STEP[hd] * p + 0.2
                            if p == 0 and hd == 8:
                                eng.wait_ge(*b.dve.at(k, "kmask", 7))
                            for ti in range(NT):
                                eng.wait_ge(*b.pe.at(k, "scores", p, ti))
                                c = p * 4 + ti * 2
                                v.tensor_reduce(b.nm[:, c:c + 2], b.bank["AB"[ti]][:, :].rearrange("p (h n) -> p h n", h=2),
                                                AXX, ALU.max, negate=True).then_inc(*b.dve.mark(k, "max", p, ti))
                        if p > 0:
                            r = p - 1
                            yield t1 + STEP[hd] * p + 2.1
                            eng.wait_ge(*b.pe.at(k, "T", r, 1))
                            if r > 0:
                                eng.wait_ge(*b.pe.at(k, "PV", r - 1))
                            v.tensor_copy(b.pT[:, 1, :], b.bank["T"][:, :]).then_inc(*b.dve.mark(k, "pT", r, 1))
                        if p < 8:
                            yield t1 + STEP[hd] * p + 3
                            eng.wait_ge(*b.act.at(k, "exp", p, 1))
                            c = p * 4
                            v.reciprocal(b.rs[:, c:c + 4], b.sums[:, c:c + 4]).then_inc(*b.dve.mark(k, "rsum", p))
                            eng.wait_ge(*b.dve.at(k, "rsum", p))
                            for i in range(4):
                                pr = b.p[:, p % 2, i * N:(i + 1) * N]
                                last = v.tensor_scalar(pr, pr, b.rs[:, c + i:c + i + 1], None, ALU.mult)
                            last.then_inc(*b.dve.mark(k, "norm", p))

                if kind == "cross":
                    t1 = t0 + 10
                    for half in range(2):
                        for ti in range(NT):
                            yield t1 + 2 * half + 0.5 + 0.01 * ti
                            eng.wait_ge(*b.pe.at(k, "scores", half, ti))
                            c = (half * 2 + ti) * 8
                            bank = b.bank["AB"[ti]][:, :].rearrange("p (h n) -> p h n", h=8)
                            v.tensor_reduce(b.nm[:, c:c + 8], bank, AXX, ALU.max, negate=True)\
                                .then_inc(*b.dve.mark(k, "max", half, ti))
                            eng.wait_ge(*b.dve.at(k, "max", half, ti))
                            pr = b.p[:, half, ti * 512:(ti + 1) * 512].rearrange("p (h n) -> p h n", h=8)
                            v.tensor_tensor(pr, bank, spread(b.nm[:, c:c + 8], J), ALU.add)\
                                .then_inc(*b.dve.mark(k, "sub", half, ti))
                    for half in range(2):
                        for ti in range(NT):
                            yield t1 + 5 + 2 * half + ti
                            eng.wait_ge(*b.act.at(k, "exp", half, ti))
                            c = (half * 2 + ti) * 8
                            pr = b.p[:, half, ti * 512:(ti + 1) * 512].rearrange("p (h n) -> p h n", h=8)
                            v.tensor_reduce(b.sums[:, c:c + 8], pr, AXX, ALU.add).then_inc(*b.dve.mark(k, "sum", half, ti))
                            eng.wait_ge(*b.dve.at(k, "sum", half, ti))
                            v.reciprocal(b.rs[:, c:c + 8], b.sums[:, c:c + 8]).then_inc(*b.dve.mark(k, "rsum", half, ti))
                            eng.wait_ge(*b.dve.at(k, "rsum", half, ti))
                            v.tensor_tensor(pr, pr, spread(b.rs[:, c:c + 8], J), ALU.mult)\
                                .then_inc(*b.dve.mark(k, "norm", half, ti))
                    for half in range(2):
                        yield t1 + 8 + 6 * half + 3 + 0.1
                        eng.wait_ge(*b.pe.at(k, "T", half, 1))
                        if half:
                            eng.wait_ge(*b.pe.at(k, "PV", 1))
                        v.tensor_copy(b.pT[:, 1, :], b.bank["T"][:, :]).then_inc(*b.dve.mark(k, "pT", half, 1))

                if kind == "ff" and blk["act"] == "glu":
                    yield t0 + 4.2
                    for c in range(4):
                        eng.wait_ge(*b.pe.at(k, "h1", 2 + c // 2))
                        eng.wait_ge(*b.act.at(k, "gelu", c))
                        v.scalar_tensor_tensor(out=b.qT[:, c, :], in0=b.bank["TO"[c // 2]][:, (c % 2) * N:(c % 2 + 1) * N],
                                               scalar=vec((la, blk["b1"]), c), in1=b.p[:, 0, c * N:(c + 1) * N],
                                               op0=ALU.add, op1=ALU.mult).then_inc(*b.dve.mark(k, "hidden", c))

                yield t0 + LENGTH[k] - 2.9
                eng.wait_ge(*b.pe.at(k, "out"))
                eng.wait_ge(*b.pool.at(k, "xb"))
                v.tensor_tensor(b.x[:, :, :], b.bank["O"][:, 0:NT * D].rearrange("p (t d) -> p t d", t=NT), b.xb[:, :, :],
                                ALU.add).then_inc(*b.dve.mark(k, "x"))

        def gpsimd_program(s, eng):
            b = S[s]
            g_ = nc.gpsimd
            for k, blk in enumerate(BLOCKS):
                t0, kind, la = START[k], blk["kind"], blk["layer"]
                hd, rope = blk.get("hd"), blk.get("rope")
                yield t0 + 0.5
                eng.wait_ge(*b.dve.at(k, "mv", 1))
                g_.tensor_scalar(b.ve[:, :], b.mv[:, :, 1], EPS[la], None, ALU.add).then_inc(*b.pool.mark(k, "ve"))
                eng.wait_ge(*b.pool.at(k, "ve"))
                g_.tensor_tensor(b.rstd[:, :], b.ve[:, :], minus_half[:, 0:NT], ALU.pow).then_inc(*b.pool.mark(k, "rstd"))
                if blk.get("normed"):
                    eng.wait_ge(*b.dve.at(k, "cmv"))
                    g_.tensor_scalar(b.cve[:, 0:1], b.cmv[:, 1:2], EPS[la], None, ALU.add).then_inc(*b.pool.mark(k, "cve"))
                    eng.wait_ge(*b.pool.at(k, "cve"))
                    g_.tensor_tensor(b.cve[:, 1:2], b.cve[:, 0:1], minus_half[0:J, 0:1], ALU.pow)\
                        .then_inc(*b.pool.mark(k, "crstd"))
                if hd == 8:
                    g_.memset(b.v[:, 0:1024], 0.0).then_inc(*b.pool.mark(k, "v_zero"))
                if kind == "cross" and rope:
                    yield t0 + 2.86
                    eng.wait_ge(*b.dve.at(k, "k_sin"))
                    t1_, t2_ = b.p[:, 1, 0:512], b.p[:, 1, 512:1024]
                    g_.tensor_tensor(t1_, t1_, t2_, ALU.add).then_inc(*b.pool.mark(k, "k_sum"))
                if rope:
                    for g in range(4):
                        yield t0 + 4.3 + 1.2 * g
                        eng.wait_ge(*b.dve.at(k, "q_sin", g))
                        half = b.p[:, 0, :].rearrange("p (r c n) -> p r c n", r=2, c=2)
                        g_.tensor_tensor(b.qT[:, 2 * g:2 * g + 2, :], half[:, 0], half[:, 1], ALU.add)\
                            .then_inc(*b.pool.mark(k, "q", g))
                        if kind == "self":
                            eng.wait_ge(*b.dve.at(k, "k_sin", g))
                            t1_, t2_ = b.p[:, 1, 0:512], b.p[:, 1, 512:1024]
                            g_.tensor_tensor(t1_, t1_, t2_, ALU.add).then_inc(*b.pool.mark(k, "k_sum", g))
                yield t0 + LENGTH[k] - 6
                g_.tensor_tensor(b.xb[:, :, :], b.x[:, :, :],
                                 out_bias[:, k, :].unsqueeze(1).broadcast_to([P, NT, D]), ALU.add)\
                    .then_inc(*b.pool.mark(k, "xb"))

        lags = [LAG * s for s in range(STREAMS)]
        with nc.Fori(0, NB // STREAMS) as turn:
            with nc.Block() as block:

                @block.sync
                def _(sp):
                    for s, b in enumerate(S):
                        at = bass.ds(turn * STREAMS + s, 1)
                        sp.dma_start(b.x[:, :, :], t["x"][at].rearrange("o (t p) d -> p (o t) d", p=P))\
                            .then_inc(b.x_loaded, 16)
                        sp.dma_start(b.ctx[:, :], t["ctx"][at].rearrange("o j c -> (o j) c")).then_inc(b.ctx_loaded, 16)
                        sp.dma_start(b.ctxT[:, :], t["ctxT"][at].rearrange("o c j -> (o c) j")).then_inc(b.ctx_loaded, 16)
                    for s, b in enumerate(S):
                        at = bass.ds(turn * STREAMS + s, 1)
                        sp.wait_ge(*b.dve.at(len(BLOCKS) - 1, "x"))
                        sp.dma_start(t["out"][at].rearrange("o (t p) d -> p (o t) d", p=P), b.x[:, :, :])\
                            .then_inc(b.stored, 16)
                    for b in S:
                        sp.wait_ge(b.stored, 16)

                @block.tensor
                def _(pe):
                    in_turn([tensor_program(s, pe) for s in range(STREAMS)], lags)

                @block.scalar
                def _(act):
                    in_turn([scalar_program(s, act) for s in range(STREAMS)], lags)

                @block.vector
                def _(dve):
                    for b in S:
                        dve.wait_ge(b.ctx_loaded, 32)
                    in_turn([vector_program(s, dve, turn) for s in range(STREAMS)], lags)

                @block.gpsimd
                def _(pool):
                    in_turn([gpsimd_program(s, pool) for s in range(STREAMS)], lags)

            lo, hi = min(sem_numbers), max(sem_numbers)
            assert hi - lo + 1 == len(sem_numbers)
            nc.vector.sem_clear(range(lo, hi + 1))
            nc.all_engine_barrier()


def packed(inputs):
    def arr(layer, name):
        return np.asarray(inputs[f"L{layer}_xcond_{name}"])

    def rows(a, chunks):
        out = np.zeros((P, chunks * a.shape[1]), a.dtype)
        if chunks == 1:
            out[:a.shape[0]] = a
        else:
            out[:] = a.reshape(chunks, P, a.shape[1]).transpose(1, 0, 2).reshape(P, -1)
        return out

    rotated = np.arange(1024).reshape(8, 2, 32, 2).transpose(0, 3, 1, 2).reshape(-1)
    order = {"sa_wq": rotated, "ca_wq": rotated}
    order["sa_wkv"] = order["ca_wkv"] = np.concatenate([rotated, np.arange(1024, 2048)])
    t = {}
    for la, ws in enumerate(WEIGHTS):
        t[f"weights{la}"] = np.concatenate(
            [rows(arr(la, n)[:, order[n]] if n in order else arr(la, n), c) for n, c, _ in ws], 1)
    t["mod_w"] = np.concatenate([arr(la, n)[:, c * P:(c + 1) * P] for la, n, c in MODS], 1)
    vec = [arr(la, n)[c * P:(c + 1) * P][:, None] for la, n, c in MOD_BIAS]
    one, zero = np.ones((P, 1), np.float32), np.zeros((P, 1), np.float32)
    vec += [one] * 6 + [arr(2, n)[:, None] for n in ("ln1_w", "ln2_w")] + [arr(3, f"ln{i}_w")[:, None] for i in (1, 2, 3)]
    vec += [zero] * 6 + [arr(2, n)[:, None] for n in ("ln1_b", "ln2_b")] + [arr(3, f"ln{i}_b")[:, None] for i in (1, 2, 3)]
    vec.append(np.asarray(inputs["cond_1024"]).T)
    for la, n, c in VECS:
        a = arr(la, n)
        if a.shape[0] < P:
            a = np.concatenate([a, np.zeros(P - a.shape[0], a.dtype)])
        vec.append(a.reshape(c, P).T)
    t["vecs"] = np.concatenate(vec, 1)
    t["out_bias"] = np.concatenate([arr(la, n) for la, n in OUT_BIAS])
    t["x"] = np.asarray(inputs["x"])
    t["ctx"] = np.asarray(inputs["ctx_768"])
    ctxT = t["ctx"].transpose(0, 2, 1)
    t["ctxT"] = np.concatenate([ctxT, ctxT], 2)

    part = np.arange(P)
    half = 64
    inv = (np.float32(1.0) / np.float32(10000.0) ** (np.arange(0, half, 2, dtype=np.float32) / np.float32(half)))
    ang = (np.arange(N, dtype=np.float32)[:, None] * inv[None, :].astype(np.float32)).astype(np.float32)
    cos = np.cos(ang).astype(np.float32)[:, part % 32].T
    sin = np.sin(ang).astype(np.float32)[:, part % 32].T * np.where(part < 64, -1, 1)[:, None].astype(np.float32)
    consts = dict(
        ident=np.eye(P), mask16=(part[:, None] // 8 == np.arange(16)[None, :]),
        mask64=(part[:, None] // 64 == np.arange(2)[None, :]),
        mask_rope=(part[:, None] // 32 % 2 == np.arange(2)[None, :]), cos_q=cos * np.float32(0.125), sin_q=sin * np.float32(0.125), cos_k=cos, sin_k=sin)
    t["consts"] = np.concatenate([np.asarray(consts[n], np.float32) for n in CONSTS], 1)
    return {n: np.ascontiguousarray(a) for n, a in t.items()}


def kernel(**inputs):
    import concourse.bacc as _bacc
    from concourse.bass_utils import run_bass_kernel_spmd as _run

    arrays = packed(inputs)
    counts = {}
    for _ in range(2):
        nc = _bacc.Bacc("TRN2", target_bir_lowering=False, num_devices=1)
        t = {n: nc.dram_tensor(f"in_{n}", a.shape, F32, kind="ExternalInput").ap() for n, a in arrays.items()}
        t["out"] = nc.dram_tensor("out_0", (NB, N, D), F32, kind="ExternalOutput").ap()
        program(nc, t, counts)
    r = _run(nc, [{f"in_{n}": a for n, a in arrays.items()}], core_ids=[0])
    return r.results[0]["out_0"]
```

```python
import concourse.bass as bass
from concourse import mybir
from contextlib import ExitStack
import numpy as np

F32 = mybir.dt.float32
ACT = mybir.ActivationFunctionType
ALU = mybir.AluOpType
AXX = mybir.AxisListType.X

NB, N, D = 8, 256, 128
J, CD = 64, 96
H = 16
P = 128
NT = N // P
STREAMS = 2
NORMS = 11

WEIGHTS = [
    [("q1", 1, 1024), ("k1", 1, 1024), ("v1", 1, 1024), ("o1_w", 8, 128), ("q2", 1, 1024), ("k2", 1, 1024),
     ("v2", 1, 1024), ("o2_w", 8, 128), ("ff_w1", 1, 1024), ("ff_w2", 4, 128)],
    [("W_qkv", 1, 384), ("W_proj", 1, 128), ("W_ctx", 1, 128), ("W_q", 1, 128), ("W_k", 1, 128), ("W_v", 1, 128),
     ("W_out", 1, 128), ("W_fc1", 1, 512), ("W_fc2", 4, 128)],
    [("sa_wq", 1, 1024), ("sa_wkv", 1, 2048), ("sa_wo", 8, 128), ("ca_wq", 1, 1024), ("ca_wkv", 1, 2048),
     ("ca_wo", 8, 128), ("ff_w1", 1, 512), ("ff_w2", 4, 128)],
    [("Wqkv", 1, 384), ("Wos", 1, 128), ("Wq", 1, 128), ("Wk", 1, 128), ("Wv", 1, 128), ("Woc", 1, 128),
     ("W1", 1, 512), ("W2", 4, 128)],
]

MODS = (
    [(0, f"n{m}_w", c) for m in (1, 2, 3) for c in (0, 1)]
    + [(1, "W_ada", c) for c in (1, 0, 3, 2, 5, 4)]
    + [(2, n, 0) for n in ("g1_w", "b1_w", "g2_w", "b2_w")]
    + [(3, "Wmod", c) for c in (1, 0, 3, 2, 5, 4)]
)
MOD_BIAS = (
    [(0, f"n{m}_b", c) for m in (1, 2, 3) for c in (0, 1)]
    + [(1, "b_ada", c) for c in (1, 0, 3, 2, 5, 4)]
    + [(2, n, 0) for n in ("g1_b", "b1_b", "g2_b", "b2_b")]
    + [(3, "bmod", c) for c in (1, 0, 3, 2, 5, 4)]
)
VECS = [(0, "ff_b1", 8), (1, "b_qkv", 3), (1, "b_ctx", 1), (1, "b_fc1", 4), (2, "ca_lnc_w", 1), (2, "ca_lnc_b", 1),
        (2, "ff_b1", 4), (3, "bqkv", 3), (3, "bq", 1), (3, "bk", 1), (3, "bv", 1), (3, "b1", 4)]
OUT_BIAS = [(0, "o1_b"), (0, "o2_b"), (0, "ff_b2"), (1, "b_proj"), (1, "b_out"), (1, "b_fc2"),
            (2, "sa_bo"), (2, "ca_bo"), (2, "ff_b2"), (3, "bos"), (3, "boc"), (3, "b2")]

BLOCKS = [
    dict(kind="self", layer=0, norm=0, hd=64, q=("q1", 0), k=("k1", 0), v=("v1", 0), o="o1_w"),
    dict(kind="cross", layer=0, norm=1, hd=64, q=("q2", 0), k=("k2", 0), v=("v2", 0), o="o2_w"),
    dict(kind="ff", layer=0, norm=2, w1="ff_w1", b1="ff_b1", w2="ff_w2", act="glu"),
    dict(kind="self", layer=1, norm=3, hd=8, q=("W_qkv", 0), k=("W_qkv", 128), v=("W_qkv", 256), o="W_proj",
         bq=("b_qkv", 0), bk=("b_qkv", 1), bv=("b_qkv", 2)),
    dict(kind="cross", layer=1, norm=4, hd=8, q=("W_q", 0), k=("W_k", 0), v=("W_v", 0), o="W_out", project=True),
    dict(kind="ff", layer=1, norm=5, w1="W_fc1", b1="b_fc1", w2="W_fc2", act="tanh"),
    dict(kind="self", layer=2, norm=6, hd=64, q=("sa_wq", 0), k=("sa_wkv", 0), v=("sa_wkv", 1024), o="sa_wo",
         rope=True),
    dict(kind="cross", layer=2, norm=6, hd=64, q=("ca_wq", 0), k=("ca_wkv", 0), v=("ca_wkv", 1024), o="ca_wo",
         rope=True, normed=True),
    dict(kind="ff", layer=2, norm=7, w1="ff_w1", b1="ff_b1", w2="ff_w2", act="erf"),
    dict(kind="self", layer=3, norm=8, hd=8, q=("Wqkv", 0), k=("Wqkv", 128), v=("Wqkv", 256), o="Wos",
         bq=("bqkv", 0), bk=("bqkv", 1), bv=("bqkv", 2)),
    dict(kind="cross", layer=3, norm=9, hd=8, q=("Wq", 0), k=("Wk", 0), v=("Wv", 0), o="Woc",
         bq=("bq", 0), bk=("bk", 0), bv=("bv", 0)),
    dict(kind="ff", layer=3, norm=10, w1="W1", b1="b1", w2="W2", act="erf"),
]
EPS = [1e-5, 1e-6, 1e-5, 1e-5]
ORDER = dict(
    tensor=("1110110011001001010100111000101110001011100010111000101110001011100010110101010011001100110010101110"
        "0011001100101011001011001011001011100010111000101110001011100010111000101110001011010101010011100100"
        "1010101100110010110010101101010110101011101011000111010011100010111000101110001011100010111000101100"
        "1010010001101001010101001101110110110010010001010101011001101111001011100010111000101110001011100010"
        "111000101100010010100100111001010111011010011001000100110100"),
    scalar=("1110110011001000110011100011100011100011100011100011100011001011001100110011001110100011001010110011"
        "0010110011001100110011001100110011001011100011001110001010101100101111100011100111000111000111000111"
        "0001110001100010001110001111110000110101000011001101011011001100110011001100110010010010110011111000"
        "100100101100"),
    vector=("1010111100001110001100101100101100101100101100101100101100101110010011001111010001010010111000101100"
        "1010101100110010110100110010110100110010110100110011010100101100110011110100010110001010101010111001"
        "0110101011011010011001011001011001011001011001011000100110100101010101001111111001100000010110100011"
        "10010101110110011010011001011010011001011010011000001101010011010110111110011100000000110101001010"),
    gpsimd=("110011001100110011001100101110110000101101010110001100110011001100"),
)

ORDER8 = [(4 * (2 * (p % 2)) + p // 2, 4 * (2 * (p % 2) + 1) + p // 2) for p in range(8)]

CONSTS = dict(ident=128, mask16=16, mask64=2, mask_rope=2, cos_q=N, sin_q=N, cos_k=N, sin_k=N)


def columns(sizes):
    at, out = 0, {}
    for name, n in sizes:
        out[name] = (at, at + n)
        at += n
    return out, at


WCOLS = [columns([(n, c * w) for n, c, w in ws]) for ws in WEIGHTS]
CCOLS = columns(CONSTS.items())
VCOLS = columns([("mod_bias", 2 * NORMS), ("ln_w", NORMS), ("ln_b", NORMS), ("cond", NB)]
                + [((la, n), c) for la, n, c in VECS])


class Signal:

    def __init__(self, sem, counts):
        self.sem, self.counts, self.n = sem, counts, 0

    def mark(self, *label):
        self.n += 1
        assert self.counts.setdefault(label, self.n) == self.n, label
        return self.sem, 1

    def at(self, *label):
        return self.sem, self.counts.get(label, 1)


def in_turn(order, programs):
    for g in programs:
        next(g)
    for s in order:
        next(programs[int(s)], None)
    assert [next(g, None) for g in programs] == [None] * len(programs)


def program(nc, t, counts):
    ctx = ExitStack()
    with ctx:
        def sb(name, shape):
            return ctx.enter_context(nc.sbuf_tensor(name, shape, F32))

        consts = sb("consts", [P, CCOLS[1]])
        vecs = sb("vecs", [P, VCOLS[1]])
        out_bias = sb("out_bias", [P, len(BLOCKS), D])
        weights = [sb(f"weights{la}", [P, WCOLS[la][1]]) for la in range(4)]
        mod_all = sb("mod_all", [P, NB, 2 * NORMS])
        silu = sb("silu", [P, 4, NB])
        minus_half = sb("minus_half", [P, 2])

        def const(name):
            a, b = CCOLS[0][name]
            return consts[:, a:b]

        def vec(key, i=0, n=1):
            a = VCOLS[0][key][0] + i
            return vecs[:, a:a + n]

        def w(layer, name, rows=P):
            a, b = WCOLS[layer][0][name]
            return weights[layer][0:rows, a:b]

        ident, mask16, mask64, mask_rope = (const(n) for n in ("ident", "mask16", "mask64", "mask_rope"))
        table = {"q": (const("cos_q"), const("sin_q")), "k": (const("cos_k"), const("sin_k"))}

        class Stream:
            pass

        S = []
        for s in range(STREAMS):
            b = Stream()
            b.x = sb(f"x{s}", [P, NT, D])
            b.y = sb(f"y{s}", [P, NT, D])
            b.xb = sb(f"x_plus_bias{s}", [P, NT, D])
            b.xn = sb(f"x_normed{s}", [P, NT, D])
            b.hT = sb(f"hT{s}", [P, N])
            b.mod = sb(f"mod{s}", [P, 2 * NORMS])
            b.stats = sb(f"stats{s}", [P, NT, 6])
            b.mv = sb(f"mean_var{s}", [P, NT, 2])
            b.ve = sb(f"var_eps{s}", [P, NT])
            b.rstd = sb(f"rstd{s}", [P, NT])
            b.ctx = sb(f"ctx{s}", [J, CD])
            b.ctxT = sb(f"ctxT{s}", [CD, 2 * J])
            b.ctx_nT = sb(f"ctx_nT{s}", [P, 2 * J])
            b.ctx_n = sb(f"ctx_n{s}", [J, CD])
            b.cstats = sb(f"cstats{s}", [J, 6])
            b.cmv = sb(f"cmv{s}", [J, 2])
            b.cve = sb(f"cve{s}", [J, 2])
            b.qT = sb(f"qT{s}", [P, 8, N])
            b.kk = sb(f"keys{s}", [P, 16 * N])
            b.v = sb(f"values{s}", [P, NT * 1024])
            b.p = sb(f"probs{s}", [P, 2, 1024])
            b.pT = sb(f"probsT{s}", [P, 2, 512])
            b.nm = sb(f"negmax{s}", [P, 32])
            b.sums = sb(f"sums{s}", [P, 32])
            b.rs = sb(f"rsums{s}", [P, 32])
            b.bank = {n: ctx.enter_context(nc.psum_tensor(f"psum_{n}{s}", [P, 512], F32)) for n in ("A", "B", "T", "O")}
            S.append(b)

        def sem(name):
            x = ctx.enter_context(nc.semaphore(name))
            return x

        consts_loaded = sem("consts_loaded")
        mods_loaded = sem("mods_loaded")
        weights_loaded = [sem(f"weights_loaded{la}") for la in range(4)]
        pre_act, pre_dve, pre_pe = sem("pre_act"), sem("pre_dve"), sem("pre_pe")

        names = ("x_loaded", "ctx_loaded", "stored", "tensor_done", "scalar_done", "vector_done", "gpsimd_done")
        phase_sems = {(n, s): sem(f"{n}{s}") for s in range(STREAMS) for n in names}

        def begin(phase):
            for s, b in enumerate(S):
                b.x_loaded, b.ctx_loaded, b.stored = (phase_sems[n, s] for n in names[:3])
                b.pe, b.act, b.dve, b.pool = (
                    Signal(phase_sems[n, s], counts.setdefault((phase, n, s), {})) for n in names[3:])

        def end():
            numbers = sorted(x.num for x in phase_sems.values())
            assert numbers[-1] - numbers[0] + 1 == len(numbers)
            nc.vector.sem_clear(range(numbers[0], numbers[-1] + 1))
            nc.all_engine_barrier()

        mod_w = S[0].kk[:, 0:2 * NORMS * D]
        with nc.Block() as block:

            @block.sync
            def _(sp):
                sp.dma_start(vecs[:, :], t["vecs"]).then_inc(mods_loaded, 16)
                sp.dma_start(mod_w, t["mod_w"]).then_inc(mods_loaded, 16)
                sp.dma_start(consts[:, :], t["consts"]).then_inc(consts_loaded, 16)
                sp.dma_start(out_bias[:, :, :].rearrange("p k d -> p (k d)"),
                             t["out_bias"].partition_broadcast(P)).then_inc(consts_loaded, 16)
                for la in range(4):
                    sp.dma_start(weights[la][:, :], t[f"weights{la}"]).then_inc(weights_loaded[la], 16)
                sp.wait_ge(consts_loaded, 32)
                sp.wait_ge(mods_loaded, 32)

            @block.scalar
            def _(act):
                act.wait_ge(mods_loaded, 32)
                nc.scalar.activation(silu[:, 0, :], vec("cond", 0, NB), ACT.Exp, scale=-1.0).then_inc(pre_act, 1)

            @block.tensor
            def _(pe):
                ps = S[0].bank["A"]
                pe.wait_ge(mods_loaded, 32)
                pe.wait_ge(pre_dve, 4)
                for j, (la, _, _) in enumerate(MODS):
                    rhs = silu[:, 3, :] if la in (1, 3) else vec("cond", 0, NB)
                    last = nc.tensor.matmul(ps[:, j * NB:(j + 1) * NB], mod_w[:, j * D:(j + 1) * D], rhs,
                                            start=True, stop=True)
                last.then_inc(pre_pe, 1)

            @block.vector
            def _(dve):
                nc.vector.memset(minus_half[:, :], -0.5).then_inc(pre_dve, 1)
                dve.wait_ge(pre_act, 1)
                nc.vector.tensor_scalar(silu[:, 1, :], silu[:, 0, :], 1.0, None, ALU.add).then_inc(pre_dve, 1)
                dve.wait_ge(pre_dve, 2)
                nc.vector.reciprocal(silu[:, 2, :], silu[:, 1, :]).then_inc(pre_dve, 1)
                dve.wait_ge(pre_dve, 3)
                dve.wait_ge(mods_loaded, 32)
                nc.vector.tensor_tensor(silu[:, 3, :], silu[:, 2, :], vec("cond", 0, NB), ALU.mult).then_inc(pre_dve, 1)
                dve.wait_ge(pre_pe, 1)
                m = mod_all[:, :, :].rearrange("p b j -> p j b")
                nc.vector.tensor_tensor(m, S[0].bank["A"][:, 0:2 * NORMS * NB].rearrange("p (j b) -> p j b", b=NB),
                                        vec("mod_bias", 0, 2 * NORMS).unsqueeze(2).broadcast_to([P, 2 * NORMS, NB]),
                                        ALU.add).then_inc(pre_dve, 1)
                sc = mod_all[:, :, 0:2 * NORMS:2]
                sh = mod_all[:, :, 1:2 * NORMS:2]
                tmp = S[0].p[:, 0, 0:NB * NORMS].rearrange("p (b m) -> p b m", b=NB)
                dve.wait_ge(pre_dve, 5)
                nc.vector.tensor_scalar(tmp, sc, 1.0, None, ALU.add).then_inc(pre_dve, 1)
                dve.wait_ge(pre_dve, 6)
                nc.vector.tensor_tensor(sc, tmp, vec("ln_w", 0, NORMS).unsqueeze(1).broadcast_to([P, NB, NORMS]),
                                        ALU.mult).then_inc(pre_dve, 1)
                tmp2 = S[0].p[:, 1, 0:NB * NORMS].rearrange("p (b m) -> p b m", b=NB)
                nc.vector.tensor_tensor(tmp2, tmp, vec("ln_b", 0, NORMS).unsqueeze(1).broadcast_to([P, NB, NORMS]),
                                        ALU.mult).then_inc(pre_dve, 1)
                dve.wait_ge(pre_dve, 8)
                nc.vector.tensor_tensor(sh, sh, tmp2, ALU.add).then_inc(pre_dve, 1)

        last_k = len(BLOCKS) - 1

        def tensor_program(s, pe):
            b = S[s]
            reader = {}

            def claim(name, sig, *label):
                if name in reader:
                    pe.wait_ge(*reader[name])
                reader[name] = sig.at(*label)
                return b.bank[name]

            def mm(out, lhsT, rhs, start=True, stop=True):
                return nc.tensor.matmul(out, lhsT, rhs, start=start, stop=stop)

            def tr(out, in_, n=P):
                return nc.tensor.transpose(out, in_, ident[0:n, 0:n])

            def mm_swapped(out, lhsT, rhs):
                mm(out[0:64, :], lhsT[:, 64:P], rhs)
                return mm(out[64:P, :], lhsT[:, 0:64], rhs)

            for k, blk in enumerate(BLOCKS):
                kind, la = blk["kind"], blk["layer"]
                yield
                T = claim("T", b.act, k, "hT")
                for ti in range(NT):
                    pe.wait_ge(*b.dve.at(k, "xn", ti))
                    last = tr(T[:, ti * P:(ti + 1) * P], b.xn[:, ti, :])
                last.then_inc(*b.pe.mark(k, "xnT"))
                pe.wait_ge(weights_loaded[la], 16)
                ctxT = b.ctxT
                if kind == "cross":
                    if k == 1:
                        pe.wait_ge(b.ctx_loaded, 32)
                    if blk.get("normed"):
                        yield
                        O = claim("O", b.act, k, "ctx_nT")
                        pe.wait_ge(*b.dve.at(k, "ctx_n"))
                        tr(O[0:CD, 0:J], b.ctx_n[:, :], J).then_inc(*b.pe.mark(k, "ctxT"))
                        ctxT = b.ctx_nT[0:CD, :]
                    if blk.get("project"):
                        yield
                        O = claim("O", b.act, k, "ctx_nT")
                        mm(O[:, 0:2 * J], w(la, "W_ctx", CD), b.ctxT[:, :]).then_inc(*b.pe.mark(k, "ctxT"))
                        ctxT = b.ctx_nT
                rows = P if blk.get("project") else CD

                if kind in ("self", "cross"):
                    wq = w(la, blk["q"][0])[:, blk["q"][1]:]
                    hd, rope = blk["hd"], blk.get("rope")
                    q_maker = b.pool if rope else b.act if hd == 64 else b.dve
                    if kind == "cross":
                        yield
                        wk = w(la, blk["k"][0], rows)[:, blk["k"][1]:]
                        wv = w(la, blk["v"][0], rows)[:, blk["v"][1]:]
                        if k == 7 or k == 4:
                            pe.wait_ge(*b.act.at(k, "ctx_nT"))
                        if hd == 64:
                            A = claim("A", b.dve, k, "k_cos" if rope else "k")
                            for c in range(8):
                                last = mm(A[:, c * J:(c + 1) * J], wk[:, c * P:(c + 1) * P], ctxT[:, 0:J])
                            last.then_inc(*b.pe.mark(k, "k"))
                            if rope:
                                B = claim("B", b.dve, k, "k_sin")
                                for c in range(8):
                                    last = mm_swapped(B[:, c * J:(c + 1) * J], wk[:, c * P:(c + 1) * P], ctxT[:, 0:J])
                                last.then_inc(*b.pe.mark(k, "k_swapped"))
                            for half in range(2):
                                B = claim("BA"[half], b.act, k, "v", half)
                                mm(B[:, :], ctxT[:, :], wv[:, half * 512:(half + 1) * 512])\
                                    .then_inc(*b.pe.mark(k, "v", half))
                        else:
                            A = claim("A", b.act, k, "k_plain")
                            mm(A[:, 0:J], wk[:, 0:P], ctxT[:, 0:J]).then_inc(*b.pe.mark(k, "k"))
                            B = claim("B", b.dve, k, "v")
                            mm(B[:, 0:D], ctxT[:, :], wv[:, 0:P]).then_inc(*b.pe.mark(k, "v"))
                    yield
                    pe.wait_ge(*b.act.at(k, "hT"))
                    if hd == 64:
                        for g in range(4):
                            if g:
                                yield
                            names = ("A", "B") if rope else ("AT"[g % 2],)
                            for r, name in enumerate(names):
                                A = claim(name, *((b.dve, k, ("q_cos", "q_sin")[r], g) if rope else (b.act, k, "q", g)))
                                for i in range(2):
                                    c = 2 * g + i
                                    lhsT = wq[:, c * P:(c + 1) * P]
                                    last = (mm_swapped if r else mm)(A[:, i * N:(i + 1) * N], lhsT, b.hT[:, :])
                                last.then_inc(*b.pe.mark(k, ("q", "q_swapped")[r], g))
                            if kind == "self":
                                wk = w(la, blk["k"][0])[:, blk["k"][1]:]
                                names = ("T", "O") if rope else ("BO"[g % 2],)
                                for r, name in enumerate(names):
                                    A = claim(name, b.dve, k, *((("k_cos", "k_sin")[r], g) if rope else ("k", g)))
                                    for i in range(2):
                                        c = 2 * g + i
                                        lhsT = wk[:, c * P:(c + 1) * P]
                                        last = (mm_swapped if r else mm)(A[:, i * N:(i + 1) * N], lhsT, b.hT[:, :])
                                    last.then_inc(*b.pe.mark(k, ("k", "k_swapped")[r], g))
                    else:
                        A = claim("A", b.dve, k, "q", 0)
                        mm(A[:, 0:N], wq[:, 0:P], b.hT[:, :]).then_inc(*b.pe.mark(k, "q", 0))
                        if kind == "self":
                            wk = w(la, blk["k"][0])[:, blk["k"][1]:]
                            A = claim("B", b.act, k, "k_plain")
                            mm(A[:, 0:N], wk[:, 0:P], b.hT[:, :]).then_inc(*b.pe.mark(k, "k", 0))
                    if kind == "self":
                        wv = w(la, blk["v"][0])[:, blk["v"][1]:]
                        if hd == 64:
                            for ti in range(NT):
                                yield
                                for half in range(2):
                                    A = claim(("AT", "BO")[half][ti], b.act, k, "v", ti, half)
                                    mm(A[:, :], b.hT[:, ti * P:(ti + 1) * P], wv[:, half * 512:(half + 1) * 512])\
                                        .then_inc(*b.pe.mark(k, "v", ti, half))
                        else:
                            A = claim("T", b.dve, k, "v")
                            for ti in range(NT):
                                last = mm(A[:, ti * P:(ti + 1) * P], b.hT[:, ti * P:(ti + 1) * P], wv[:, 0:P])
                            last.then_inc(*b.pe.mark(k, "v"))

                if kind == "self":
                    for p in range(8 + 1):
                        if p < 8:
                            yield
                            if p == 0:
                                for g in range(4 if hd == 64 else 1):
                                    pe.wait_ge(*q_maker.at(k, "q", g))
                                    if hd == 64:
                                        pe.wait_ge(*b.dve.at(k, "k", g))
                            if hd == 8:
                                pe.wait_ge(*b.dve.at(k, "kmask", p))
                            for ti in range(NT):
                                A = claim("AB"[ti], b.act, k, "exp", p, ti)
                                qc = b.qT[:, p if hd == 64 else 0, ti * P:(ti + 1) * P]
                                mm(A[:, :], qc, b.kk[:, p * 512:(p + 1) * 512]).then_inc(*b.pe.mark(k, "scores", p, ti))
                        if p > 0:
                            r = p - 1
                            if hd == 8 and p == 8:
                                yield
                                T = claim("T", b.act, k, "R")
                                pe.wait_ge(*b.dve.at(k, "spread"))
                                for ti in range(NT):
                                    last = tr(T[:, ti * P:(ti + 1) * P], b.xn[:, ti, :])
                                last.then_inc(*b.pe.mark(k, "R"))
                            for h2 in range(2):
                                yield
                                T = claim("T", (b.act, b.dve)[h2], k, "pT", r, h2)
                                if hd == 64:
                                    pe.wait_ge(*b.dve.at(k, "norm", r))
                                else:
                                    pe.wait_ge(*b.act.at(k, "exp", r, 1))
                                for kt in range(NT):
                                    for ti in range(NT):
                                        last = tr(T[:, kt * N + ti * P:kt * N + (ti + 1) * P],
                                                  b.p[:, r % 2, (ti * 2 + h2) * N + kt * P:(ti * 2 + h2) * N + (kt + 1) * P])
                                last.then_inc(*b.pe.mark(k, "T", r, h2))
                            yield
                            if hd == 64 or r == 0:
                                O = claim("O", *((b.act, k, "attn", r) if hd == 64 else (b.dve, k, "attn_n")))
                            if r == 0:
                                for ti in range(NT):
                                    for half in range(2):
                                        if hd == 64:
                                            pe.wait_ge(*b.act.at(k, "v", ti, half))
                                if hd == 8:
                                    pe.wait_ge(*b.dve.at(k, "v"))
                            pe.wait_ge(*b.act.at(k, "pT", r, 0))
                            pe.wait_ge(*b.dve.at(k, "pT", r, 1))
                            for kt in range(NT):
                                for h2 in range(2):
                                    rhs = b.pT[:, h2, kt * N:(kt + 1) * N]
                                    if hd == 64:
                                        c = (2 * r + h2) * 64
                                        last = mm(O[64 * h2:64 * h2 + 64, 0:N], b.v[:, kt * 1024 + c:kt * 1024 + c + 64],
                                                  rhs, kt == 0, kt == NT - 1)
                                    else:
                                        h = ORDER8[r][h2]
                                        q0 = 32 * (h // 4)
                                        last = mm(O[q0:q0 + 32, 0:N], b.v[:, kt * 512 + h * 32:kt * 512 + h * 32 + 32],
                                                  rhs, kt == 0 and r < 2, kt == NT - 1 and r >= 6)
                            last.then_inc(*b.pe.mark(k, "PV", r))

                if kind == "cross":
                    for half in range(2):
                        yield
                        if half == 0:
                            for g in range(4 if hd == 64 else 1):
                                pe.wait_ge(*q_maker.at(k, "q", g))
                            pe.wait_ge(*b.dve.at(k, "k"))
                        for ti in range(NT):
                            A = claim("AB"[ti], *((b.dve, k, "sub", half, ti) if ti == 0 else (b.act, k, "exp", half, ti)))
                            if hd == 64:
                                for p in range(4 * half, 4 * half + 4):
                                    last = mm(A[:, (p % 4) * P:(p % 4 + 1) * P], b.qT[:, p, ti * P:(ti + 1) * P],
                                              b.kk[:, p * P:(p + 1) * P])
                            else:
                                last = mm(A[:, :], b.qT[:, 0, ti * P:(ti + 1) * P], b.kk[:, half * 512:(half + 1) * 512])
                            last.then_inc(*b.pe.mark(k, "scores", half, ti))
                    for half in range(2):
                        for i in range(2):
                            yield
                            T = claim("T", (b.act, b.dve)[i], k, "pT", half, i)
                            for ti in range(NT):
                                if hd == 64:
                                    pe.wait_ge(*b.dve.at(k, "norm", half, ti))
                                else:
                                    pe.wait_ge(*b.act.at(k, "exp", half, ti))
                            for pp in range(2):
                                for ti in range(NT):
                                    last = tr(T[:, pp * N + ti * P:pp * N + (ti + 1) * P],
                                              b.p[:, half, ti * 512 + (2 * i + pp) * P:ti * 512 + (2 * i + pp + 1) * P])
                            last.then_inc(*b.pe.mark(k, "T", half, i))
                            yield
                            g = 2 * half + i
                            if hd == 64 or g == 0:
                                O = claim("O", *((b.act, k, "attn", g) if hd == 64 else (b.dve, k, "attn_n")))
                            if g == 0:
                                if hd == 64:
                                    pe.wait_ge(*b.act.at(k, "v", 1))
                                    pe.wait_ge(*b.act.at(k, "v", 0))
                                else:
                                    pe.wait_ge(*b.dve.at(k, "v"))
                            pe.wait_ge(*(b.act, b.dve)[i].at(k, "pT", half, i))
                            for pp in range(2):
                                p = 2 * g + pp
                                rhs = b.pT[:, i, pp * N:(pp + 1) * N]
                                if hd == 64:
                                    last = mm(O[:, pp * N:(pp + 1) * N], b.v[:, p * P:(p + 1) * P], rhs)
                                else:
                                    last = mm(O[32 * g:32 * g + 32, 0:N], b.v[:, p * 32:(p + 1) * 32], rhs,
                                              pp == 0, pp == 1)
                            last.then_inc(*b.pe.mark(k, "PV", g))
                            if hd == 8 and g == 1:
                                yield
                                T = claim("T", b.act, k, "R")
                                pe.wait_ge(*b.dve.at(k, "spread"))
                                for ti in range(NT):
                                    last = tr(T[:, ti * P:(ti + 1) * P], b.xn[:, ti, :])
                                last.then_inc(*b.pe.mark(k, "R"))

                if kind == "ff":
                    chunks = (4, 6, 0, 2) if blk["act"] == "glu" else (0, 2)
                    w1 = w(la, blk["w1"])
                    yield
                    pe.wait_ge(*b.act.at(k, "hT"))
                    for i, c0 in enumerate(chunks):
                        if i == 2:
                            A = claim("TO"[i - 2], b.dve, k, "hidden", c0 + 1)
                        elif i == 3:
                            A = claim("TO"[i - 2], b.dve, k, "hidden", c0 + 1)
                        else:
                            A = claim("AB"[i], b.act, k, "gelu", c0 % 4 + 1)
                        for c in (c0, c0 + 1):
                            last = mm(A[:, (c - c0) * N:(c - c0 + 1) * N], w1[:, c * P:(c + 1) * P], b.hT[:, :])
                        last.then_inc(*b.pe.mark(k, "h1", i))

                yield
                O = claim("O", b.dve, k, "x")
                if kind == "ff":
                    nchunk, wo = 4, w(la, blk["w2"])
                    for c in range(4):
                        pe.wait_ge(*(b.dve.at(k, "hidden", c) if blk["act"] == "glu" else b.act.at(k, "gelu", c)))
                else:
                    nchunk, wo = (8 if hd == 64 else 1), w(la, blk["o"])
                    last_attn = 0 if hd == 8 else (7 if kind == "self" else 3)
                    pe.wait_ge(*b.act.at(k, "attn", last_attn))
                for ti in range(NT):
                    for c in range(nchunk):
                        last = mm(O[:, ti * D:(ti + 1) * D], b.qT[:, c, ti * P:(ti + 1) * P], wo[:, c * D:(c + 1) * D],
                                  c == 0, c == nchunk - 1)
                last.then_inc(*b.pe.mark(k, "out"))

        def scalar_program(s, eng):
            b = S[s]

            def act(out, in_, func=ACT.Identity, **kw):
                return nc.scalar.activation(out, in_, func, **kw)

            for k, blk in enumerate(BLOCKS):
                kind, la, m = blk["kind"], blk["layer"], blk["norm"]
                hd, rope = blk.get("hd"), blk.get("rope")
                yield
                eng.wait_ge(*b.pe.at(k, "xnT"))
                if k == 0:
                    eng.wait_ge(*b.dve.at("mod"))
                act(b.hT[:, :], b.bank["T"][:, 0:N], scale=b.mod[:, 2 * m:2 * m + 1],
                    bias=b.mod[:, 2 * m + 1:2 * m + 2]).then_inc(*b.act.mark(k, "hT"))
                if blk.get("normed"):
                    yield
                    eng.wait_ge(*b.pe.at(k, "ctxT"))
                    for i in range(2):
                        last = act(b.ctx_nT[0:CD, i * J:(i + 1) * J], b.bank["O"][0:CD, 0:J],
                                   scale=vec((2, "ca_lnc_w"))[0:CD, :], bias=vec((2, "ca_lnc_b"))[0:CD, :])
                    last.then_inc(*b.act.mark(k, "ctx_nT"))
                if blk.get("project"):
                    yield
                    eng.wait_ge(*b.pe.at(k, "ctxT"))
                    act(b.ctx_nT[:, :], b.bank["O"][:, 0:2 * J], bias=vec((la, "b_ctx"))).then_inc(*b.act.mark(k, "ctx_nT"))

                def bias(name):
                    return vec((la, blk[name][0]), blk[name][1]) if name in blk else 0.0

                if kind == "cross":
                    yield
                    if hd == 64:
                        for half in range(2):
                            eng.wait_ge(*b.pe.at(k, "v", half))
                            bank = b.bank["BA"[half]][:, :].rearrange("p (c h d) -> p c h d", h=2, d=64)
                            out = b.v[:, half * 512:(half + 1) * 512].rearrange("p (c h d) -> p c h d", h=2, d=64)
                            for h2 in range(2):
                                last = act(out[:, :, h2, :], bank[:, :, h2, :], scale=mask64[:, h2:h2 + 1])
                            last.then_inc(*b.act.mark(k, "v", half))
                    else:
                        eng.wait_ge(*b.pe.at(k, "k"))
                        act(b.p[:, 0, 0:J], b.bank["A"][:, 0:J], bias=bias("bk")).then_inc(*b.act.mark(k, "k_plain"))
                if kind == "self" and hd == 8:
                    yield
                    eng.wait_ge(*b.pe.at(k, "k", 0))
                    act(b.p[:, 0, 0:N], b.bank["B"][:, 0:N], bias=bias("bk")).then_inc(*b.act.mark(k, "k_plain"))
                if kind in ("self", "cross") and hd == 64 and not rope:
                    for g in range(4):
                        yield
                        eng.wait_ge(*b.pe.at(k, "q", g))
                        act(b.qT[:, 2 * g:2 * g + 2, :], b.bank["AT"[g % 2]][:, :].rearrange("p (c n) -> p c n", c=2), ACT.Copy, scale=0.125)\
                            .then_inc(*b.act.mark(k, "q", g))
                if kind == "self" and hd == 64:
                    for ti in range(NT):
                        yield
                        for half in range(2):
                            eng.wait_ge(*b.pe.at(k, "v", ti, half))
                            act(b.v[:, ti * 1024 + half * 512:ti * 1024 + (half + 1) * 512],
                                b.bank[("AT", "BO")[half][ti]][:, :], ACT.Copy).then_inc(*b.act.mark(k, "v", ti, half))

                if kind == "self":
                    for p in range(8 + 1):
                        if p > 0:
                            r = p - 1
                            if p == 8 and hd == 8:
                                yield
                                eng.wait_ge(*b.pe.at(k, "R"))
                                act(b.hT[:, :], b.bank["T"][:, 0:N], ACT.Copy).then_inc(*b.act.mark(k, "R"))
                            yield
                            eng.wait_ge(*b.pe.at(k, "T", r, 0))
                            if r > 0:
                                eng.wait_ge(*b.pe.at(k, "PV", r - 1))
                            act(b.pT[:, 0, :], b.bank["T"][:, :], ACT.Copy).then_inc(*b.act.mark(k, "pT", r, 0))
                        if p < 8:
                            yield
                            if p >= 2:
                                eng.wait_ge(*b.pe.at(k, "T", p - 2, 1))
                            for ti in range(NT):
                                eng.wait_ge(*b.dve.at(k, "max", p, ti))
                                for h2 in range(2):
                                    c = p * 4 + ti * 2 + h2
                                    last = act(b.p[:, p % 2, (ti * 2 + h2) * N:(ti * 2 + h2 + 1) * N],
                                               b.bank["AB"[ti]][:, h2 * N:(h2 + 1) * N], ACT.Exp,
                                               bias=b.nm[:, c:c + 1], accum_out=b.sums[:, c:c + 1])
                                last.then_inc(*b.act.mark(k, "exp", p, ti))
                        if p > 0 and (hd == 64 or p == 8):
                            yield
                            if hd == 64:
                                eng.wait_ge(*b.pe.at(k, "PV", r))
                                act(b.qT[:, r, :], b.bank["O"][:, 0:N], ACT.Copy).then_inc(*b.act.mark(k, "attn", r))
                            else:
                                eng.wait_ge(*b.dve.at(k, "attn_n"))
                                act(b.qT[:, 0, :], b.qT[:, 1, :], bias=bias("bv")).then_inc(*b.act.mark(k, "attn", 0))

                if kind == "cross":
                    for half in range(2):
                        yield
                        eng.wait_ge(*b.dve.at(k, "sub", half, 0))
                        act(b.p[:, half, 0:512], b.p[:, half, 0:512], ACT.Exp).then_inc(*b.act.mark(k, "exp", half, 0))
                        yield
                        eng.wait_ge(*b.dve.at(k, "max", half, 1))
                        for h in range(8):
                            c = half * 16 + 8 + h
                            last = act(b.p[:, half, 512 + h * J:512 + (h + 1) * J], b.bank["B"][:, h * J:(h + 1) * J],
                                       ACT.Exp, bias=b.nm[:, c:c + 1], accum_out=b.sums[:, c:c + 1])
                        last.then_inc(*b.act.mark(k, "exp", half, 1))
                    for half in range(2):
                        for i in range(2):
                            g = 2 * half + i
                            if i == 0:
                                yield
                                eng.wait_ge(*b.pe.at(k, "T", half, i))
                                if half:
                                    eng.wait_ge(*b.pe.at(k, "PV", g - 2))
                                act(b.pT[:, i, :], b.bank["T"][:, :], ACT.Copy).then_inc(*b.act.mark(k, "pT", half, i))
                            if hd == 8 and g == 1:
                                yield
                                eng.wait_ge(*b.pe.at(k, "R"))
                                act(b.hT[:, :], b.bank["T"][:, 0:N], ACT.Copy).then_inc(*b.act.mark(k, "R"))
                            if hd == 64 or g == 3:
                                yield
                                if hd == 64:
                                    eng.wait_ge(*b.pe.at(k, "PV", g))
                                    act(b.qT[:, 2 * g:2 * g + 2, :], b.bank["O"][:, :].rearrange("p (c n) -> p c n", c=2),
                                        ACT.Copy).then_inc(*b.act.mark(k, "attn", g))
                                else:
                                    eng.wait_ge(*b.dve.at(k, "attn_n"))
                                    act(b.qT[:, 0, :], b.qT[:, 1, :], bias=bias("bv"))\
                                        .then_inc(*b.act.mark(k, "attn", 0))

                if kind == "ff":
                    yield
                    glu = blk["act"] == "glu"
                    func = ACT.Gelu_apprx_tanh if blk["act"] == "tanh" else ACT.Gelu
                    for c in range(4):
                        eng.wait_ge(*b.pe.at(k, "h1", c // 2))
                        out = b.p[:, 0, c * N:(c + 1) * N] if glu else b.qT[:, c, :]
                        act(out, b.bank["AB"[c // 2]][:, (c % 2) * N:(c % 2 + 1) * N], func,
                            bias=vec((la, blk["b1"]), c + (4 if glu else 0))).then_inc(*b.act.mark(k, "gelu", c))

        def vector_program(s, eng, turn):
            b = S[s]
            v = nc.vector

            def spread(ap, n):
                return ap.unsqueeze(2).broadcast_to([ap.shape[0], ap.shape[1], n])

            for k, blk in enumerate(BLOCKS):
                kind, la, m = blk["kind"], blk["layer"], blk["norm"]
                hd, rope = blk.get("hd"), blk.get("rope")
                yield
                if k == 0:
                    v.tensor_copy(b.mod[:, :].unsqueeze(1), mod_all[:, bass.ds(turn * STREAMS + s, 1), :])\
                        .then_inc(*b.dve.mark("mod"))
                    eng.wait_ge(b.x_loaded, 16)
                else:
                    eng.wait_ge(*b.dve.at(k - 1, "x"))
                if k == 7:
                    eng.wait_ge(b.ctx_loaded, 32)
                for ti in range(NT):
                    v.bn_stats(b.stats[:, ti, :], b.x[:, ti, :]).then_inc(*b.dve.mark(k, "stats", ti))
                for ti in range(NT):
                    eng.wait_ge(*b.dve.at(k, "stats", ti))
                    v.bn_aggr(b.mv[:, ti, :], b.stats[:, ti, :]).then_inc(*b.dve.mark(k, "mv", ti))
                if blk.get("normed"):
                    v.bn_stats(b.cstats[:, :], b.ctx[:, :]).then_inc(*b.dve.mark(k, "cstats"))
                    eng.wait_ge(*b.dve.at(k, "cstats"))
                    v.bn_aggr(b.cmv[:, :], b.cstats[:, :]).then_inc(*b.dve.mark(k, "cmv"))
                yield
                eng.wait_ge(*b.dve.at(k, "mv", 1))
                eng.wait_ge(*b.pool.at(k, "rstd"))
                for ti in range(NT):
                    v.tensor_scalar(b.xn[:, ti, :], b.x[:, ti, :], b.mv[:, ti, 0:1], b.rstd[:, ti:ti + 1],
                                    ALU.subtract, ALU.mult).then_inc(*b.dve.mark(k, "xn", ti))
                if blk.get("normed"):
                    eng.wait_ge(*b.pool.at(k, "crstd"))
                    v.tensor_scalar(b.ctx_n[:, :], b.ctx[:, :], b.cmv[:, 0:1], b.cve[:, 1:2],
                                    ALU.subtract, ALU.mult).then_inc(*b.dve.mark(k, "ctx_n"))

                if kind == "cross" and hd == 64:
                    yield
                    kv = b.kk[:, 0:16 * J].rearrange("p (c h n) -> p c h n", c=8, h=2)
                    src = b.bank["A"][:, :].rearrange("p (c n) -> p c n", c=8)
                    if rope:
                        cos, sin = table["k"]
                        t1_, t2_ = b.p[:, 1, 0:512], b.p[:, 1, 512:1024]
                        eng.wait_ge(*b.pe.at(k, "k"))
                        v.tensor_tensor(t1_.rearrange("p (c n) -> p c n", c=8), src,
                                        cos[:, 0:J].unsqueeze(1).broadcast_to([P, 8, J]), ALU.mult)\
                            .then_inc(*b.dve.mark(k, "k_cos"))
                        eng.wait_ge(*b.pe.at(k, "k_swapped"))
                        v.tensor_tensor(t2_.rearrange("p (c n) -> p c n", c=8),
                                        b.bank["B"][:, :].rearrange("p (c n) -> p c n", c=8),
                                        sin[:, 0:J].unsqueeze(1).broadcast_to([P, 8, J]), ALU.mult)\
                            .then_inc(*b.dve.mark(k, "k_sin"))
                        src = t1_.rearrange("p (c n) -> p c n", c=8)
                        eng.wait_ge(*b.pool.at(k, "k_sum"))
                    else:
                        eng.wait_ge(*b.pe.at(k, "k"))
                    for h2 in range(2):
                        last = v.tensor_scalar(kv[:, :, h2, :], src, (mask_rope if rope else mask64)[:, h2:h2 + 1], None,
                                               ALU.mult)
                    last.then_inc(*b.dve.mark(k, "k"))
                if kind == "cross" and hd == 8:
                    yield
                    eng.wait_ge(*b.act.at(k, "k_plain"))
                    v.tensor_tensor(b.kk[:, 0:16 * J].rearrange("p (h n) -> p h n", h=16),
                                    b.p[:, 0, 0:J].unsqueeze(1).broadcast_to([P, 16, J]), spread(mask16, J), ALU.mult)\
                        .then_inc(*b.dve.mark(k, "k"))
                    eng.wait_ge(*b.pe.at(k, "v"))
                    eng.wait_ge(*b.pool.at(k, "v_zero"))
                    bank = b.bank["B"][:, 0:D].rearrange("p (g j d) -> p g j d", g=4, j=4)
                    out = b.v[:, 0:256].rearrange("p (g i c) -> p g i c", g=4, i=2)
                    for j in range(4):
                        last = v.tensor_scalar(out[:, :, j // 2, 8 * j:8 * j + 8], bank[:, :, j, :],
                                               mask64[:, j % 2:j % 2 + 1], None, ALU.mult)
                    last.then_inc(*b.dve.mark(k, "v"))

                if kind in ("self", "cross") and hd == 64 and (rope or kind == "self"):
                    for g in range(4):
                        yield
                        if rope:
                            cos, sin = table["q"]
                            if g:
                                eng.wait_ge(*b.pool.at(k, "q", g - 1))
                            for r, (tab, bank, name, src) in enumerate(
                                    ((cos, "A", "q_cos", "q"), (sin, "B", "q_sin", "q_swapped"))):
                                eng.wait_ge(*b.pe.at(k, src, g))
                                v.tensor_tensor(b.p[:, 0, r * 512:(r + 1) * 512].rearrange("p (c n) -> p c n", c=2),
                                                b.bank[bank][:, :].rearrange("p (c n) -> p c n", c=2),
                                                tab.unsqueeze(1).broadcast_to([P, 2, N]), ALU.mult)\
                                    .then_inc(*b.dve.mark(k, name, g))
                        if kind == "cross":
                            continue
                        src = b.bank["BO"[g % 2]][:, :].rearrange("p (c n) -> p c n", c=2)
                        if rope:
                            cos, sin = table["k"]
                            if g:
                                eng.wait_ge(*b.dve.at(k, "k", g - 1))
                            for r, (tab, bank, name, src) in enumerate(
                                    ((cos, "T", "k_cos", "k"), (sin, "O", "k_sin", "k_swapped"))):
                                eng.wait_ge(*b.pe.at(k, src, g))
                                v.tensor_tensor(b.p[:, 1, r * 512:(r + 1) * 512].rearrange("p (c n) -> p c n", c=2),
                                                b.bank[bank][:, :].rearrange("p (c n) -> p c n", c=2),
                                                tab.unsqueeze(1).broadcast_to([P, 2, N]), ALU.mult)\
                                    .then_inc(*b.dve.mark(k, name, g))
                            eng.wait_ge(*b.pool.at(k, "k_sum", g))
                            src = b.p[:, 1, 0:512].rearrange("p (c n) -> p c n", c=2)
                        else:
                            eng.wait_ge(*b.pe.at(k, "k", g))
                        kv = b.kk[:, g * 1024:(g + 1) * 1024].rearrange("p (c h n) -> p c h n", c=2, h=2)
                        for h2 in range(2):
                            last = v.tensor_scalar(kv[:, :, h2, :], src, (mask_rope if rope else mask64)[:, h2:h2 + 1], None,
                                               ALU.mult)
                        last.then_inc(*b.dve.mark(k, "k", g))
                if kind in ("self", "cross") and hd == 8:
                    yield
                    eng.wait_ge(*b.pe.at(k, "q", 0))
                    bq = vec((la, blk["bq"][0]), blk["bq"][1]) if "bq" in blk else 0.0
                    v.tensor_scalar(b.qT[:, 0, :], b.bank["A"][:, 0:N], bq, float(np.float32(8.0 ** -0.5)), ALU.add, ALU.mult)\
                        .then_inc(*b.dve.mark(k, "q", 0))
                    if kind == "self":
                        eng.wait_ge(*b.pe.at(k, "v"))
                        eng.wait_ge(*b.pool.at(k, "v_zero"))
                        bank = b.bank["T"][:, 0:N].rearrange("p (t g j d) -> p t g j d", t=2, g=4, j=4)
                        out = b.v[:, 0:1024].rearrange("p (t g j c) -> p t g j c", t=2, g=4, j=4)
                        for j in range(4):
                            last = v.tensor_copy(out[:, :, :, j, 8 * j:8 * j + 8], bank[:, :, :, j, :])
                        last.then_inc(*b.dve.mark(k, "v"))
                        eng.wait_ge(*b.act.at(k, "k_plain"))
                        for p in range(8):
                            for h2 in range(2):
                                h, c = ORDER8[p][h2], (2 * p + h2) * N
                                last = v.tensor_scalar(b.kk[:, c:c + N], b.p[:, 0, 0:N], mask16[:, h:h + 1], None, ALU.mult)
                            last.then_inc(*b.dve.mark(k, "kmask", p))

                if kind == "self":
                    for p in range(8 + 1):
                        if p < 8:
                            yield
                            if p == 0 and hd == 8:
                                eng.wait_ge(*b.dve.at(k, "kmask", 7))
                            for ti in range(NT):
                                eng.wait_ge(*b.pe.at(k, "scores", p, ti))
                                c = p * 4 + ti * 2
                                v.tensor_reduce(b.nm[:, c:c + 2], b.bank["AB"[ti]][:, :].rearrange("p (h n) -> p h n", h=2),
                                                AXX, ALU.max, negate=True).then_inc(*b.dve.mark(k, "max", p, ti))
                        if p > 0:
                            r = p - 1
                            yield
                            eng.wait_ge(*b.pe.at(k, "T", r, 1))
                            if r > 0:
                                eng.wait_ge(*b.pe.at(k, "PV", r - 1))
                            v.tensor_copy(b.pT[:, 1, :], b.bank["T"][:, :]).then_inc(*b.dve.mark(k, "pT", r, 1))
                        if p < 8:
                            yield
                            eng.wait_ge(*b.act.at(k, "exp", p, 1))
                            c = p * 4
                            v.reciprocal(b.rs[:, c:c + 4], b.sums[:, c:c + 4]).then_inc(*b.dve.mark(k, "rsum", p))
                            if hd == 8:
                                if p == 7:
                                    eng.wait_ge(*b.dve.at(k, "rsum", 7))
                                    rs = b.rs[:, :].rearrange("p (j i t h) -> p j i t h", j=4, i=2, t=NT)
                                    out = b.xn[:, :, :].rearrange("p t (i h j d) -> p t i h j d", i=2, h=2, j=4)
                                    for ti in range(NT):
                                        for i in range(2):
                                            for h2 in range(2):
                                                last = v.tensor_copy(out[:, ti, i, h2], spread(rs[:, :, i, ti, h2], 8))
                                    last.then_inc(*b.dve.mark(k, "spread"))
                                continue
                            eng.wait_ge(*b.dve.at(k, "rsum", p))
                            for i in range(4):
                                pr = b.p[:, p % 2, i * N:(i + 1) * N]
                                last = v.tensor_scalar(pr, pr, b.rs[:, c + i:c + i + 1], None, ALU.mult)
                            last.then_inc(*b.dve.mark(k, "norm", p))

                    if hd == 8:
                        yield
                        eng.wait_ge(*b.pe.at(k, "PV", 7))
                        eng.wait_ge(*b.act.at(k, "R"))
                        v.tensor_tensor(b.qT[:, 1, :], b.bank["O"][:, 0:N], b.hT[:, :], ALU.mult)\
                            .then_inc(*b.dve.mark(k, "attn_n"))

                if kind == "cross":
                    for half in range(2):
                        for ti in range(NT):
                            yield
                            eng.wait_ge(*b.pe.at(k, "scores", half, ti))
                            c = (half * 2 + ti) * 8
                            bank = b.bank["AB"[ti]][:, :].rearrange("p (h n) -> p h n", h=8)
                            v.tensor_reduce(b.nm[:, c:c + 8], bank, AXX, ALU.max, negate=True)\
                                .then_inc(*b.dve.mark(k, "max", half, ti))
                            if ti:
                                continue
                            eng.wait_ge(*b.dve.at(k, "max", half, ti))
                            pr = b.p[:, half, ti * 512:(ti + 1) * 512].rearrange("p (h n) -> p h n", h=8)
                            v.tensor_tensor(pr, bank, spread(b.nm[:, c:c + 8], J), ALU.add)\
                                .then_inc(*b.dve.mark(k, "sub", half, ti))
                    for half in range(2):
                        for ti in range(NT):
                            yield
                            eng.wait_ge(*b.act.at(k, "exp", half, ti))
                            c = (half * 2 + ti) * 8
                            pr = b.p[:, half, ti * 512:(ti + 1) * 512].rearrange("p (h n) -> p h n", h=8)
                            if ti == 0:
                                v.tensor_reduce(b.sums[:, c:c + 8], pr, AXX, ALU.add)\
                                    .then_inc(*b.dve.mark(k, "sum", half, ti))
                                eng.wait_ge(*b.dve.at(k, "sum", half, ti))
                            v.reciprocal(b.rs[:, c:c + 8], b.sums[:, c:c + 8]).then_inc(*b.dve.mark(k, "rsum", half, ti))
                            if hd == 8:
                                continue
                            eng.wait_ge(*b.dve.at(k, "rsum", half, ti))
                            v.tensor_tensor(pr, pr, spread(b.rs[:, c:c + 8], J), ALU.mult)\
                                .then_inc(*b.dve.mark(k, "norm", half, ti))
                    for half in range(2):
                        if hd == 8 and half == 0:
                            yield
                            eng.wait_ge(*b.dve.at(k, "rsum", 1, 1))
                            for ti in range(NT):
                                rs = b.rs[:, :].rearrange("p (f t h) -> p f t h", f=2, t=NT)[:, :, ti, :]
                                out = b.xn[:, ti, :].rearrange("p (f h d) -> p f h d", f=2, h=8)
                                last = v.tensor_copy(out, rs.unsqueeze(3).broadcast_to([P, 2, 8, 8]))
                            last.then_inc(*b.dve.mark(k, "spread"))
                        yield
                        eng.wait_ge(*b.pe.at(k, "T", half, 1))
                        if half:
                            eng.wait_ge(*b.pe.at(k, "PV", 1))
                        v.tensor_copy(b.pT[:, 1, :], b.bank["T"][:, :]).then_inc(*b.dve.mark(k, "pT", half, 1))
                    if hd == 8:
                        yield
                        eng.wait_ge(*b.pe.at(k, "PV", 3))
                        eng.wait_ge(*b.act.at(k, "R"))
                        v.tensor_tensor(b.qT[:, 1, :], b.bank["O"][:, 0:N], b.hT[:, :], ALU.mult)\
                            .then_inc(*b.dve.mark(k, "attn_n"))

                if kind == "ff" and blk["act"] == "glu":
                    yield
                    for c in range(4):
                        eng.wait_ge(*b.pe.at(k, "h1", 2 + c // 2))
                        eng.wait_ge(*b.act.at(k, "gelu", c))
                        v.scalar_tensor_tensor(out=b.qT[:, c, :], in0=b.bank["TO"[c // 2]][:, (c % 2) * N:(c % 2 + 1) * N],
                                               scalar=vec((la, blk["b1"]), c), in1=b.p[:, 0, c * N:(c + 1) * N],
                                               op0=ALU.add, op1=ALU.mult).then_inc(*b.dve.mark(k, "hidden", c))

                yield
                eng.wait_ge(*b.pe.at(k, "out"))
                eng.wait_ge(*b.pool.at(k, "xb"))
                v.tensor_tensor((b.y if k == last_k else b.x)[:, :, :], b.bank["O"][:, 0:NT * D].rearrange("p (t d) -> p t d", t=NT), b.xb[:, :, :],
                                ALU.add).then_inc(*b.dve.mark(k, "x"))

        def gpsimd_program(s, eng):
            b = S[s]
            g_ = nc.gpsimd
            for k, blk in enumerate(BLOCKS):
                kind, la = blk["kind"], blk["layer"]
                hd, rope = blk.get("hd"), blk.get("rope")
                yield
                eng.wait_ge(*b.dve.at(k, "mv", 1))
                g_.tensor_scalar(b.ve[:, :], b.mv[:, :, 1], EPS[la], None, ALU.add).then_inc(*b.pool.mark(k, "ve"))
                eng.wait_ge(*b.pool.at(k, "ve"))
                g_.tensor_tensor(b.rstd[:, :], b.ve[:, :], minus_half[:, 0:NT], ALU.pow).then_inc(*b.pool.mark(k, "rstd"))
                if blk.get("normed"):
                    eng.wait_ge(*b.dve.at(k, "cmv"))
                    g_.tensor_scalar(b.cve[:, 0:1], b.cmv[:, 1:2], EPS[la], None, ALU.add).then_inc(*b.pool.mark(k, "cve"))
                    eng.wait_ge(*b.pool.at(k, "cve"))
                    g_.tensor_tensor(b.cve[:, 1:2], b.cve[:, 0:1], minus_half[0:J, 0:1], ALU.pow)\
                        .then_inc(*b.pool.mark(k, "crstd"))
                if hd == 8:
                    g_.memset(b.v[:, 0:1024], 0.0).then_inc(*b.pool.mark(k, "v_zero"))
                if kind == "cross" and rope:
                    yield
                    eng.wait_ge(*b.dve.at(k, "k_sin"))
                    t1_, t2_ = b.p[:, 1, 0:512], b.p[:, 1, 512:1024]
                    g_.tensor_tensor(t1_, t1_, t2_, ALU.add).then_inc(*b.pool.mark(k, "k_sum"))
                if rope:
                    for g in range(4):
                        yield
                        eng.wait_ge(*b.dve.at(k, "q_sin", g))
                        half = b.p[:, 0, :].rearrange("p (r c n) -> p r c n", r=2, c=2)
                        g_.tensor_tensor(b.qT[:, 2 * g:2 * g + 2, :], half[:, 0], half[:, 1], ALU.add)\
                            .then_inc(*b.pool.mark(k, "q", g))
                        if kind == "self":
                            eng.wait_ge(*b.dve.at(k, "k_sin", g))
                            t1_, t2_ = b.p[:, 1, 0:512], b.p[:, 1, 512:1024]
                            g_.tensor_tensor(t1_, t1_, t2_, ALU.add).then_inc(*b.pool.mark(k, "k_sum", g))
                yield
                g_.tensor_tensor(b.xb[:, :, :], b.x[:, :, :],
                                 out_bias[:, k, :].unsqueeze(1).broadcast_to([P, NT, D]), ALU.add)\
                    .then_inc(*b.pool.mark(k, "xb"))

        def load(sp, b, batch):
            at = bass.ds(batch, 1)
            sp.dma_start(b.x[:, :, :], t["x"][at].rearrange("o (t p) d -> p (o t) d", p=P)).then_inc(b.x_loaded, 16)
            sp.dma_start(b.ctx[:, :], t["ctx"][at].rearrange("o j c -> (o j) c")).then_inc(b.ctx_loaded, 16)
            sp.dma_start(b.ctxT[:, :], t["ctxT"][at].rearrange("o c j -> (o c) j")).then_inc(b.ctx_loaded, 16)

        def store(sp, b, batch):
            at = bass.ds(batch, 1)
            sp.wait_ge(*b.dve.at(last_k, "x"))
            sp.dma_start(t["out"][at].rearrange("o (t p) d -> p (o t) d", p=P), b.y[:, :, :]).then_inc(b.stored, 16)

        with nc.Fori(0, NB // STREAMS) as turn:
            begin("loop")
            with nc.Block() as block:

                @block.sync
                def _(sp):
                    for s, b in enumerate(S):
                        load(sp, b, turn * STREAMS + s)
                    for s, b in enumerate(S):
                        store(sp, b, turn * STREAMS + s)
                    for b in S:
                        sp.wait_ge(b.ctx_loaded, 32)
                        sp.wait_ge(b.stored, 16)

                @block.tensor
                def _(pe):
                    in_turn(ORDER["tensor"], [tensor_program(s, pe) for s in range(STREAMS)])

                @block.scalar
                def _(act):
                    in_turn(ORDER["scalar"], [scalar_program(s, act) for s in range(STREAMS)])

                @block.vector
                def _(dve):
                    in_turn(ORDER["vector"], [vector_program(s, dve, turn) for s in range(STREAMS)])

                @block.gpsimd
                def _(pool):
                    in_turn(ORDER["gpsimd"], [gpsimd_program(s, pool) for s in range(STREAMS)])
            end()


def packed(inputs):
    def arr(layer, name):
        return np.asarray(inputs[f"L{layer}_xcond_{name}"])

    def rows(a, chunks):
        out = np.zeros((P, chunks * a.shape[1]), a.dtype)
        if chunks == 1:
            out[:a.shape[0]] = a
        else:
            out[:] = a.reshape(chunks, P, a.shape[1]).transpose(1, 0, 2).reshape(P, -1)
        return out

    rotated = np.arange(1024).reshape(8, 2, 32, 2).transpose(0, 3, 1, 2).reshape(-1)
    order = {"sa_wq": rotated, "ca_wq": rotated}
    order["sa_wkv"] = order["ca_wkv"] = np.concatenate([rotated, np.arange(1024, 2048)])
    t = {}
    for la, ws in enumerate(WEIGHTS):
        t[f"weights{la}"] = np.concatenate(
            [rows(arr(la, n)[:, order[n]] if n in order else arr(la, n), c) for n, c, _ in ws], 1)
    t["mod_w"] = np.concatenate([arr(la, n)[:, c * P:(c + 1) * P] for la, n, c in MODS], 1)
    vec = [arr(la, n)[c * P:(c + 1) * P][:, None] for la, n, c in MOD_BIAS]
    one, zero = np.ones((P, 1), np.float32), np.zeros((P, 1), np.float32)
    vec += [one] * 6 + [arr(2, n)[:, None] for n in ("ln1_w", "ln2_w")] + [arr(3, f"ln{i}_w")[:, None] for i in (1, 2, 3)]
    vec += [zero] * 6 + [arr(2, n)[:, None] for n in ("ln1_b", "ln2_b")] + [arr(3, f"ln{i}_b")[:, None] for i in (1, 2, 3)]
    vec.append(np.asarray(inputs["cond_1024"]).T)
    for la, n, c in VECS:
        a = arr(la, n)
        if a.shape[0] < P:
            a = np.concatenate([a, np.zeros(P - a.shape[0], a.dtype)])
        vec.append(a.reshape(c, P).T)
    t["vecs"] = np.concatenate(vec, 1)
    t["out_bias"] = np.concatenate([arr(la, n) for la, n in OUT_BIAS])
    t["x"] = np.asarray(inputs["x"])
    t["ctx"] = np.asarray(inputs["ctx_768"])
    ctxT = t["ctx"].transpose(0, 2, 1)
    t["ctxT"] = np.concatenate([ctxT, ctxT], 2)

    part = np.arange(P)
    half = 64
    inv = (np.float32(1.0) / np.float32(10000.0) ** (np.arange(0, half, 2, dtype=np.float32) / np.float32(half)))
    ang = (np.arange(N, dtype=np.float32)[:, None] * inv[None, :].astype(np.float32)).astype(np.float32)
    cos = np.cos(ang).astype(np.float32)[:, part % 32].T
    sin = np.sin(ang).astype(np.float32)[:, part % 32].T * np.where(part < 64, -1, 1)[:, None].astype(np.float32)
    consts = dict(
        ident=np.eye(P), mask16=(part[:, None] // 8 == np.arange(16)[None, :]),
        mask64=(part[:, None] // 64 == np.arange(2)[None, :]),
        mask_rope=(part[:, None] // 32 % 2 == np.arange(2)[None, :]), cos_q=cos * np.float32(0.125), sin_q=sin * np.float32(0.125), cos_k=cos, sin_k=sin)
    t["consts"] = np.concatenate([np.asarray(consts[n], np.float32) for n in CONSTS], 1)
    return {n: np.ascontiguousarray(a) for n, a in t.items()}


def kernel(**inputs):
    import concourse.bacc as _bacc
    from concourse.bass_utils import run_bass_kernel_spmd as _run

    arrays = packed(inputs)
    counts = {}
    for _ in range(2):
        nc = _bacc.Bacc("TRN2", target_bir_lowering=False, num_devices=1)
        t = {n: nc.dram_tensor(f"in_{n}", a.shape, F32, kind="ExternalInput").ap() for n, a in arrays.items()}
        t["out"] = nc.dram_tensor("out_0", (NB, N, D), F32, kind="ExternalOutput").ap()
        program(nc, t, counts)
    r = _run(nc, [{f"in_{n}": a for n, a in arrays.items()}], core_ids=[0])
    return r.results[0]["out_0"]
```

```python
import concourse.bass as bass
from concourse import mybir
from contextlib import ExitStack
import numpy as np

F32 = mybir.dt.float32
ACT = mybir.ActivationFunctionType
ALU = mybir.AluOpType
AXX = mybir.AxisListType.X

NB, N, D = 8, 256, 128
J, CD = 64, 96
H = 16
P = 128
NT = N // P
STREAMS = 2
NORMS = 11

WEIGHTS = [
    [("q1", 1, 1024), ("k1", 1, 1024), ("v1", 1, 1024), ("o1_w", 8, 128), ("q2", 1, 1024), ("k2", 1, 1024),
     ("v2", 1, 1024), ("o2_w", 8, 128), ("ff_w1", 1, 1024), ("ff_w2", 4, 128)],
    [("W_qkv", 1, 384), ("W_proj", 1, 128), ("W_ctx", 1, 128), ("W_q", 1, 128), ("W_k", 1, 128), ("W_v", 1, 128),
     ("W_out", 1, 128), ("W_fc1", 1, 512), ("W_fc2", 4, 128)],
    [("sa_wq", 1, 1024), ("sa_wkv", 1, 2048), ("sa_wo", 8, 128), ("ca_wq", 1, 1024), ("ca_wkv", 1, 2048),
     ("ca_wo", 8, 128), ("ff_w1", 1, 512), ("ff_w2", 4, 128)],
    [("Wqkv", 1, 384), ("Wos", 1, 128), ("Wq", 1, 128), ("Wk", 1, 128), ("Wv", 1, 128), ("Woc", 1, 128),
     ("W1", 1, 512), ("W2", 4, 128)],
]

MODS = (
    [(0, f"n{m}_w", c) for m in (1, 2, 3) for c in (0, 1)]
    + [(1, "W_ada", c) for c in (1, 0, 3, 2, 5, 4)]
    + [(2, n, 0) for n in ("g1_w", "b1_w", "g2_w", "b2_w")]
    + [(3, "Wmod", c) for c in (1, 0, 3, 2, 5, 4)]
)
MOD_BIAS = (
    [(0, f"n{m}_b", c) for m in (1, 2, 3) for c in (0, 1)]
    + [(1, "b_ada", c) for c in (1, 0, 3, 2, 5, 4)]
    + [(2, n, 0) for n in ("g1_b", "b1_b", "g2_b", "b2_b")]
    + [(3, "bmod", c) for c in (1, 0, 3, 2, 5, 4)]
)
VECS = [(0, "ff_b1", 8), (1, "b_qkv", 3), (1, "b_ctx", 1), (1, "b_fc1", 4), (2, "ca_lnc_w", 1), (2, "ca_lnc_b", 1),
        (2, "ff_b1", 4), (3, "bqkv", 3), (3, "bq", 1), (3, "bk", 1), (3, "bv", 1), (3, "b1", 4)]
OUT_BIAS = [(0, "o1_b"), (0, "o2_b"), (0, "ff_b2"), (1, "b_proj"), (1, "b_out"), (1, "b_fc2"),
            (2, "sa_bo"), (2, "ca_bo"), (2, "ff_b2"), (3, "bos"), (3, "boc"), (3, "b2")]

BLOCKS = [
    dict(kind="self", layer=0, norm=0, hd=64, q=("q1", 0), k=("k1", 0), v=("v1", 0), o="o1_w"),
    dict(kind="cross", layer=0, norm=1, hd=64, q=("q2", 0), k=("k2", 0), v=("v2", 0), o="o2_w"),
    dict(kind="ff", layer=0, norm=2, w1="ff_w1", b1="ff_b1", w2="ff_w2", act="glu"),
    dict(kind="self", layer=1, norm=3, hd=8, q=("W_qkv", 0), k=("W_qkv", 128), v=("W_qkv", 256), o="W_proj",
         bq=("b_qkv", 0), bk=("b_qkv", 1), bv=("b_qkv", 2)),
    dict(kind="cross", layer=1, norm=4, hd=8, q=("W_q", 0), k=("W_k", 0), v=("W_v", 0), o="W_out", project=True),
    dict(kind="ff", layer=1, norm=5, w1="W_fc1", b1="b_fc1", w2="W_fc2", act="tanh"),
    dict(kind="self", layer=2, norm=6, hd=64, q=("sa_wq", 0), k=("sa_wkv", 0), v=("sa_wkv", 1024), o="sa_wo",
         rope=True, norm_ctx=True),
    dict(kind="cross", layer=2, norm=6, hd=64, q=("ca_wq", 0), k=("ca_wkv", 0), v=("ca_wkv", 1024), o="ca_wo",
         rope=True, normed=True),
    dict(kind="ff", layer=2, norm=7, w1="ff_w1", b1="ff_b1", w2="ff_w2", act="erf"),
    dict(kind="self", layer=3, norm=8, hd=8, q=("Wqkv", 0), k=("Wqkv", 128), v=("Wqkv", 256), o="Wos",
         bq=("bqkv", 0), bk=("bqkv", 1), bv=("bqkv", 2)),
    dict(kind="cross", layer=3, norm=9, hd=8, q=("Wq", 0), k=("Wk", 0), v=("Wv", 0), o="Woc",
         bq=("bq", 0), bk=("bk", 0), bv=("bv", 0)),
    dict(kind="ff", layer=3, norm=10, w1="W1", b1="b1", w2="W2", act="erf"),
]
EPS = [1e-5, 1e-6, 1e-5, 1e-5]

ORDER = dict(
    tensor=("0000000000001000111111111000011111000010110010011001100011001000011011010001110100011110110001100110"
        "1110010001111010100110111001011011110001000100001100111111011011000001111010001100000010111000100100"
        "0100110100111100110001110011011100110111000011011001100111011000110111101101001100110010000100110001"
        "1111110110001011101000000010001111000000001111001111001111100011101100100011101100011100110001011001"
        "1001100110111100100101110001101110000101100011000010111001101101011011001101001011001010000001101001"
        "1111101011000111011000010111000011000011100100010111000011001110001100111000110011100011011100110011"
        "1101100110110110010101100010000100110001111111110001011011"),
    scalar=("0000000010110011100011111000011001010110000100011101010011010001110110011101111001100100011100101110"
        "0110001010111110100001111100000010100010010111000111001110110100111000110101011010110111000001101010"
        "1111000001111101000000101110011000110110001101100010110100111001110010101100101011011010001011110000"
        "0110001011011110100001111100100100011000111000111000110010111000110010110101110101101100000110101011"
        "110000011111"),
    vector=("0011000001001110100001101010011001100001100011001100110011001101100111011101011000011111110000000110"
        "0110111110000011111000010000011110000100111000100000111101000011000110011110011000111100110111001101"
        "1100110011010110110110000110100111101100110000011000111101011100001101111100000001111100100100000000"
        "1111000000011111011111001110110100110011001100110110001010110011010111001100110011001011101000010001"
        "1110010110110011001101001000110001111011100001011111000001111000100010100110001110000110011011000011"
        "1001110000110111001100011100011100110111101101001000100111110110010000011000111001111100001101111100"
        "11"),
    gpsimd=("0011001100110001110001110011010000010010011111110001101010011100110001110001110011"),
)

ORDER8 = [(4 * (2 * (p % 2)) + p // 2, 4 * (2 * (p % 2) + 1) + p // 2) for p in range(8)]

CONSTS = dict(ident=128, mask16=16, mask64=2, mask_rope=2, cos_q=N, sin_q=N, cos_k=N, sin_k=N)


def columns(sizes):
    at, out = 0, {}
    for name, n in sizes:
        out[name] = (at, at + n)
        at += n
    return out, at


WCOLS = [columns([(n, c * w) for n, c, w in ws]) for ws in WEIGHTS]
CCOLS = columns(CONSTS.items())
VCOLS = columns([("mod_bias", 2 * NORMS), ("ln_w", NORMS), ("ln_b", NORMS), ("cond", NB)]
                + [((la, n), c) for la, n, c in VECS])


class Signal:

    def __init__(self, sem, counts):
        self.sem, self.counts, self.n = sem, counts, 0

    def mark(self, *label):
        self.n += 1
        assert self.counts.setdefault(label, self.n) == self.n, label
        return self.sem, 1

    def at(self, *label):
        return self.sem, self.counts.get(label, 1)


def in_turn(order, programs):
    for g in programs:
        next(g)
    for s in order:
        next(programs[int(s)], None)
    assert all(next(g, "done") == "done" for g in programs), "order leaves steps out"


def program(nc, t, counts):
    ctx = ExitStack()
    with ctx:
        def sb(name, shape):
            return ctx.enter_context(nc.sbuf_tensor(name, shape, F32))

        consts = sb("consts", [P, CCOLS[1]])
        vecs = sb("vecs", [P, VCOLS[1]])
        out_bias = sb("out_bias", [P, len(BLOCKS), D])
        weights = [sb(f"weights{la}", [P, WCOLS[la][1]]) for la in range(4)]
        mod_all = sb("mod_all", [P, NB, 2 * NORMS])
        silu = sb("silu", [P, 4, NB])
        minus_half = sb("minus_half", [P, 2])

        def const(name):
            a, b = CCOLS[0][name]
            return consts[:, a:b]

        def vec(key, i=0, n=1):
            a = VCOLS[0][key][0] + i
            return vecs[:, a:a + n]

        def w(layer, name, rows=P):
            a, b = WCOLS[layer][0][name]
            return weights[layer][0:rows, a:b]

        ident, mask16, mask64, mask_rope = (const(n) for n in ("ident", "mask16", "mask64", "mask_rope"))
        table = {"q": (const("cos_q"), const("sin_q")), "k": (const("cos_k"), const("sin_k"))}

        class Stream:
            pass

        S = []
        for s in range(STREAMS):
            b = Stream()
            b.x = sb(f"x{s}", [P, NT, D])
            b.y = sb(f"y{s}", [P, NT, D])
            b.xb = sb(f"x_plus_bias{s}", [P, NT, D])
            b.xn = sb(f"x_normed{s}", [P, NT, D])
            b.hT = sb(f"hT{s}", [P, N])
            b.mod = sb(f"mod{s}", [P, 2 * NORMS])
            b.stats = sb(f"stats{s}", [P, NT, 6])
            b.mv = sb(f"mean_var{s}", [P, NT, 2])
            b.ve = sb(f"var_eps{s}", [P, NT])
            b.rstd = sb(f"rstd{s}", [P, NT])
            b.ctx = sb(f"ctx{s}", [J, CD])
            b.ctxT = sb(f"ctxT{s}", [CD, 2 * J])
            b.ctx_nT = sb(f"ctx_nT{s}", [P, 2 * J])
            b.ctx_n = sb(f"ctx_n{s}", [J, CD])
            b.cstats = sb(f"cstats{s}", [J, 6])
            b.cmv = sb(f"cmv{s}", [J, 2])
            b.cve = sb(f"cve{s}", [J, 2])
            b.qT = sb(f"qT{s}", [P, 8, N])
            b.kk = sb(f"keys{s}", [P, 16 * N])
            b.v = sb(f"values{s}", [P, NT * 1024])
            b.p = sb(f"probs{s}", [P, 2, 1024])
            b.pT = sb(f"probsT{s}", [P, 2, 512])
            b.nm = sb(f"negmax{s}", [P, 32])
            b.sums = sb(f"sums{s}", [P, 32])
            b.rs = sb(f"rsums{s}", [P, 32])
            b.bank = {n: ctx.enter_context(nc.psum_tensor(f"psum_{n}{s}", [P, 512], F32)) for n in ("A", "B", "T", "O")}
            S.append(b)

        def sem(name):
            x = ctx.enter_context(nc.semaphore(name))
            return x

        consts_loaded = sem("consts_loaded")
        first_loaded = sem("first_loaded")
        mods_loaded = sem("mods_loaded")
        weights_loaded = [sem(f"weights_loaded{la}") for la in range(4)]
        pre_act, pre_dve, pre_pe = sem("pre_act"), sem("pre_dve"), sem("pre_pe")

        names = ("x_loaded", "ctx_loaded", "stored", "tensor_done", "scalar_done", "vector_done", "gpsimd_done")
        phase_sems = {(n, s): sem(f"{n}{s}") for s in range(STREAMS) for n in names}

        def begin(phase):
            for s, b in enumerate(S):
                b.x_loaded, b.ctx_loaded, b.stored = (phase_sems[n, s] for n in names[:3])
                b.pe, b.act, b.dve, b.pool = (
                    Signal(phase_sems[n, s], counts.setdefault((phase, n, s), {})) for n in names[3:])

        def end():
            numbers = sorted(x.num for x in phase_sems.values())
            assert numbers[-1] - numbers[0] + 1 == len(numbers)
            nc.vector.sem_clear(range(numbers[0], numbers[-1] + 1))
            nc.all_engine_barrier()

        def load(sp, b, batch, x_loaded, ctx_loaded):
            at = bass.ds(batch, 1)
            sp.dma_start(b.x[:, :, :], t["x"][at].rearrange("o (t p) d -> p (o t) d", p=P)).then_inc(x_loaded, 16)
            sp.dma_start(b.ctx[:, :], t["ctx"][at].rearrange("o j c -> (o j) c")).then_inc(ctx_loaded, 16)
            sp.dma_start(b.ctxT[:, :], t["ctxT"][at].rearrange("o c j -> (o c) j")).then_inc(ctx_loaded, 16)

        mod_w = S[0].kk[:, 0:2 * NORMS * D]
        with nc.Block() as block:

            @block.sync
            def _(sp):
                sp.dma_start(vecs[:, :], t["vecs"]).then_inc(mods_loaded, 16)
                sp.dma_start(mod_w, t["mod_w"]).then_inc(mods_loaded, 16)
                sp.dma_start(consts[:, :], t["consts"]).then_inc(consts_loaded, 16)
                sp.dma_start(out_bias[:, :, :].rearrange("p k d -> p (k d)"),
                             t["out_bias"].partition_broadcast(P)).then_inc(consts_loaded, 16)
                for s, b in enumerate(S):
                    load(sp, b, s, first_loaded, first_loaded)
                for la in range(4):
                    sp.dma_start(weights[la][:, :], t[f"weights{la}"]).then_inc(weights_loaded[la], 16)
                sp.wait_ge(consts_loaded, 32)
                sp.wait_ge(mods_loaded, 32)
                sp.wait_ge(first_loaded, 3 * 16 * STREAMS)

            @block.scalar
            def _(act):
                act.wait_ge(mods_loaded, 32)
                nc.scalar.activation(silu[:, 0, :], vec("cond", 0, NB), ACT.Exp, scale=-1.0).then_inc(pre_act, 1)

            @block.tensor
            def _(pe):
                ps = S[0].bank["A"]
                pe.wait_ge(mods_loaded, 32)
                pe.wait_ge(pre_dve, 4)
                for j, (la, _, _) in enumerate(MODS):
                    rhs = silu[:, 3, :] if la in (1, 3) else vec("cond", 0, NB)
                    last = nc.tensor.matmul(ps[:, j * NB:(j + 1) * NB], mod_w[:, j * D:(j + 1) * D], rhs,
                                            start=True, stop=True)
                last.then_inc(pre_pe, 1)

            @block.vector
            def _(dve):
                nc.vector.memset(minus_half[:, :], -0.5).then_inc(pre_dve, 1)
                dve.wait_ge(pre_act, 1)
                nc.vector.tensor_scalar(silu[:, 1, :], silu[:, 0, :], 1.0, None, ALU.add).then_inc(pre_dve, 1)
                dve.wait_ge(pre_dve, 2)
                nc.vector.reciprocal(silu[:, 2, :], silu[:, 1, :]).then_inc(pre_dve, 1)
                dve.wait_ge(pre_dve, 3)
                dve.wait_ge(mods_loaded, 32)
                nc.vector.tensor_tensor(silu[:, 3, :], silu[:, 2, :], vec("cond", 0, NB), ALU.mult).then_inc(pre_dve, 1)
                dve.wait_ge(pre_pe, 1)
                m = mod_all[:, :, :].rearrange("p b j -> p j b")
                nc.vector.tensor_tensor(m, S[0].bank["A"][:, 0:2 * NORMS * NB].rearrange("p (j b) -> p j b", b=NB),
                                        vec("mod_bias", 0, 2 * NORMS).unsqueeze(2).broadcast_to([P, 2 * NORMS, NB]),
                                        ALU.add).then_inc(pre_dve, 1)
                sc = mod_all[:, :, 0:2 * NORMS:2]
                sh = mod_all[:, :, 1:2 * NORMS:2]
                tmp = S[0].p[:, 0, 0:NB * NORMS].rearrange("p (b m) -> p b m", b=NB)
                dve.wait_ge(pre_dve, 5)
                nc.vector.tensor_scalar(tmp, sc, 1.0, None, ALU.add).then_inc(pre_dve, 1)
                dve.wait_ge(pre_dve, 6)
                nc.vector.tensor_tensor(sc, tmp, vec("ln_w", 0, NORMS).unsqueeze(1).broadcast_to([P, NB, NORMS]),
                                        ALU.mult).then_inc(pre_dve, 1)
                tmp2 = S[0].p[:, 1, 0:NB * NORMS].rearrange("p (b m) -> p b m", b=NB)
                nc.vector.tensor_tensor(tmp2, tmp, vec("ln_b", 0, NORMS).unsqueeze(1).broadcast_to([P, NB, NORMS]),
                                        ALU.mult).then_inc(pre_dve, 1)
                dve.wait_ge(pre_dve, 8)
                nc.vector.tensor_tensor(sh, sh, tmp2, ALU.add).then_inc(pre_dve, 1)

        last_k = len(BLOCKS) - 1

        def out_banks(k):
            if BLOCKS[k]["kind"] == "ff":
                return "AB" if BLOCKS[k]["act"] == "glu" else "TO"
            return "TO" if BLOCKS[k]["kind"] == "cross" else "AB"

        def keys_plain(b):
            return b.xn[:, :, :].rearrange("p t d -> p (t d)")

        def tensor_program(s, pe):
            b = S[s]
            reader = {}

            def claim(name, sig, *label):
                if name in reader:
                    pe.wait_ge(*reader[name])
                reader[name] = sig.at(*label)
                return b.bank[name]

            def mm(out, lhsT, rhs, start=True, stop=True):
                return nc.tensor.matmul(out, lhsT, rhs, start=start, stop=stop)

            def tr(out, in_, n=P):
                return nc.tensor.transpose(out, in_, ident[0:n, 0:n])

            def mm_swapped(out, lhsT, rhs):
                mm(out[0:64, :], lhsT[:, 64:P], rhs)
                return mm(out[64:P, :], lhsT[:, 0:64], rhs)

            for k, blk in enumerate(BLOCKS):
                kind, la, hd = blk["kind"], blk["layer"], blk.get("hd")
                pe.wait_ge(weights_loaded[la], 16)
                rows = P if blk.get("project") else CD
                if kind == "cross":
                    ctxT = b.ctxT
                    if blk.get("normed"):
                        yield
                        O = claim("O", b.act, k, "ctx_nT")
                        pe.wait_ge(*b.dve.at(k - 1, "ctx_n"))
                        tr(O[0:CD, 0:J], b.ctx_n[:, :], J).then_inc(*b.pe.mark(k, "ctxT"))
                        ctxT = b.ctx_nT[0:CD, :]
                    if blk.get("project"):
                        yield
                        O = claim("O", b.act, k, "ctx_nT")
                        mm(O[:, 0:2 * J], w(la, "W_ctx", CD), b.ctxT[:, :]).then_inc(*b.pe.mark(k, "ctxT"))
                        ctxT = b.ctx_nT
                    yield
                    wk = w(la, blk["k"][0], rows)[:, blk["k"][1]:]
                    wv = w(la, blk["v"][0], rows)[:, blk["v"][1]:]
                    if blk.get("normed") or blk.get("project"):
                        pe.wait_ge(*b.act.at(k, "ctx_nT"))
                    if blk["hd"] == 64:
                        A = claim("A", b.dve, k, "k_cos" if blk.get("rope") else "k")
                        for c in range(8):
                            last = mm(A[:, c * J:(c + 1) * J], wk[:, c * P:(c + 1) * P], ctxT[:, 0:J])
                        last.then_inc(*b.pe.mark(k, "k"))
                        if blk.get("rope"):
                            yield
                            B = claim("B", b.dve, k, "k_sin")
                            for c in range(8):
                                last = mm_swapped(B[:, c * J:(c + 1) * J], wk[:, c * P:(c + 1) * P], ctxT[:, 0:J])
                            last.then_inc(*b.pe.mark(k, "k_swapped"))
                        for half in range(2):
                            yield
                            B = claim("OT"[half], b.act, k, "v", half)
                            mm(B[:, :], ctxT[:, :], wv[:, half * 512:(half + 1) * 512])\
                                .then_inc(*b.pe.mark(k, "v", half))
                    else:
                        A = claim("A", b.act, k, "k_plain")
                        mm(A[:, 0:J], wk[:, 0:P], ctxT[:, 0:J]).then_inc(*b.pe.mark(k, "k"))
                        B = claim("B", b.dve, k, "v")
                        mm(B[:, 0:D], ctxT[:, :], wv[:, 0:P]).then_inc(*b.pe.mark(k, "v"))
                yield
                T = claim("T", b.act, k, "hT")
                for ti in range(NT):
                    pe.wait_ge(*b.dve.at(k, "xn", ti))
                    last = tr(T[:, ti * P:(ti + 1) * P], b.xn[:, ti, :])
                last.then_inc(*b.pe.mark(k, "xnT"))

                if kind in ("self", "cross"):
                    wq = w(la, blk["q"][0])[:, blk["q"][1]:]
                    hd, rope = blk["hd"], blk.get("rope")
                    q_maker = b.pool if rope else b.act if hd == 64 else b.dve
                    yield
                    pe.wait_ge(*b.act.at(k, "hT"))
                    if hd == 64:
                        for g in range(4):
                            if g:
                                yield
                            names = ("A", "B") if rope else ("AT"[g % 2],)
                            for r, name in enumerate(names):
                                if r:
                                    yield
                                A = claim(name, *((b.dve, k, ("q_cos", "q_sin")[r], g) if rope else (b.act, k, "q", g)))
                                for i in range(2):
                                    c = 2 * g + i
                                    lhsT = wq[:, c * P:(c + 1) * P]
                                    last = (mm_swapped if r else mm)(A[:, i * N:(i + 1) * N], lhsT, b.hT[:, :])
                                last.then_inc(*b.pe.mark(k, ("q", "q_swapped")[r], g))
                            if kind == "self":
                                wk = w(la, blk["k"][0])[:, blk["k"][1]:]
                                names = ("T", "O") if rope else ("BO"[g % 2],)
                                for r, name in enumerate(names):
                                    yield
                                    A = claim(name, b.dve, k, *((("k_cos", "k_sin")[r], g) if rope else ("k", g)))
                                    for i in range(2):
                                        c = 2 * g + i
                                        lhsT = wk[:, c * P:(c + 1) * P]
                                        last = (mm_swapped if r else mm)(A[:, i * N:(i + 1) * N], lhsT, b.hT[:, :])
                                    last.then_inc(*b.pe.mark(k, ("k", "k_swapped")[r], g))
                    else:
                        A = claim("A", b.dve, k, "q", 0)
                        mm(A[:, 0:N], wq[:, 0:P], b.hT[:, :]).then_inc(*b.pe.mark(k, "q", 0))
                        if kind == "self":
                            yield
                            wk = w(la, blk["k"][0])[:, blk["k"][1]:]
                            A = claim("B", b.act, k, "k_plain")
                            mm(A[:, 0:N], wk[:, 0:P], b.hT[:, :]).then_inc(*b.pe.mark(k, "k", 0))
                    if kind == "self":
                        wv = w(la, blk["v"][0])[:, blk["v"][1]:]
                        if hd == 64:
                            for ti in range(NT):
                                yield
                                for half in range(2):
                                    if half:
                                        yield
                                    A = claim(("AT", "BO")[half][ti], b.act, k, "v", ti, half)
                                    mm(A[:, :], b.hT[:, ti * P:(ti + 1) * P], wv[:, half * 512:(half + 1) * 512])\
                                        .then_inc(*b.pe.mark(k, "v", ti, half))
                        else:
                            yield
                            A = claim("T", b.dve, k, "v")
                            for ti in range(NT):
                                last = mm(A[:, ti * P:(ti + 1) * P], b.hT[:, ti * P:(ti + 1) * P], wv[:, 0:P])
                            last.then_inc(*b.pe.mark(k, "v"))

                def project_out(chunks):
                    n = 4 if kind == "ff" else 8 if hd == 64 else 1
                    wo = w(la, blk["w2"] if kind == "ff" else blk["o"])
                    for ti in range(NT):
                        yield
                        if 0 in chunks:
                            out[ti] = claim(out_banks(k)[ti], b.dve, k, "x", ti)
                        for c in chunks:
                            pe.wait_ge(*made(c))
                            last = mm(out[ti][:, 0:D], b.qT[:, c, ti * P:(ti + 1) * P], wo[:, c * D:(c + 1) * D],
                                      c == 0, c == n - 1)
                        if n - 1 in chunks:
                            last.then_inc(*b.pe.mark(k, "out", ti))
                        else:
                            last.then_inc(*b.pe.mark(k, "out_part", ti))

                out = [None] * NT
                if kind == "self":
                    def scores(p, ti):
                        yield
                        if p == 0 and ti == 0:
                            for g in range(4 if hd == 64 else 1):
                                pe.wait_ge(*q_maker.at(k, "q", g))
                                if hd == 64:
                                    pe.wait_ge(*b.dve.at(k, "k", g))
                        if hd == 8 and ti == 0:
                            pe.wait_ge(*b.dve.at(k, "kmask", p))
                        A = claim("AB"[ti], b.act, k, "exp", p, ti)
                        qc = b.qT[:, p if hd == 64 else 0, ti * P:(ti + 1) * P]
                        mm(A[:, :], qc, b.kk[:, p * 512:(p + 1) * 512]).then_inc(*b.pe.mark(k, "scores", p, ti))

                    def turned(r, h2):
                        yield
                        T = claim("T", (b.act, b.dve)[h2], k, "pT", r, h2)
                        if hd == 64:
                            pe.wait_ge(*b.dve.at(k, "norm", r, h2))
                        else:
                            pe.wait_ge(*b.act.at(k, "exp", r, 1))
                        for kt in range(NT):
                            for ti in range(NT):
                                last = tr(T[:, kt * N + ti * P:kt * N + (ti + 1) * P],
                                          b.p[:, r % 2, (ti * 2 + h2) * N + kt * P:(ti * 2 + h2) * N + (kt + 1) * P])
                        last.then_inc(*b.pe.mark(k, "T", r, h2))

                    def values(r):
                        yield
                        if hd == 64 or r == 0:
                            O = claim("O", *((b.act, k, "attn", r) if hd == 64 else (b.dve, k, "attn_n")))
                        else:
                            O = b.bank["O"]
                        if r == 0:
                            if hd == 64:
                                for ti in range(NT):
                                    for half in range(2):
                                        pe.wait_ge(*b.act.at(k, "v", ti, half))
                            else:
                                pe.wait_ge(*b.dve.at(k, "v"))
                        pe.wait_ge(*b.act.at(k, "pT", r, 0))
                        pe.wait_ge(*b.dve.at(k, "pT", r, 1))
                        for kt in range(NT):
                            for h2 in range(2):
                                rhs = b.pT[:, h2, kt * N:(kt + 1) * N]
                                if hd == 64:
                                    c = (2 * r + h2) * 64
                                    last = mm(O[64 * h2:64 * h2 + 64, 0:N], b.v[:, kt * 1024 + c:kt * 1024 + c + 64],
                                              rhs, kt == 0, kt == NT - 1)
                                else:
                                    h = ORDER8[r][h2]
                                    q0 = 32 * (h // 4)
                                    last = mm(O[q0:q0 + 32, 0:N], b.v[:, kt * 512 + h * 32:kt * 512 + h * 32 + 32],
                                              rhs, kt == 0 and r < 2, kt == NT - 1 and r >= 6)
                        last.then_inc(*b.pe.mark(k, "PV", r))

                    def made(c):
                        return b.act.at(k, "attn", c)

                    for p in range(8):
                        yield from scores(p, 0)
                        if p > 1:
                            yield from values(p - 2)
                        if p > 0:
                            yield from turned(p - 1, 0)
                        yield from scores(p, 1)
                        if p > 0:
                            yield from turned(p - 1, 1)
                    yield from values(6)
                    yield from turned(7, 0)
                    if hd == 64:
                        yield from project_out(range(0, 6))
                    yield from turned(7, 1)
                    if hd == 8:
                        yield
                        A = claim("A", b.act, k, "R")
                        pe.wait_ge(*b.dve.at(k, "spread"))
                        for ti in range(NT):
                            last = tr(A[:, ti * P:(ti + 1) * P], b.xn[:, ti, :])
                        last.then_inc(*b.pe.mark(k, "R"))
                    yield from values(7)
                    yield from project_out(range(6, 8) if hd == 64 else range(1))

                if kind == "cross":
                    for half in range(2):
                        for ti in range(NT):
                            yield
                            if half == 0 and ti == 0:
                                for g in range(4 if hd == 64 else 1):
                                    pe.wait_ge(*q_maker.at(k, "q", g))
                                pe.wait_ge(*b.dve.at(k, "k"))
                            A = claim("AB"[ti], *((b.dve, k, "sub", half, ti) if ti == 0 else (b.act, k, "exp", half, ti)))
                            if hd == 64:
                                for p in range(4 * half, 4 * half + 4):
                                    last = mm(A[:, (p % 4) * P:(p % 4 + 1) * P], b.qT[:, p, ti * P:(ti + 1) * P],
                                              b.kk[:, p * P:(p + 1) * P])
                            else:
                                last = mm(A[:, :], b.qT[:, 0, ti * P:(ti + 1) * P], b.kk[:, half * 512:(half + 1) * 512])
                            last.then_inc(*b.pe.mark(k, "scores", half, ti))

                    def turned(g):
                        half, i = g // 2, g % 2
                        yield
                        T = claim("TA"[i], (b.act, b.dve)[i], k, "pT", half, i)
                        for ti in range(NT):
                            if hd == 64:
                                pe.wait_ge(*b.dve.at(k, "norm", half, ti))
                            else:
                                pe.wait_ge(*b.act.at(k, "exp", half, ti))
                        for pp in range(2):
                            for ti in range(NT):
                                last = tr(T[:, pp * N + ti * P:pp * N + (ti + 1) * P],
                                          b.p[:, half, ti * 512 + (2 * i + pp) * P:ti * 512 + (2 * i + pp + 1) * P])
                        last.then_inc(*b.pe.mark(k, "T", half, i))

                    def values(g):
                        half, i = g // 2, g % 2
                        yield
                        if hd == 64:
                            O = claim("OB"[i], b.act, k, "attn", g)
                        elif g == 0:
                            O = claim("O", b.dve, k, "attn_n")
                        else:
                            O = b.bank["O"]
                        if g == 0:
                            if hd == 64:
                                pe.wait_ge(*b.act.at(k, "v", 1))
                                pe.wait_ge(*b.act.at(k, "v", 0))
                            else:
                                pe.wait_ge(*b.dve.at(k, "v"))
                        pe.wait_ge(*(b.act, b.dve)[i].at(k, "pT", half, i))
                        for pp in range(2):
                            p = 2 * g + pp
                            rhs = b.pT[:, i, pp * N:(pp + 1) * N]
                            if hd == 64:
                                last = mm(O[:, pp * N:(pp + 1) * N], b.v[:, p * P:(p + 1) * P], rhs)
                            else:
                                last = mm(O[32 * g:32 * g + 32, 0:N], b.v[:, p * 32:(p + 1) * 32], rhs,
                                          pp == 0, pp == 1)
                        last.then_inc(*b.pe.mark(k, "PV", g))

                    def made(c):
                        return b.act.at(k, "attn", c // 2)

                    yield from turned(0)
                    yield from turned(1)
                    yield from values(0)
                    yield from turned(2)
                    yield from values(1)
                    yield from turned(3)
                    yield from values(2)
                    if hd == 64:
                        yield from project_out(range(0, 4))
                    else:
                        yield
                        B = claim("B", b.act, k, "R")
                        pe.wait_ge(*b.dve.at(k, "spread"))
                        for ti in range(NT):
                            last = tr(B[:, ti * P:(ti + 1) * P], b.xn[:, ti, :])
                        last.then_inc(*b.pe.mark(k, "R"))
                    yield from values(3)
                    yield from project_out(range(4, 8) if hd == 64 else range(1))

                if kind == "ff":
                    chunks = (4, 6, 0, 2) if blk["act"] == "glu" else (0, 2)
                    w1 = w(la, blk["w1"])
                    yield
                    pe.wait_ge(*b.act.at(k, "hT"))
                    for i, c0 in enumerate(chunks):
                        if i:
                            yield
                        if i < 2:
                            A = claim("AB"[i], b.act, k, "gelu", c0 % 4 + 1)
                        else:
                            A = claim("TO"[i - 2], b.dve, k, "hidden", c0 + 1)
                        for c in (c0, c0 + 1):
                            last = mm(A[:, (c - c0) * N:(c - c0 + 1) * N], w1[:, c * P:(c + 1) * P], b.hT[:, :])
                        last.then_inc(*b.pe.mark(k, "h1", i))

                    def made(c):
                        return b.dve.at(k, "hidden", c) if blk["act"] == "glu" else b.act.at(k, "gelu", c)

                    yield from project_out(range(4))

        def scalar_program(s, eng):
            b = S[s]

            def act(out, in_, func=ACT.Identity, **kw):
                return nc.scalar.activation(out, in_, func, **kw)

            for k, blk in enumerate(BLOCKS):
                kind, la, m = blk["kind"], blk["layer"], blk["norm"]
                hd, rope = blk.get("hd"), blk.get("rope")
                if blk.get("normed"):
                    yield
                    eng.wait_ge(*b.pe.at(k, "ctxT"))
                    for i in range(2):
                        last = act(b.ctx_nT[0:CD, i * J:(i + 1) * J], b.bank["O"][0:CD, 0:J],
                                   scale=vec((2, "ca_lnc_w"))[0:CD, :], bias=vec((2, "ca_lnc_b"))[0:CD, :])
                    last.then_inc(*b.act.mark(k, "ctx_nT"))
                if blk.get("project"):
                    yield
                    eng.wait_ge(*b.pe.at(k, "ctxT"))
                    act(b.ctx_nT[:, :], b.bank["O"][:, 0:2 * J], bias=vec((la, "b_ctx"))).then_inc(*b.act.mark(k, "ctx_nT"))

                def bias(name):
                    return vec((la, blk[name][0]), blk[name][1]) if name in blk else 0.0

                if kind == "cross":
                    yield
                    if hd == 64:
                        for half in range(2):
                            if half:
                                yield
                            eng.wait_ge(*b.pe.at(k, "v", half))
                            bank = b.bank["OT"[half]][:, :].rearrange("p (c h d) -> p c h d", h=2, d=64)
                            out = b.v[:, half * 512:(half + 1) * 512].rearrange("p (c h d) -> p c h d", h=2, d=64)
                            for h2 in range(2):
                                last = act(out[:, :, h2, :], bank[:, :, h2, :], scale=mask64[:, h2:h2 + 1])
                            last.then_inc(*b.act.mark(k, "v", half))
                    else:
                        eng.wait_ge(*b.pe.at(k, "k"))
                        act(b.p[:, 0, 0:J], b.bank["A"][:, 0:J], bias=bias("bk")).then_inc(*b.act.mark(k, "k_plain"))
                yield
                eng.wait_ge(*b.pe.at(k, "xnT"))
                if k == 0:
                    eng.wait_ge(*b.dve.at("mod"))
                act(b.hT[:, :], b.bank["T"][:, 0:N], scale=b.mod[:, 2 * m:2 * m + 1],
                    bias=b.mod[:, 2 * m + 1:2 * m + 2]).then_inc(*b.act.mark(k, "hT"))
                if kind == "self" and hd == 8:
                    yield
                    eng.wait_ge(*b.pe.at(k, "k", 0))
                    act(keys_plain(b), b.bank["B"][:, 0:N], bias=bias("bk")).then_inc(*b.act.mark(k, "k_plain"))
                if kind in ("self", "cross") and hd == 64 and not rope:
                    for g in range(4):
                        yield
                        eng.wait_ge(*b.pe.at(k, "q", g))
                        act(b.qT[:, 2 * g:2 * g + 2, :], b.bank["AT"[g % 2]][:, :].rearrange("p (c n) -> p c n", c=2), ACT.Copy, scale=0.125)\
                            .then_inc(*b.act.mark(k, "q", g))
                if kind == "self" and hd == 64:
                    for ti in range(NT):
                        yield
                        for half in range(2):
                            if half:
                                yield
                            eng.wait_ge(*b.pe.at(k, "v", ti, half))
                            act(b.v[:, ti * 1024 + half * 512:ti * 1024 + (half + 1) * 512],
                                b.bank[("AT", "BO")[half][ti]][:, :], ACT.Copy).then_inc(*b.act.mark(k, "v", ti, half))

                if kind == "self":
                    def exps(p, ti):
                        yield
                        if p >= 2 and ti == 0:
                            eng.wait_ge(*b.pe.at(k, "T", p - 2, 1))
                        eng.wait_ge(*b.dve.at(k, "max", p, ti))
                        for h2 in range(2):
                            c = p * 4 + ti * 2 + h2
                            last = act(b.p[:, p % 2, (ti * 2 + h2) * N:(ti * 2 + h2 + 1) * N],
                                       b.bank["AB"[ti]][:, h2 * N:(h2 + 1) * N], ACT.Exp,
                                       bias=b.nm[:, c:c + 1], accum_out=b.sums[:, c:c + 1])
                        last.then_inc(*b.act.mark(k, "exp", p, ti))

                    def turned(r):
                        yield
                        eng.wait_ge(*b.pe.at(k, "T", r, 0))
                        if r > 0:
                            eng.wait_ge(*b.pe.at(k, "PV", r - 1))
                        act(b.pT[:, 0, :], b.bank["T"][:, :], ACT.Copy).then_inc(*b.act.mark(k, "pT", r, 0))

                    def attended(r):
                        if hd == 64:
                            yield
                            eng.wait_ge(*b.pe.at(k, "PV", r))
                            act(b.qT[:, r, :], b.bank["O"][:, 0:N], ACT.Copy).then_inc(*b.act.mark(k, "attn", r))

                    for p in range(8):
                        if p > 1:
                            yield from attended(p - 2)
                        if p > 0:
                            yield from turned(p - 1)
                        yield from exps(p, 0)
                        yield from exps(p, 1)
                    yield from attended(6)
                    yield from turned(7)
                    yield from attended(7)
                    if hd == 8:
                        yield
                        eng.wait_ge(*b.pe.at(k, "R"))
                        act(b.hT[:, :], b.bank["A"][:, 0:N], ACT.Copy).then_inc(*b.act.mark(k, "R"))
                        yield
                        eng.wait_ge(*b.dve.at(k, "attn_n"))
                        act(b.qT[:, 0, :], b.qT[:, 1, :], bias=bias("bv")).then_inc(*b.act.mark(k, "attn", 0))

                if kind == "cross":
                    for half in range(2):
                        yield
                        eng.wait_ge(*b.dve.at(k, "sub", half, 0))
                        act(b.p[:, half, 0:512], b.p[:, half, 0:512], ACT.Exp).then_inc(*b.act.mark(k, "exp", half, 0))
                        yield
                        eng.wait_ge(*b.dve.at(k, "max", half, 1))
                        for h in range(8):
                            c = half * 16 + 8 + h
                            last = act(b.p[:, half, 512 + h * J:512 + (h + 1) * J], b.bank["B"][:, h * J:(h + 1) * J],
                                       ACT.Exp, bias=b.nm[:, c:c + 1], accum_out=b.sums[:, c:c + 1])
                        last.then_inc(*b.act.mark(k, "exp", half, 1))
                    def turned(half):
                        yield
                        eng.wait_ge(*b.pe.at(k, "T", half, 0))
                        if half:
                            eng.wait_ge(*b.pe.at(k, "PV", 0))
                        act(b.pT[:, 0, :], b.bank["T"][:, :], ACT.Copy).then_inc(*b.act.mark(k, "pT", half, 0))

                    def attended(g):
                        if hd == 64:
                            yield
                            eng.wait_ge(*b.pe.at(k, "PV", g))
                            act(b.qT[:, 2 * g:2 * g + 2, :], b.bank["OB"[g % 2]][:, :].rearrange("p (c n) -> p c n", c=2),
                                ACT.Copy).then_inc(*b.act.mark(k, "attn", g))

                    yield from turned(0)
                    yield from attended(0)
                    yield from turned(1)
                    for g in range(1, 4):
                        yield from attended(g)
                    if hd == 8:
                        yield
                        eng.wait_ge(*b.pe.at(k, "R"))
                        act(b.hT[:, :], b.bank["B"][:, 0:N], ACT.Copy).then_inc(*b.act.mark(k, "R"))
                        yield
                        eng.wait_ge(*b.dve.at(k, "attn_n"))
                        act(b.qT[:, 0, :], b.qT[:, 1, :], bias=bias("bv")).then_inc(*b.act.mark(k, "attn", 0))

                if kind == "ff":
                    yield
                    glu = blk["act"] == "glu"
                    func = ACT.Gelu_apprx_tanh if blk["act"] == "tanh" else ACT.Gelu
                    for c in range(4):
                        if c:
                            yield
                        eng.wait_ge(*b.pe.at(k, "h1", c // 2))
                        out = b.p[:, 0, c * N:(c + 1) * N] if glu else b.qT[:, c, :]
                        act(out, b.bank["AB"[c // 2]][:, (c % 2) * N:(c % 2 + 1) * N], func,
                            bias=vec((la, blk["b1"]), c + (4 if glu else 0))).then_inc(*b.act.mark(k, "gelu", c))

        def vector_program(s, eng, turn):
            b = S[s]
            v = nc.vector

            def spread(ap, n):
                return ap.unsqueeze(2).broadcast_to([ap.shape[0], ap.shape[1], n])

            for k, blk in enumerate(BLOCKS):
                kind, la, m = blk["kind"], blk["layer"], blk["norm"]
                hd, rope = blk.get("hd"), blk.get("rope")
                yield
                if k == 0:
                    v.tensor_copy(b.mod[:, :].unsqueeze(1), mod_all[:, bass.ds(turn * STREAMS + s, 1), :])\
                        .then_inc(*b.dve.mark("mod"))
                    for ti in range(NT):
                        v.bn_stats(b.stats[:, ti, :], b.x[:, ti, :]).then_inc(*b.dve.mark(k, "stats", ti))
                yield
                for ti in range(NT):
                    eng.wait_ge(*b.dve.at(k, "stats", ti))
                    v.bn_aggr(b.mv[:, ti, :], b.stats[:, ti, :]).then_inc(*b.dve.mark(k, "mv", ti))
                if blk.get("norm_ctx"):
                    yield
                    v.bn_stats(b.cstats[:, :], b.ctx[:, :]).then_inc(*b.dve.mark(k, "cstats"))
                    eng.wait_ge(*b.dve.at(k, "cstats"))
                    v.bn_aggr(b.cmv[:, :], b.cstats[:, :]).then_inc(*b.dve.mark(k, "cmv"))
                if kind == "cross" and hd == 64:
                    yield
                    kv = b.kk[:, 0:16 * J].rearrange("p (c h n) -> p c h n", c=8, h=2)
                    src = b.bank["A"][:, :].rearrange("p (c n) -> p c n", c=8)
                    if rope:
                        cos, sin = table["k"]
                        t1_, t2_ = b.p[:, 1, 0:512], b.p[:, 1, 512:1024]
                        eng.wait_ge(*b.pe.at(k, "k"))
                        v.tensor_tensor(t1_.rearrange("p (c n) -> p c n", c=8), src,
                                        cos[:, 0:J].unsqueeze(1).broadcast_to([P, 8, J]), ALU.mult)\
                            .then_inc(*b.dve.mark(k, "k_cos"))
                        eng.wait_ge(*b.pe.at(k, "k_swapped"))
                        v.tensor_tensor(t2_.rearrange("p (c n) -> p c n", c=8),
                                        b.bank["B"][:, :].rearrange("p (c n) -> p c n", c=8),
                                        sin[:, 0:J].unsqueeze(1).broadcast_to([P, 8, J]), ALU.mult)\
                            .then_inc(*b.dve.mark(k, "k_sin"))
                    else:
                        eng.wait_ge(*b.pe.at(k, "k"))
                        for h2 in range(2):
                            last = v.tensor_scalar(kv[:, :, h2, :], src, mask64[:, h2:h2 + 1], None, ALU.mult)
                        last.then_inc(*b.dve.mark(k, "k"))

                if kind == "cross" and hd == 8:
                    yield
                    eng.wait_ge(*b.act.at(k, "k_plain"))
                    v.tensor_tensor(b.kk[:, 0:16 * J].rearrange("p (h n) -> p h n", h=16),
                                    b.p[:, 0, 0:J].unsqueeze(1).broadcast_to([P, 16, J]), spread(mask16, J), ALU.mult)\
                        .then_inc(*b.dve.mark(k, "k"))

                yield
                eng.wait_ge(*b.dve.at(k, "mv", 1))
                eng.wait_ge(*b.pool.at(k, "rstd"))
                for ti in range(NT):
                    v.tensor_scalar(b.xn[:, ti, :], b.x[:, ti, :], b.mv[:, ti, 0:1], b.rstd[:, ti:ti + 1],
                                    ALU.subtract, ALU.mult).then_inc(*b.dve.mark(k, "xn", ti))
                if blk.get("norm_ctx"):
                    yield
                    eng.wait_ge(*b.pool.at(k, "crstd"))
                    v.tensor_scalar(b.ctx_n[:, :], b.ctx[:, :], b.cmv[:, 0:1], b.cve[:, 1:2],
                                    ALU.subtract, ALU.mult).then_inc(*b.dve.mark(k, "ctx_n"))

                if kind == "cross" and rope:
                    yield
                    eng.wait_ge(*b.pool.at(k, "k_sum"))
                    src = b.p[:, 1, 0:512].rearrange("p (c n) -> p c n", c=8)
                    for h2 in range(2):
                        last = v.tensor_scalar(kv[:, :, h2, :], src, mask_rope[:, h2:h2 + 1], None, ALU.mult)
                    last.then_inc(*b.dve.mark(k, "k"))
                if kind == "cross" and hd == 8:
                    yield
                    eng.wait_ge(*b.pe.at(k, "v"))
                    eng.wait_ge(*b.pool.at(k, "v_zero"))
                    bank = b.bank["B"][:, 0:D].rearrange("p (g j d) -> p g j d", g=4, j=4)
                    out = b.v[:, 0:256].rearrange("p (g i c) -> p g i c", g=4, i=2)
                    for j in range(4):
                        last = v.tensor_scalar(out[:, :, j // 2, 8 * j:8 * j + 8], bank[:, :, j, :],
                                               mask64[:, j % 2:j % 2 + 1], None, ALU.mult)
                    last.then_inc(*b.dve.mark(k, "v"))

                if kind in ("self", "cross") and hd == 64 and (rope or kind == "self"):
                    def rotated(name, slot, banks, g):
                        for r, (tab, bank) in enumerate(zip(table[name], banks)):
                            yield
                            if r == 0 and g and name == "q":
                                eng.wait_ge(*b.pool.at(k, "q", g - 1))
                            if r == 0 and g and name == "k":
                                eng.wait_ge(*b.dve.at(k, "k", g - 1))
                            eng.wait_ge(*b.pe.at(k, name + ("", "_swapped")[r], g))
                            v.tensor_tensor(b.p[:, slot, r * 512:(r + 1) * 512].rearrange("p (c n) -> p c n", c=2),
                                            b.bank[bank][:, :].rearrange("p (c n) -> p c n", c=2),
                                            tab.unsqueeze(1).broadcast_to([P, 2, N]), ALU.mult)\
                                .then_inc(*b.dve.mark(k, name + ("_cos", "_sin")[r], g))

                    def masked(g):
                        yield
                        if rope:
                            eng.wait_ge(*b.pool.at(k, "k_sum", g))
                            src = b.p[:, 1, 0:512].rearrange("p (c n) -> p c n", c=2)
                        else:
                            eng.wait_ge(*b.pe.at(k, "k", g))
                            src = b.bank["BO"[g % 2]][:, :].rearrange("p (c n) -> p c n", c=2)
                        kv = b.kk[:, g * 1024:(g + 1) * 1024].rearrange("p (c h n) -> p c h n", c=2, h=2)
                        for h2 in range(2):
                            last = v.tensor_scalar(kv[:, :, h2, :], src, (mask_rope if rope else mask64)[:, h2:h2 + 1],
                                                   None, ALU.mult)
                        last.then_inc(*b.dve.mark(k, "k", g))

                    for g in range(4):
                        if rope:
                            yield from rotated("q", 0, "AB", g)
                            if kind == "self":
                                if g:
                                    yield from masked(g - 1)
                                yield from rotated("k", 1, "TO", g)
                        else:
                            yield from masked(g)
                    if rope and kind == "self":
                        yield from masked(3)
                if kind in ("self", "cross") and hd == 8:
                    yield
                    eng.wait_ge(*b.pe.at(k, "q", 0))
                    bq = vec((la, blk["bq"][0]), blk["bq"][1]) if "bq" in blk else 0.0
                    v.tensor_scalar(b.qT[:, 0, :], b.bank["A"][:, 0:N], bq, float(np.float32(8.0 ** -0.5)), ALU.add, ALU.mult)\
                        .then_inc(*b.dve.mark(k, "q", 0))
                    if kind == "self":
                        yield
                        eng.wait_ge(*b.pe.at(k, "v"))
                        eng.wait_ge(*b.pool.at(k, "v_zero"))
                        bank = b.bank["T"][:, 0:N].rearrange("p (t g j d) -> p t g j d", t=2, g=4, j=4)
                        out = b.v[:, 0:1024].rearrange("p (t g j c) -> p t g j c", t=2, g=4, j=4)
                        for j in range(4):
                            last = v.tensor_copy(out[:, :, :, j, 8 * j:8 * j + 8], bank[:, :, :, j, :])
                        last.then_inc(*b.dve.mark(k, "v"))

                if kind == "self":
                    def maxima(p, ti):
                        yield
                        eng.wait_ge(*b.pe.at(k, "scores", p, ti))
                        c = p * 4 + ti * 2
                        v.tensor_reduce(b.nm[:, c:c + 2], b.bank["AB"[ti]][:, :].rearrange("p (h n) -> p h n", h=2),
                                        AXX, ALU.max, negate=True).then_inc(*b.dve.mark(k, "max", p, ti))

                    def turned(r):
                        yield
                        eng.wait_ge(*b.pe.at(k, "T", r, 1))
                        if r > 0:
                            eng.wait_ge(*b.pe.at(k, "PV", r - 1))
                        v.tensor_copy(b.pT[:, 1, :], b.bank["T"][:, :]).then_inc(*b.dve.mark(k, "pT", r, 1))

                    def normalised(p):
                        yield
                        eng.wait_ge(*b.act.at(k, "exp", p, 1))
                        c = p * 4
                        v.reciprocal(b.rs[:, c:c + 4], b.sums[:, c:c + 4]).then_inc(*b.dve.mark(k, "rsum", p))
                        if hd == 64:
                            eng.wait_ge(*b.dve.at(k, "rsum", p))
                            for h2 in range(2):
                                for i in (h2, 2 + h2):
                                    pr = b.p[:, p % 2, i * N:(i + 1) * N]
                                    last = v.tensor_scalar(pr, pr, b.rs[:, c + i:c + i + 1], None, ALU.mult)
                                last.then_inc(*b.dve.mark(k, "norm", p, h2))
                        elif p == 7:
                            eng.wait_ge(*b.dve.at(k, "rsum", 7))
                            rs = b.rs[:, :].rearrange("p (j i t h) -> p j i t h", j=4, i=2, t=NT)
                            out = b.xn[:, :, :].rearrange("p t (i h j d) -> p t i h j d", i=2, h=2, j=4)
                            for ti in range(NT):
                                for i in range(2):
                                    for h2 in range(2):
                                        last = v.tensor_copy(out[:, ti, i, h2], spread(rs[:, :, i, ti, h2], 8))
                            last.then_inc(*b.dve.mark(k, "spread"))

                    def masked(p):
                        yield
                        eng.wait_ge(*b.act.at(k, "k_plain"))
                        for h2 in range(2):
                            h, c = ORDER8[p][h2], (2 * p + h2) * N
                            last = v.tensor_scalar(b.kk[:, c:c + N], keys_plain(b), mask16[:, h:h + 1], None, ALU.mult)
                        last.then_inc(*b.dve.mark(k, "kmask", p))

                    if hd == 8:
                        yield from masked(0)
                        yield from masked(1)
                    for p in range(8):
                        yield from maxima(p, 0)
                        yield from maxima(p, 1)
                        if hd == 8 and p + 2 < 8:
                            yield from masked(p + 2)
                        if p > 0:
                            yield from turned(p - 1)
                        yield from normalised(p)
                    yield from turned(7)
                    if hd == 8:
                        yield
                        eng.wait_ge(*b.pe.at(k, "PV", 7))
                        eng.wait_ge(*b.act.at(k, "R"))
                        v.tensor_tensor(b.qT[:, 1, :], b.bank["O"][:, 0:N], b.hT[:, :], ALU.mult)\
                            .then_inc(*b.dve.mark(k, "attn_n"))

                if kind == "cross":
                    def maxima(half, ti):
                        yield
                        eng.wait_ge(*b.pe.at(k, "scores", half, ti))
                        c = (half * 2 + ti) * 8
                        bank = b.bank["AB"[ti]][:, :].rearrange("p (h n) -> p h n", h=8)
                        v.tensor_reduce(b.nm[:, c:c + 8], bank, AXX, ALU.max, negate=True)\
                            .then_inc(*b.dve.mark(k, "max", half, ti))
                        if ti == 0:
                            eng.wait_ge(*b.dve.at(k, "max", half, ti))
                            pr = b.p[:, half, 0:512].rearrange("p (h n) -> p h n", h=8)
                            v.tensor_tensor(pr, bank, spread(b.nm[:, c:c + 8], J), ALU.add)\
                                .then_inc(*b.dve.mark(k, "sub", half, ti))

                    def normalised(half, ti):
                        yield
                        eng.wait_ge(*b.act.at(k, "exp", half, ti))
                        c = (half * 2 + ti) * 8
                        pr = b.p[:, half, ti * 512:(ti + 1) * 512].rearrange("p (h n) -> p h n", h=8)
                        if ti == 0:
                            v.tensor_reduce(b.sums[:, c:c + 8], pr, AXX, ALU.add)\
                                .then_inc(*b.dve.mark(k, "sum", half, ti))
                            eng.wait_ge(*b.dve.at(k, "sum", half, ti))
                        v.reciprocal(b.rs[:, c:c + 8], b.sums[:, c:c + 8]).then_inc(*b.dve.mark(k, "rsum", half, ti))
                        if hd == 64:
                            eng.wait_ge(*b.dve.at(k, "rsum", half, ti))
                            v.tensor_tensor(pr, pr, spread(b.rs[:, c:c + 8], J), ALU.mult)\
                                .then_inc(*b.dve.mark(k, "norm", half, ti))

                    def turned(half):
                        yield
                        eng.wait_ge(*b.pe.at(k, "T", half, 1))
                        if half:
                            eng.wait_ge(*b.pe.at(k, "PV", 1))
                        v.tensor_copy(b.pT[:, 1, :], b.bank["A"][:, :]).then_inc(*b.dve.mark(k, "pT", half, 1))

                    yield from maxima(0, 0)
                    yield from maxima(0, 1)
                    yield from maxima(1, 0)
                    yield from normalised(0, 0)
                    yield from maxima(1, 1)
                    yield from normalised(0, 1)
                    yield from normalised(1, 0)
                    if hd == 64:
                        yield from turned(0)
                    yield from normalised(1, 1)
                    if hd == 8:
                        yield
                        eng.wait_ge(*b.dve.at(k, "rsum", 1, 1))
                        for ti in range(NT):
                            rs = b.rs[:, :].rearrange("p (f t h) -> p f t h", f=2, t=NT)[:, :, ti, :]
                            out = b.xn[:, ti, :].rearrange("p (f h d) -> p f h d", f=2, h=8)
                            last = v.tensor_copy(out, rs.unsqueeze(3).broadcast_to([P, 2, 8, 8]))
                        last.then_inc(*b.dve.mark(k, "spread"))
                        yield from turned(0)
                    yield from turned(1)
                    if hd == 8:
                        yield
                        eng.wait_ge(*b.pe.at(k, "PV", 3))
                        eng.wait_ge(*b.act.at(k, "R"))
                        v.tensor_tensor(b.qT[:, 1, :], b.bank["O"][:, 0:N], b.hT[:, :], ALU.mult)\
                            .then_inc(*b.dve.mark(k, "attn_n"))

                if kind == "ff" and blk["act"] == "glu":
                    yield
                    for c in range(4):
                        if c:
                            yield
                        eng.wait_ge(*b.pe.at(k, "h1", 2 + c // 2))
                        eng.wait_ge(*b.act.at(k, "gelu", c))
                        v.scalar_tensor_tensor(out=b.qT[:, c, :], in0=b.bank["TO"[c // 2]][:, (c % 2) * N:(c % 2 + 1) * N],
                                               scalar=vec((la, blk["b1"]), c), in1=b.p[:, 0, c * N:(c + 1) * N],
                                               op0=ALU.add, op1=ALU.mult).then_inc(*b.dve.mark(k, "hidden", c))

                for ti in range(NT):
                    yield
                    eng.wait_ge(*b.pe.at(k, "out", ti))
                    eng.wait_ge(*b.pool.at(k, "xb"))
                    x_new = b.y if k == last_k else b.x
                    v.tensor_tensor(x_new[:, ti, :], b.bank[out_banks(k)[ti]][:, 0:D], b.xb[:, ti, :], ALU.add)\
                        .then_inc(*b.dve.mark(k, "x", ti))
                    if k < last_k:
                        eng.wait_ge(*b.dve.at(k, "x", ti))
                        v.bn_stats(b.stats[:, ti, :], b.x[:, ti, :]).then_inc(*b.dve.mark(k + 1, "stats", ti))

        def gpsimd_program(s, eng):
            b = S[s]
            g_ = nc.gpsimd
            for k, blk in enumerate(BLOCKS):
                kind, la = blk["kind"], blk["layer"]
                hd, rope = blk.get("hd"), blk.get("rope")
                yield
                eng.wait_ge(*b.dve.at(k, "mv", 1))
                g_.tensor_scalar(b.ve[:, :], b.mv[:, :, 1], EPS[la], None, ALU.add).then_inc(*b.pool.mark(k, "ve"))
                eng.wait_ge(*b.pool.at(k, "ve"))
                g_.tensor_tensor(b.rstd[:, :], b.ve[:, :], minus_half[:, 0:NT], ALU.pow).then_inc(*b.pool.mark(k, "rstd"))
                if blk.get("norm_ctx"):
                    eng.wait_ge(*b.dve.at(k, "cmv"))
                    g_.tensor_scalar(b.cve[:, 0:1], b.cmv[:, 1:2], EPS[la], None, ALU.add).then_inc(*b.pool.mark(k, "cve"))
                    eng.wait_ge(*b.pool.at(k, "cve"))
                    g_.tensor_tensor(b.cve[:, 1:2], b.cve[:, 0:1], minus_half[0:J, 0:1], ALU.pow)\
                        .then_inc(*b.pool.mark(k, "crstd"))
                if hd == 8:
                    yield
                    g_.memset(b.v[:, 0:(1024 if kind == "self" else 256)], 0.0).then_inc(*b.pool.mark(k, "v_zero"))
                if kind == "cross" and rope:
                    yield
                    eng.wait_ge(*b.dve.at(k, "k_sin"))
                    t1_, t2_ = b.p[:, 1, 0:512], b.p[:, 1, 512:1024]
                    g_.tensor_tensor(t1_, t1_, t2_, ALU.add).then_inc(*b.pool.mark(k, "k_sum"))
                if rope:
                    for g in range(4):
                        yield
                        eng.wait_ge(*b.dve.at(k, "q_sin", g))
                        half = b.p[:, 0, :].rearrange("p (r c n) -> p r c n", r=2, c=2)
                        g_.tensor_tensor(b.qT[:, 2 * g:2 * g + 2, :], half[:, 0], half[:, 1], ALU.add)\
                            .then_inc(*b.pool.mark(k, "q", g))
                        if kind == "self":
                            yield
                            eng.wait_ge(*b.dve.at(k, "k_sin", g))
                            t1_, t2_ = b.p[:, 1, 0:512], b.p[:, 1, 512:1024]
                            g_.tensor_tensor(t1_, t1_, t2_, ALU.add).then_inc(*b.pool.mark(k, "k_sum", g))
                yield
                g_.tensor_tensor(b.xb[:, :, :], b.x[:, :, :],
                                 out_bias[:, k, :].unsqueeze(1).broadcast_to([P, NT, D]), ALU.add)\
                    .then_inc(*b.pool.mark(k, "xb"))

        def store(sp, b, batch):
            at = bass.ds(batch, 1)
            sp.wait_ge(*b.dve.at(last_k, "x", NT - 1))
            sp.dma_start(t["out"][at].rearrange("o (t p) d -> p (o t) d", p=P), b.y[:, :, :]).then_inc(b.stored, 16)

        with nc.Fori(0, NB // STREAMS) as turn:
            begin("loop")
            with nc.Block() as block:

                @block.sync
                def _(sp):
                    for s, b in enumerate(S):
                        sp.wait_ge(*b.dve.at(last_k, "xn", NT - 1))
                        sp.wait_ge(*b.pool.at(last_k, "xb"))
                        load(sp, b, (turn + 1) * STREAMS + s, b.x_loaded, b.ctx_loaded)
                    for s, b in enumerate(S):
                        store(sp, b, turn * STREAMS + s)
                    for b in S:
                        sp.wait_ge(b.x_loaded, 16)
                        sp.wait_ge(b.ctx_loaded, 32)
                        sp.wait_ge(b.stored, 16)

                @block.tensor
                def _(pe):
                    in_turn(ORDER["tensor"], [tensor_program(s, pe) for s in range(STREAMS)])

                @block.scalar
                def _(act):
                    in_turn(ORDER["scalar"], [scalar_program(s, act) for s in range(STREAMS)])

                @block.vector
                def _(dve):
                    in_turn(ORDER["vector"], [vector_program(s, dve, turn) for s in range(STREAMS)])

                @block.gpsimd
                def _(pool):
                    in_turn(ORDER["gpsimd"], [gpsimd_program(s, pool) for s in range(STREAMS)])
            end()


def packed(inputs):
    def arr(layer, name):
        return np.asarray(inputs[f"L{layer}_xcond_{name}"])

    def rows(a, chunks):
        out = np.zeros((P, chunks * a.shape[1]), a.dtype)
        if chunks == 1:
            out[:a.shape[0]] = a
        else:
            out[:] = a.reshape(chunks, P, a.shape[1]).transpose(1, 0, 2).reshape(P, -1)
        return out

    rotated = np.arange(1024).reshape(8, 2, 32, 2).transpose(0, 3, 1, 2).reshape(-1)
    order = {"sa_wq": rotated, "ca_wq": rotated}
    order["sa_wkv"] = order["ca_wkv"] = np.concatenate([rotated, np.arange(1024, 2048)])
    t = {}
    for la, ws in enumerate(WEIGHTS):
        t[f"weights{la}"] = np.concatenate(
            [rows(arr(la, n)[:, order[n]] if n in order else arr(la, n), c) for n, c, _ in ws], 1)
    t["mod_w"] = np.concatenate([arr(la, n)[:, c * P:(c + 1) * P] for la, n, c in MODS], 1)
    vec = [arr(la, n)[c * P:(c + 1) * P][:, None] for la, n, c in MOD_BIAS]
    one, zero = np.ones((P, 1), np.float32), np.zeros((P, 1), np.float32)
    vec += [one] * 6 + [arr(2, n)[:, None] for n in ("ln1_w", "ln2_w")] + [arr(3, f"ln{i}_w")[:, None] for i in (1, 2, 3)]
    vec += [zero] * 6 + [arr(2, n)[:, None] for n in ("ln1_b", "ln2_b")] + [arr(3, f"ln{i}_b")[:, None] for i in (1, 2, 3)]
    vec.append(np.asarray(inputs["cond_1024"]).T)
    for la, n, c in VECS:
        a = arr(la, n)
        if a.shape[0] < P:
            a = np.concatenate([a, np.zeros(P - a.shape[0], a.dtype)])
        vec.append(a.reshape(c, P).T)
    t["vecs"] = np.concatenate(vec, 1)
    t["out_bias"] = np.concatenate([arr(la, n) for la, n in OUT_BIAS])
    t["x"], t["ctx"] = (np.concatenate([a, np.zeros_like(a[:STREAMS])]) for a in
                        (np.asarray(inputs["x"]), np.asarray(inputs["ctx_768"])))
    ctxT = t["ctx"].transpose(0, 2, 1)
    t["ctxT"] = np.concatenate([ctxT, ctxT], 2)

    part = np.arange(P)
    half = 64
    inv = (np.float32(1.0) / np.float32(10000.0) ** (np.arange(0, half, 2, dtype=np.float32) / np.float32(half)))
    ang = (np.arange(N, dtype=np.float32)[:, None] * inv[None, :].astype(np.float32)).astype(np.float32)
    cos = np.cos(ang).astype(np.float32)[:, part % 32].T
    sin = np.sin(ang).astype(np.float32)[:, part % 32].T * np.where(part < 64, -1, 1)[:, None].astype(np.float32)
    consts = dict(
        ident=np.eye(P), mask16=(part[:, None] // 8 == np.arange(16)[None, :]),
        mask64=(part[:, None] // 64 == np.arange(2)[None, :]),
        mask_rope=(part[:, None] // 32 % 2 == np.arange(2)[None, :]), cos_q=cos * np.float32(0.125), sin_q=sin * np.float32(0.125), cos_k=cos, sin_k=sin)
    t["consts"] = np.concatenate([np.asarray(consts[n], np.float32) for n in CONSTS], 1)
    return {n: np.ascontiguousarray(a) for n, a in t.items()}


def kernel(**inputs):
    import concourse.bacc as _bacc
    from concourse.bass_utils import run_bass_kernel_spmd as _run

    arrays = packed(inputs)
    counts = {}
    for _ in range(2):
        nc = _bacc.Bacc("TRN2", target_bir_lowering=False, num_devices=1)
        t = {n: nc.dram_tensor(f"in_{n}", a.shape, F32, kind="ExternalInput").ap() for n, a in arrays.items()}
        t["out"] = nc.dram_tensor("out_0", (NB, N, D), F32, kind="ExternalOutput").ap()
        program(nc, t, counts)
    r = _run(nc, [{f"in_{n}": a for n, a in arrays.items()}], core_ids=[0])
    return r.results[0]["out_0"]
```
